# Optimizing a Trainium2 kernel written in Bass

```python
import numpy as np
import jax
import jax.numpy as jnp

def _softmax(x, axis=-1):
    return jax.nn.softmax(x, axis=axis)

def _gelu(x):
    return jax.nn.gelu(x, approximate=True)

def _silu(x):
    return jax.nn.silu(x)

def _sigmoid(x):
    return jax.nn.sigmoid(x)

def _layernorm(x, axis=-1, eps=1e-05):
    m = jnp.mean(x, axis=axis, keepdims=True)
    v = jnp.var(x, axis=axis, keepdims=True)
    return (x - m) / jnp.sqrt(v + eps)

def _scatter_add(tgt, idx, src, axis=0):
    return tgt.at[idx].add(src)

def _segment_sum(src, seg, n):
    return jax.ops.segment_sum(src, seg, n)
kernel_name = 'mk_vit_tower_d2_tok_img1024_r4_1f72a9'

def setup_inputs(seed: int=0):
    np.random.seed(seed)
    _w = jnp.asarray

    def _rec_inputs():
        import jax
        import jax.numpy as jnp
        _rk = jax.random.key(seed)
        x = -0.000169711 + 1.00022 * jax.random.normal(jax.random.fold_in(_rk, 1), (64, 3, 168, 168), jnp.float32)
        return x
    x = _rec_inputs()

    def _L0_tok_setup():
        import jax, jax.numpy as jnp
        import numpy as np
        C = 256
        H8 = 8
        DH = C // H8
        PS = 14
        CS = 3
        IMG = 168
        B = 4

        def _ln(x, g, b):
            mu = jnp.mean(x, axis=-1, keepdims=True)
            xc = x - mu
            var = jnp.mean(xc * xc, axis=-1, keepdims=True)
            return xc * jax.lax.rsqrt(var + 1e-05) * g + b

        def _forward(pixel_values, conv_w, class_emb, la_ln_q_g, la_ln_q_b, la_wq, la_ln_kv_g, la_ln_kv_b, la_wkv, la_proj_w, la_proj_b, ga_ln_q_g, ga_ln_q_b, ga_wq, ga_ln_kv_g, ga_ln_kv_b, ga_wkv, ga_proj_w, ga_proj_b, mod_w, mod_b):
            b = pixel_values.shape[0]
            pe = jax.lax.conv_general_dilated(pixel_values, conv_w, (PS, PS), 'VALID', dimension_numbers=('NCHW', 'OIHW', 'NCHW'))
            HP = pe.shape[2]
            h = HP // CS
            hw, N = (h * h, CS * CS)
            scale = C ** (-0.5)
            grid = pe.reshape(b, C, h, CS, h, CS)
            red = grid.mean(axis=(3, 5)).reshape(b, C, hw).transpose(0, 2, 1)
            win = grid.transpose(0, 2, 4, 3, 5, 1).reshape(b, hw, N, C)
            q = _ln(red, la_ln_q_g, la_ln_q_b) @ la_wq
            q = q.reshape(b, hw, H8, DH).transpose(0, 2, 1, 3)
            kv = _ln(win, la_ln_kv_g, la_ln_kv_b) @ la_wkv
            kv = kv.reshape(b, hw, N, 2, H8, DH).transpose(3, 0, 4, 1, 2, 5)
            k_, v_ = (kv[0], kv[1])
            attn = jax.nn.softmax(jnp.einsum('bhnd,bhnkd->bhnk', q * scale, k_), axis=-1)
            agg = jnp.einsum('bhnk,bhnkd->bhnd', attn, v_)
            agg = agg.transpose(0, 2, 1, 3).reshape(b, hw, C)
            local_out = red + agg @ la_proj_w + la_proj_b
            cls = jnp.broadcast_to(class_emb, (b, 1, C))
            gq = (_ln(cls, ga_ln_q_g, ga_ln_q_b) @ ga_wq).reshape(b, H8, DH)
            gkv = _ln(local_out, ga_ln_kv_g, ga_ln_kv_b) @ ga_wkv
            gkv = gkv.reshape(b, hw, 2, H8, DH).transpose(2, 0, 3, 1, 4)
            gk, gv = (gkv[0], gkv[1])
            gattn = jax.nn.softmax(jnp.einsum('bhd,bhnd->bhn', gq * scale, gk), axis=-1)
            gagg = jnp.einsum('bhn,bhnd->bhd', gattn, gv).reshape(b, 1, C)
            cls_out = cls + gagg @ ga_proj_w + ga_proj_b
            patch_out = local_out @ mod_w + mod_b
            return jnp.concatenate([patch_out, cls_out], axis=1)
        key = jax.random.key(seed)
        ks = jax.random.split(key, 16)
        nrm = lambda k, shape: jax.random.normal(k, shape, jnp.float32) * 0.02
        return {'pixel_values': jax.random.normal(ks[0], (B, 3, IMG, IMG), jnp.float32), 'pixel_masks': jnp.ones((B, 1, IMG, IMG), jnp.float32), 'conv_w': nrm(ks[1], (C, 3, PS, PS)), 'class_emb': nrm(ks[2], (C,)), 'la_ln_q_g': jnp.ones((C,)), 'la_ln_q_b': jnp.zeros((C,)), 'la_wq': nrm(ks[3], (C, C)), 'la_ln_kv_g': jnp.ones((C,)), 'la_ln_kv_b': jnp.zeros((C,)), 'la_wkv': nrm(ks[4], (C, 2 * C)), 'la_proj_w': nrm(ks[5], (C, C)), 'la_proj_b': jnp.zeros((C,)), 'ga_ln_q_g': jnp.ones((C,)), 'ga_ln_q_b': jnp.zeros((C,)), 'ga_wq': nrm(ks[6], (C, C)), 'ga_ln_kv_g': jnp.ones((C,)), 'ga_ln_kv_b': jnp.zeros((C,)), 'ga_wkv': nrm(ks[7], (C, 2 * C)), 'ga_proj_w': nrm(ks[8], (C, C)), 'ga_proj_b': jnp.zeros((C,)), 'mod_w': nrm(ks[9], (C, C)), 'mod_b': jnp.zeros((C,))}
    _L0_tok_all = _L0_tok_setup()
    _L0_tok_in = {k: v for k, v in _L0_tok_all.items() if k in ('pixel_masks', 'conv_w', 'class_emb', 'la_ln_q_g', 'la_ln_q_b', 'la_wq', 'la_ln_kv_g', 'la_ln_kv_b', 'la_wkv', 'la_proj_w', 'la_proj_b', 'ga_ln_q_g', 'ga_ln_q_b', 'ga_wq', 'ga_ln_kv_g', 'ga_ln_kv_b', 'ga_wkv', 'ga_proj_w', 'ga_proj_b', 'mod_w', 'mod_b')}
    del _L0_tok_all

    def _L0_attn_setup():
        import jax, jax.numpy as jnp
        import numpy as np
        HIDDEN = 256
        NUM_HEADS = 16
        INDEXER_HEADS = 4
        D_IDX = 32
        K_BASE = 128
        K_MIN = 32
        K_MAX = 256
        ROPE_BASE = 2500
        SINK = 4

        def _apply_rotary(x, cos_e, sin_e):
            x1, x2 = (x[..., ::2], x[..., 1::2])
            return jnp.concatenate((x1 * cos_e - x2 * sin_e, x1 * sin_e + x2 * cos_e), axis=-1)

        def _gsa_forward(x, W_Iq, W_Ik, W_Iw, gate_bias, head_importance_bias, W_q, W_k, W_v, W_gv, W_go, W_o):
            B, T, C = x.shape
            H = NUM_HEADS
            HI = INDEXER_HEADS
            hd = C // H
            hpi = H // HI
            q_I = (x @ W_Iq.T).reshape(B, T, HI, D_IDX)
            k_I = (x @ W_Ik.T).reshape(B, T, HI, D_IDX)
            w = jax.nn.sigmoid(x @ W_Iw.T)
            match_logits = jnp.einsum('bqhd,bkhd->bhqk', q_I, k_I)
            match_logits = match_logits + gate_bias[None, :, None, None]
            match_gate = jax.nn.sigmoid(match_logits)
            w_exp = jnp.transpose(w, (0, 2, 1))[..., None]
            imp_per_indexer = w_exp * match_gate
            importance = jnp.repeat(imp_per_indexer, hpi, axis=1)
            importance = importance * jax.nn.sigmoid(head_importance_bias)[None, :, None, None]
            pos = jnp.arange(T)
            causal = pos[:, None] >= pos[None, :]
            imp_masked = jnp.where(causal[None, None], importance, 0.0)
            var_t = jnp.var(imp_masked, axis=-1)
            k_t = jnp.clip(jnp.floor(K_BASE * var_t / 1.0), K_MIN, K_MAX).astype(jnp.int32)
            imp_sel = jnp.where(causal[None, None], importance, -jnp.inf)
            if T > SINK:
                imp_sel = imp_sel.at[..., :SINK].set(jnp.inf)
            k_limit = min(T, K_MAX)
            _, top_idx = jax.lax.top_k(imp_sel, k_limit)
            keep = jnp.arange(k_limit)[None, None, None, :] < k_t[..., None]
            b_ix = jnp.arange(B)[:, None, None, None]
            h_ix = jnp.arange(H)[None, :, None, None]
            q_ix = jnp.arange(T)[None, None, :, None]
            sel = jnp.zeros((B, H, T, T), bool).at[b_ix, h_ix, q_ix, top_idx].set(keep)
            sel = sel & causal[None, None]
            q = (x @ W_q.T).reshape(B, T, H, hd)
            k = (x @ W_k.T).reshape(B, T, H, hd)
            v = x @ W_v.T * jax.nn.sigmoid(x @ W_gv.T)
            v = v.reshape(B, T, H, hd)
            inv_freq = 1.0 / ROPE_BASE ** (jnp.arange(0, hd, 2, dtype=jnp.float32) / hd)
            freqs = jnp.outer(jnp.arange(T, dtype=jnp.float32), inv_freq)
            emb = jnp.concatenate((freqs, freqs), axis=-1)
            cos_e = jnp.cos(emb)[:, ::2][None, :, None, :].astype(x.dtype)
            sin_e = jnp.sin(emb)[:, ::2][None, :, None, :].astype(x.dtype)
            q = _apply_rotary(q, cos_e, sin_e)
            k = _apply_rotary(k, cos_e, sin_e)
            q = jnp.transpose(q, (0, 2, 1, 3))
            k = jnp.transpose(k, (0, 2, 1, 3))
            v = jnp.transpose(v, (0, 2, 1, 3))
            min_val = jnp.finfo(q.dtype).min
            bias = jnp.where(sel, jnp.array(0.0, q.dtype), min_val)
            scores = jnp.einsum('bhqd,bhkd->bhqk', q, k) / jnp.sqrt(jnp.array(hd, q.dtype)) + bias
            attn = jax.nn.softmax(scores, axis=-1)
            o = jnp.einsum('bhqk,bhkd->bhqd', attn, v)
            o = jnp.transpose(o, (0, 2, 1, 3)).reshape(B, T, C)
            g_o = jax.nn.sigmoid(x @ W_go.T)
            return o * g_o @ W_o.T
        key = jax.random.key(seed)
        ks = jax.random.split(key, 12)
        std = 0.02
        B, T, C = (1, 512, HIDDEN)
        inp = {'x': jax.random.normal(ks[0], (B, T, C), jnp.float32), 'W_Iq': jax.random.normal(ks[1], (INDEXER_HEADS * D_IDX, C), jnp.float32) * std, 'W_Ik': jax.random.normal(ks[2], (INDEXER_HEADS * D_IDX, C), jnp.float32) * std, 'W_Iw': jax.random.normal(ks[3], (INDEXER_HEADS, C), jnp.float32) * std, 'gate_bias': jnp.zeros((INDEXER_HEADS,), jnp.float32), 'head_importance_bias': jnp.zeros((NUM_HEADS,), jnp.float32), 'W_q': jax.random.normal(ks[4], (C, C), jnp.float32) * std, 'W_k': jax.random.normal(ks[5], (C, C), jnp.float32) * std, 'W_v': jax.random.normal(ks[6], (C, C), jnp.float32) * std, 'W_gv': jax.random.normal(ks[7], (C, C), jnp.float32) * std, 'W_go': jax.random.normal(ks[8], (C, C), jnp.float32) * std, 'W_o': jax.random.normal(ks[9], (C, C), jnp.float32) * std}
        return inp
    _L0_attn_all = _L0_attn_setup()
    _L0_attn_in = {k: v for k, v in _L0_attn_all.items() if k in ('W_Iq', 'W_Ik', 'W_Iw', 'gate_bias', 'head_importance_bias', 'W_q', 'W_k', 'W_v', 'W_gv', 'W_go', 'W_o')}
    del _L0_attn_all

    def _L0_ffn_setup():
        import jax, jax.numpy as jnp
        import numpy as np
        D_MODEL = 256
        NUM_HEADS = 4
        NUM_EXPERTS = 8
        TOP_K = 2
        D_FF = 256
        EPS = 1e-06

        def _rmsnorm(x, g):
            return x * jax.lax.rsqrt(jnp.mean(x * x, axis=-1, keepdims=True) + EPS) * g

        def _swiglu(x, w1, w2, w3):
            return jax.nn.silu(x @ w1.T) * (x @ w3.T) @ w2.T
        key = jax.random.key(seed)
        ks = jax.random.split(key, 16)
        d, e, f = (D_MODEL, NUM_EXPERTS, D_FF)
        dc = d // 4
        s = 0.02
        return {'X': jax.random.normal(ks[0], (2, 256, d), dtype=jnp.float32), 'g1': jnp.ones((d,), jnp.float32), 'g2': jnp.ones((d,), jnp.float32), 'Wq': jax.random.normal(ks[1], (d, d), jnp.float32) * s, 'Wkc': jax.random.normal(ks[2], (dc, d), jnp.float32) * s, 'Wvc': jax.random.normal(ks[3], (dc, d), jnp.float32) * s, 'Wo': jax.random.normal(ks[4], (d, d), jnp.float32) * s, 'Wr': jax.random.normal(ks[5], (e, d), jnp.float32) * s, 'expert_bias': jnp.zeros((e,), jnp.float32), 'sW1': jax.random.normal(ks[6], (f, d), jnp.float32) * s, 'sW2': jax.random.normal(ks[7], (d, f), jnp.float32) * s, 'sW3': jax.random.normal(ks[8], (f, d), jnp.float32) * s, 'eW1': jax.random.normal(ks[9], (e, f, d), jnp.float32) * s, 'eW2': jax.random.normal(ks[10], (e, d, f), jnp.float32) * s, 'eW3': jax.random.normal(ks[11], (e, f, d), jnp.float32) * s}
    _L0_ffn_all = _L0_ffn_setup()
    _L0_ffn_in = {k: v for k, v in _L0_ffn_all.items() if k in ('g1', 'g2', 'Wq', 'Wkc', 'Wvc', 'Wo', 'Wr', 'expert_bias', 'sW1', 'sW2', 'sW3', 'eW1', 'eW2', 'eW3')}
    del _L0_ffn_all

    def _L1_attn_setup():
        import math
        import jax, jax.numpy as jnp
        import numpy as np
        B, L, DIM, HEADS = (4, 512, 256, 8)
        HEAD = DIM // HEADS
        SCALE_BASE = 512.0
        EPS = 1e-05

        def _xpos(x, downscale=False):
            l, dh = (x.shape[-2], x.shape[-1])
            half = dh // 2
            pos = jnp.arange(l, dtype=x.dtype)
            base = (jnp.arange(0, dh, 2, dtype=x.dtype) + 0.4 * dh) / (1.4 * dh)
            scale = base[None, :] ** (pos[:, None] / SCALE_BASE)
            inv_freq = 1.0 / 10000.0 ** (jnp.arange(half, dtype=x.dtype) / half)
            sinusoid = pos[:, None] * inv_freq[None, :]
            sin, cos = (jnp.sin(sinusoid), jnp.cos(sinusoid))
            if downscale:
                scale = 1.0 / scale
            s = jnp.repeat(sin * scale, 2, axis=-1)
            c = jnp.repeat(cos * scale, 2, axis=-1)
            x1, x2 = (x[..., ::2], x[..., 1::2])
            rot = jnp.stack([-x2, x1], axis=-1).reshape(x.shape)
            return x * c + rot * s

        def _decay_mask(l, gammas):
            n = jnp.arange(l)[:, None]
            m = jnp.arange(l)[None, :]
            lg = jnp.log(gammas)
            expo = (n - m).astype(jnp.float32)[None, :, :] * lg[:, None, None]
            return jnp.where((n >= m)[None], jnp.exp(expo), 0.0)
        key = jax.random.key(seed)
        ks = jax.random.split(key, 6)
        d = DIM
        return {'X': jax.random.normal(ks[0], (B, L, DIM), dtype=jnp.float32), 'W_Q': jax.random.normal(ks[1], (HEADS, DIM, HEAD), dtype=jnp.float32) / d, 'W_K': jax.random.normal(ks[2], (HEADS, DIM, HEAD), dtype=jnp.float32) / d, 'W_V': jax.random.normal(ks[3], (HEADS, DIM, HEAD), dtype=jnp.float32) / d, 'W_G': jax.random.normal(ks[4], (DIM, DIM), dtype=jnp.float32) / d, 'W_O': jax.random.normal(ks[5], (DIM, DIM), dtype=jnp.float32) / d, 'gn_weight': jnp.ones((DIM,), dtype=jnp.float32), 'gn_bias': jnp.zeros((DIM,), dtype=jnp.float32)}
    _L1_attn_all = _L1_attn_setup()
    _L1_attn_in = {k: v for k, v in _L1_attn_all.items() if k in ('W_Q', 'W_K', 'W_V', 'W_G', 'W_O', 'gn_weight', 'gn_bias')}
    del _L1_attn_all

    def _L1_ffn_setup():
        import jax, jax.numpy as jnp
        import numpy as np
        EPS = 1e-05

        def _quantize(W):
            gamma = jnp.mean(jnp.abs(W))
            return jnp.clip(jnp.round(W / (gamma + EPS)), -1.0, 1.0)
        key = jax.random.key(seed)
        k_x, k_w1, k_b1, k_w2, k_b2 = jax.random.split(key, 5)
        n_embd = 256
        d_ff = 4 * n_embd
        B, S = (4, 1024)
        bound1 = 1.0 / np.sqrt(n_embd)
        bound2 = 1.0 / np.sqrt(d_ff)
        x = jax.random.normal(k_x, (B, S, n_embd), dtype=jnp.float32)
        W1 = jax.random.uniform(k_w1, (d_ff, n_embd), jnp.float32, -bound1, bound1)
        b1 = jax.random.uniform(k_b1, (d_ff,), jnp.float32, -bound1, bound1)
        W2 = jax.random.uniform(k_w2, (n_embd, d_ff), jnp.float32, -bound2, bound2)
        b2 = jax.random.uniform(k_b2, (n_embd,), jnp.float32, -bound2, bound2)
        return {'x': x, 'W1': W1, 'b1': b1, 'W2': W2, 'b2': b2}
    _L1_ffn_all = _L1_ffn_setup()
    _L1_ffn_in = {k: v for k, v in _L1_ffn_all.items() if k in ('W1', 'b1', 'W2', 'b2')}
    del _L1_ffn_all
    return {'x': x, 'L0_tok_pixel_masks': _L0_tok_in['pixel_masks'], 'L0_tok_conv_w': _L0_tok_in['conv_w'], 'L0_tok_class_emb': _L0_tok_in['class_emb'], 'L0_tok_la_ln_q_g': _L0_tok_in['la_ln_q_g'], 'L0_tok_la_ln_q_b': _L0_tok_in['la_ln_q_b'], 'L0_tok_la_wq': _L0_tok_in['la_wq'], 'L0_tok_la_ln_kv_g': _L0_tok_in['la_ln_kv_g'], 'L0_tok_la_ln_kv_b': _L0_tok_in['la_ln_kv_b'], 'L0_tok_la_wkv': _L0_tok_in['la_wkv'], 'L0_tok_la_proj_w': _L0_tok_in['la_proj_w'], 'L0_tok_la_proj_b': _L0_tok_in['la_proj_b'], 'L0_tok_ga_ln_q_g': _L0_tok_in['ga_ln_q_g'], 'L0_tok_ga_ln_q_b': _L0_tok_in['ga_ln_q_b'], 'L0_tok_ga_wq': _L0_tok_in['ga_wq'], 'L0_tok_ga_ln_kv_g': _L0_tok_in['ga_ln_kv_g'], 'L0_tok_ga_ln_kv_b': _L0_tok_in['ga_ln_kv_b'], 'L0_tok_ga_wkv': _L0_tok_in['ga_wkv'], 'L0_tok_ga_proj_w': _L0_tok_in['ga_proj_w'], 'L0_tok_ga_proj_b': _L0_tok_in['ga_proj_b'], 'L0_tok_mod_w': _L0_tok_in['mod_w'], 'L0_tok_mod_b': _L0_tok_in['mod_b'], 'L0_attn_W_Iq': _L0_attn_in['W_Iq'], 'L0_attn_W_Ik': _L0_attn_in['W_Ik'], 'L0_attn_W_Iw': _L0_attn_in['W_Iw'], 'L0_attn_gate_bias': _L0_attn_in['gate_bias'], 'L0_attn_head_importance_bias': _L0_attn_in['head_importance_bias'], 'L0_attn_W_q': _L0_attn_in['W_q'], 'L0_attn_W_k': _L0_attn_in['W_k'], 'L0_attn_W_v': _L0_attn_in['W_v'], 'L0_attn_W_gv': _L0_attn_in['W_gv'], 'L0_attn_W_go': _L0_attn_in['W_go'], 'L0_attn_W_o': _L0_attn_in['W_o'], 'L0_ffn_g1': _L0_ffn_in['g1'], 'L0_ffn_g2': _L0_ffn_in['g2'], 'L0_ffn_Wq': _L0_ffn_in['Wq'], 'L0_ffn_Wkc': _L0_ffn_in['Wkc'], 'L0_ffn_Wvc': _L0_ffn_in['Wvc'], 'L0_ffn_Wo': _L0_ffn_in['Wo'], 'L0_ffn_Wr': _L0_ffn_in['Wr'], 'L0_ffn_expert_bias': _L0_ffn_in['expert_bias'], 'L0_ffn_sW1': _L0_ffn_in['sW1'], 'L0_ffn_sW2': _L0_ffn_in['sW2'], 'L0_ffn_sW3': _L0_ffn_in['sW3'], 'L0_ffn_eW1': _L0_ffn_in['eW1'], 'L0_ffn_eW2': _L0_ffn_in['eW2'], 'L0_ffn_eW3': _L0_ffn_in['eW3'], 'L1_attn_W_Q': _L1_attn_in['W_Q'], 'L1_attn_W_K': _L1_attn_in['W_K'], 'L1_attn_W_V': _L1_attn_in['W_V'], 'L1_attn_W_G': _L1_attn_in['W_G'], 'L1_attn_W_O': _L1_attn_in['W_O'], 'L1_attn_gn_weight': _L1_attn_in['gn_weight'], 'L1_attn_gn_bias': _L1_attn_in['gn_bias'], 'L1_ffn_W1': _L1_ffn_in['W1'], 'L1_ffn_b1': _L1_ffn_in['b1'], 'L1_ffn_W2': _L1_ffn_in['W2'], 'L1_ffn_b2': _L1_ffn_in['b2']}

def reference(x, L0_tok_pixel_masks, L0_tok_conv_w, L0_tok_class_emb, L0_tok_la_ln_q_g, L0_tok_la_ln_q_b, L0_tok_la_wq, L0_tok_la_ln_kv_g, L0_tok_la_ln_kv_b, L0_tok_la_wkv, L0_tok_la_proj_w, L0_tok_la_proj_b, L0_tok_ga_ln_q_g, L0_tok_ga_ln_q_b, L0_tok_ga_wq, L0_tok_ga_ln_kv_g, L0_tok_ga_ln_kv_b, L0_tok_ga_wkv, L0_tok_ga_proj_w, L0_tok_ga_proj_b, L0_tok_mod_w, L0_tok_mod_b, L0_attn_W_Iq, L0_attn_W_Ik, L0_attn_W_Iw, L0_attn_gate_bias, L0_attn_head_importance_bias, L0_attn_W_q, L0_attn_W_k, L0_attn_W_v, L0_attn_W_gv, L0_attn_W_go, L0_attn_W_o, L0_ffn_g1, L0_ffn_g2, L0_ffn_Wq, L0_ffn_Wkc, L0_ffn_Wvc, L0_ffn_Wo, L0_ffn_Wr, L0_ffn_expert_bias, L0_ffn_sW1, L0_ffn_sW2, L0_ffn_sW3, L0_ffn_eW1, L0_ffn_eW2, L0_ffn_eW3, L1_attn_W_Q, L1_attn_W_K, L1_attn_W_V, L1_attn_W_G, L1_attn_W_O, L1_attn_gn_weight, L1_attn_gn_bias, L1_ffn_W1, L1_ffn_b1, L1_ffn_W2, L1_ffn_b2):
    import jax
    import jax.numpy as jnp

    def _L0_tok_ref(pixel_values, pixel_masks, conv_w, class_emb, la_ln_q_g, la_ln_q_b, la_wq, la_ln_kv_g, la_ln_kv_b, la_wkv, la_proj_w, la_proj_b, ga_ln_q_g, ga_ln_q_b, ga_wq, ga_ln_kv_g, ga_ln_kv_b, ga_wkv, ga_proj_w, ga_proj_b, mod_w, mod_b):
        import jax, jax.numpy as jnp
        import numpy as np
        C = 256
        H8 = 8
        DH = C // H8
        PS = 14
        CS = 3
        IMG = 168
        B = 4

        def _ln(x, g, b):
            mu = jnp.mean(x, axis=-1, keepdims=True)
            xc = x - mu
            var = jnp.mean(xc * xc, axis=-1, keepdims=True)
            return xc * jax.lax.rsqrt(var + 1e-05) * g + b

        def _forward(pixel_values, conv_w, class_emb, la_ln_q_g, la_ln_q_b, la_wq, la_ln_kv_g, la_ln_kv_b, la_wkv, la_proj_w, la_proj_b, ga_ln_q_g, ga_ln_q_b, ga_wq, ga_ln_kv_g, ga_ln_kv_b, ga_wkv, ga_proj_w, ga_proj_b, mod_w, mod_b):
            b = pixel_values.shape[0]
            pe = jax.lax.conv_general_dilated(pixel_values, conv_w, (PS, PS), 'VALID', dimension_numbers=('NCHW', 'OIHW', 'NCHW'))
            HP = pe.shape[2]
            h = HP // CS
            hw, N = (h * h, CS * CS)
            scale = C ** (-0.5)
            grid = pe.reshape(b, C, h, CS, h, CS)
            red = grid.mean(axis=(3, 5)).reshape(b, C, hw).transpose(0, 2, 1)
            win = grid.transpose(0, 2, 4, 3, 5, 1).reshape(b, hw, N, C)
            q = _ln(red, la_ln_q_g, la_ln_q_b) @ la_wq
            q = q.reshape(b, hw, H8, DH).transpose(0, 2, 1, 3)
            kv = _ln(win, la_ln_kv_g, la_ln_kv_b) @ la_wkv
            kv = kv.reshape(b, hw, N, 2, H8, DH).transpose(3, 0, 4, 1, 2, 5)
            k_, v_ = (kv[0], kv[1])
            attn = jax.nn.softmax(jnp.einsum('bhnd,bhnkd->bhnk', q * scale, k_), axis=-1)
            agg = jnp.einsum('bhnk,bhnkd->bhnd', attn, v_)
            agg = agg.transpose(0, 2, 1, 3).reshape(b, hw, C)
            local_out = red + agg @ la_proj_w + la_proj_b
            cls = jnp.broadcast_to(class_emb, (b, 1, C))
            gq = (_ln(cls, ga_ln_q_g, ga_ln_q_b) @ ga_wq).reshape(b, H8, DH)
            gkv = _ln(local_out, ga_ln_kv_g, ga_ln_kv_b) @ ga_wkv
            gkv = gkv.reshape(b, hw, 2, H8, DH).transpose(2, 0, 3, 1, 4)
            gk, gv = (gkv[0], gkv[1])
            gattn = jax.nn.softmax(jnp.einsum('bhd,bhnd->bhn', gq * scale, gk), axis=-1)
            gagg = jnp.einsum('bhn,bhnd->bhd', gattn, gv).reshape(b, 1, C)
            cls_out = cls + gagg @ ga_proj_w + ga_proj_b
            patch_out = local_out @ mod_w + mod_b
            return jnp.concatenate([patch_out, cls_out], axis=1)
        del pixel_masks
        return _forward(pixel_values, conv_w, class_emb, la_ln_q_g, la_ln_q_b, la_wq, la_ln_kv_g, la_ln_kv_b, la_wkv, la_proj_w, la_proj_b, ga_ln_q_g, ga_ln_q_b, ga_wq, ga_ln_kv_g, ga_ln_kv_b, ga_wkv, ga_proj_w, ga_proj_b, mod_w, mod_b)

    def _L0_attn_ref(x, W_Iq, W_Ik, W_Iw, gate_bias, head_importance_bias, W_q, W_k, W_v, W_gv, W_go, W_o):
        import jax, jax.numpy as jnp
        import numpy as np
        HIDDEN = 256
        NUM_HEADS = 16
        INDEXER_HEADS = 4
        D_IDX = 32
        K_BASE = 128
        K_MIN = 32
        K_MAX = 256
        ROPE_BASE = 2500
        SINK = 4

        def _apply_rotary(x, cos_e, sin_e):
            x1, x2 = (x[..., ::2], x[..., 1::2])
            return jnp.concatenate((x1 * cos_e - x2 * sin_e, x1 * sin_e + x2 * cos_e), axis=-1)

        def _gsa_forward(x, W_Iq, W_Ik, W_Iw, gate_bias, head_importance_bias, W_q, W_k, W_v, W_gv, W_go, W_o):
            B, T, C = x.shape
            H = NUM_HEADS
            HI = INDEXER_HEADS
            hd = C // H
            hpi = H // HI
            q_I = (x @ W_Iq.T).reshape(B, T, HI, D_IDX)
            k_I = (x @ W_Ik.T).reshape(B, T, HI, D_IDX)
            w = jax.nn.sigmoid(x @ W_Iw.T)
            match_logits = jnp.einsum('bqhd,bkhd->bhqk', q_I, k_I)
            match_logits = match_logits + gate_bias[None, :, None, None]
            match_gate = jax.nn.sigmoid(match_logits)
            w_exp = jnp.transpose(w, (0, 2, 1))[..., None]
            imp_per_indexer = w_exp * match_gate
            importance = jnp.repeat(imp_per_indexer, hpi, axis=1)
            importance = importance * jax.nn.sigmoid(head_importance_bias)[None, :, None, None]
            pos = jnp.arange(T)
            causal = pos[:, None] >= pos[None, :]
            imp_masked = jnp.where(causal[None, None], importance, 0.0)
            var_t = jnp.var(imp_masked, axis=-1)
            k_t = jnp.clip(jnp.floor(K_BASE * var_t / 1.0), K_MIN, K_MAX).astype(jnp.int32)
            imp_sel = jnp.where(causal[None, None], importance, -jnp.inf)
            if T > SINK:
                imp_sel = imp_sel.at[..., :SINK].set(jnp.inf)
            k_limit = min(T, K_MAX)
            _, top_idx = jax.lax.top_k(imp_sel, k_limit)
            keep = jnp.arange(k_limit)[None, None, None, :] < k_t[..., None]
            b_ix = jnp.arange(B)[:, None, None, None]
            h_ix = jnp.arange(H)[None, :, None, None]
            q_ix = jnp.arange(T)[None, None, :, None]
            sel = jnp.zeros((B, H, T, T), bool).at[b_ix, h_ix, q_ix, top_idx].set(keep)
            sel = sel & causal[None, None]
            q = (x @ W_q.T).reshape(B, T, H, hd)
            k = (x @ W_k.T).reshape(B, T, H, hd)
            v = x @ W_v.T * jax.nn.sigmoid(x @ W_gv.T)
            v = v.reshape(B, T, H, hd)
            inv_freq = 1.0 / ROPE_BASE ** (jnp.arange(0, hd, 2, dtype=jnp.float32) / hd)
            freqs = jnp.outer(jnp.arange(T, dtype=jnp.float32), inv_freq)
            emb = jnp.concatenate((freqs, freqs), axis=-1)
            cos_e = jnp.cos(emb)[:, ::2][None, :, None, :].astype(x.dtype)
            sin_e = jnp.sin(emb)[:, ::2][None, :, None, :].astype(x.dtype)
            q = _apply_rotary(q, cos_e, sin_e)
            k = _apply_rotary(k, cos_e, sin_e)
            q = jnp.transpose(q, (0, 2, 1, 3))
            k = jnp.transpose(k, (0, 2, 1, 3))
            v = jnp.transpose(v, (0, 2, 1, 3))
            min_val = jnp.finfo(q.dtype).min
            bias = jnp.where(sel, jnp.array(0.0, q.dtype), min_val)
            scores = jnp.einsum('bhqd,bhkd->bhqk', q, k) / jnp.sqrt(jnp.array(hd, q.dtype)) + bias
            attn = jax.nn.softmax(scores, axis=-1)
            o = jnp.einsum('bhqk,bhkd->bhqd', attn, v)
            o = jnp.transpose(o, (0, 2, 1, 3)).reshape(B, T, C)
            g_o = jax.nn.sigmoid(x @ W_go.T)
            return o * g_o @ W_o.T
        return _gsa_forward(x, W_Iq, W_Ik, W_Iw, gate_bias, head_importance_bias, W_q, W_k, W_v, W_gv, W_go, W_o)

    def _L0_ffn_ref(X, g1, g2, Wq, Wkc, Wvc, Wo, Wr, expert_bias, sW1, sW2, sW3, eW1, eW2, eW3):
        import jax, jax.numpy as jnp
        import numpy as np
        D_MODEL = 256
        NUM_HEADS = 4
        NUM_EXPERTS = 8
        TOP_K = 2
        D_FF = 256
        EPS = 1e-06

        def _rmsnorm(x, g):
            return x * jax.lax.rsqrt(jnp.mean(x * x, axis=-1, keepdims=True) + EPS) * g

        def _swiglu(x, w1, w2, w3):
            return jax.nn.silu(x @ w1.T) * (x @ w3.T) @ w2.T
        B, S, d = X.shape
        H = NUM_HEADS
        dk = d // H
        scale = 1.0 / jnp.sqrt(jnp.float32(dk))
        nx = _rmsnorm(X, g1)
        Q = (nx @ Wq.T).reshape(B, S, H, dk).transpose(0, 2, 1, 3)
        Kc = nx @ Wkc.T
        Vc = nx @ Wvc.T
        scores = jnp.einsum('bhsd,btd->bhst', Q, Kc) * scale
        attn = jax.nn.softmax(scores, axis=-1)
        out = jnp.einsum('bhst,btd->bhsd', attn, Vc)
        out = out.transpose(0, 2, 1, 3).reshape(B, S, d) @ Wo.T
        X = X + out
        nx = _rmsnorm(X, g2)
        xf = nx.reshape(-1, d)
        logits = xf @ Wr.T + expert_bias
        rw = jax.nn.softmax(logits, axis=-1)
        topw, topi = jax.lax.top_k(rw, TOP_K)
        topw = jax.nn.softmax(topw, axis=-1)
        combine = jnp.sum(jax.nn.one_hot(topi, NUM_EXPERTS, dtype=xf.dtype) * topw[..., None], axis=1)
        shared = _swiglu(xf, sW1, sW2, sW3)
        h = jax.nn.silu(jnp.einsum('td,efd->etf', xf, eW1)) * jnp.einsum('td,efd->etf', xf, eW3)
        eo = jnp.einsum('etf,edf->etd', h, eW2)
        specialist = jnp.einsum('te,etd->td', combine, eo)
        moe_out = (shared + specialist).reshape(B, S, d)
        return X + moe_out

    def _L1_attn_ref(X, W_Q, W_K, W_V, W_G, W_O, gn_weight, gn_bias):
        import math
        import jax, jax.numpy as jnp
        import numpy as np
        B, L, DIM, HEADS = (4, 512, 256, 8)
        HEAD = DIM // HEADS
        SCALE_BASE = 512.0
        EPS = 1e-05

        def _xpos(x, downscale=False):
            l, dh = (x.shape[-2], x.shape[-1])
            half = dh // 2
            pos = jnp.arange(l, dtype=x.dtype)
            base = (jnp.arange(0, dh, 2, dtype=x.dtype) + 0.4 * dh) / (1.4 * dh)
            scale = base[None, :] ** (pos[:, None] / SCALE_BASE)
            inv_freq = 1.0 / 10000.0 ** (jnp.arange(half, dtype=x.dtype) / half)
            sinusoid = pos[:, None] * inv_freq[None, :]
            sin, cos = (jnp.sin(sinusoid), jnp.cos(sinusoid))
            if downscale:
                scale = 1.0 / scale
            s = jnp.repeat(sin * scale, 2, axis=-1)
            c = jnp.repeat(cos * scale, 2, axis=-1)
            x1, x2 = (x[..., ::2], x[..., 1::2])
            rot = jnp.stack([-x2, x1], axis=-1).reshape(x.shape)
            return x * c + rot * s

        def _decay_mask(l, gammas):
            n = jnp.arange(l)[:, None]
            m = jnp.arange(l)[None, :]
            lg = jnp.log(gammas)
            expo = (n - m).astype(jnp.float32)[None, :, :] * lg[:, None, None]
            return jnp.where((n >= m)[None], jnp.exp(expo), 0.0)
        b, l, d = X.shape
        h = W_Q.shape[0]
        gammas = 1.0 - jnp.exp(jnp.linspace(math.log(1.0 / 32.0), math.log(1.0 / 512.0), h)).astype(jnp.float32)
        Q = jnp.einsum('bld,hde->bhle', X, W_Q)
        K = jnp.einsum('bld,hde->bhle', X, W_K)
        V = jnp.einsum('bld,hdv->bhlv', X, W_V)
        Q = _xpos(Q)
        K = _xpos(K, downscale=True)
        D = _decay_mask(l, gammas).astype(X.dtype)
        scores = jnp.einsum('bhle,bhme->bhlm', Q, K) * D[None]
        Y = jnp.einsum('bhlm,bhmv->bhlv', scores, V)
        mean = Y.mean(axis=-1, keepdims=True)
        var = Y.var(axis=-1, keepdims=True)
        Yn = (Y - mean) * jax.lax.rsqrt(var + EPS)
        Yn = jnp.transpose(Yn, (0, 2, 1, 3)).reshape(b, l, -1)
        Yn = Yn * gn_weight + gn_bias
        G = X @ W_G
        out = G * jax.nn.sigmoid(G) * Yn @ W_O
        return out

    def _L1_ffn_ref(x, W1, b1, W2, b2):
        import jax, jax.numpy as jnp
        import numpy as np
        EPS = 1e-05

        def _quantize(W):
            gamma = jnp.mean(jnp.abs(W))
            return jnp.clip(jnp.round(W / (gamma + EPS)), -1.0, 1.0)
        Wq1 = _quantize(W1)
        Wq2 = _quantize(W2)
        h = jax.nn.relu(jnp.einsum('bsd,fd->bsf', x, Wq1) + b1)
        out = jnp.einsum('bsf,df->bsd', h, Wq2) + b2
        return out
    h = _L0_tok_ref(x, L0_tok_pixel_masks, L0_tok_conv_w, L0_tok_class_emb, L0_tok_la_ln_q_g, L0_tok_la_ln_q_b, L0_tok_la_wq, L0_tok_la_ln_kv_g, L0_tok_la_ln_kv_b, L0_tok_la_wkv, L0_tok_la_proj_w, L0_tok_la_proj_b, L0_tok_ga_ln_q_g, L0_tok_ga_ln_q_b, L0_tok_ga_wq, L0_tok_ga_ln_kv_g, L0_tok_ga_ln_kv_b, L0_tok_ga_wkv, L0_tok_ga_proj_w, L0_tok_ga_proj_b, L0_tok_mod_w, L0_tok_mod_b)
    h = h + _L0_attn_ref(_layernorm(h, axis=-1), L0_attn_W_Iq, L0_attn_W_Ik, L0_attn_W_Iw, L0_attn_gate_bias, L0_attn_head_importance_bias, L0_attn_W_q, L0_attn_W_k, L0_attn_W_v, L0_attn_W_gv, L0_attn_W_go, L0_attn_W_o)
    h = h + _L0_ffn_ref(_layernorm(h, axis=-1), L0_ffn_g1, L0_ffn_g2, L0_ffn_Wq, L0_ffn_Wkc, L0_ffn_Wvc, L0_ffn_Wo, L0_ffn_Wr, L0_ffn_expert_bias, L0_ffn_sW1, L0_ffn_sW2, L0_ffn_sW3, L0_ffn_eW1, L0_ffn_eW2, L0_ffn_eW3)
    h = h + _L1_attn_ref(_layernorm(h, axis=-1), L1_attn_W_Q, L1_attn_W_K, L1_attn_W_V, L1_attn_W_G, L1_attn_W_O, L1_attn_gn_weight, L1_attn_gn_bias)
    h = h + _L1_ffn_ref(_layernorm(h, axis=-1), L1_ffn_W1, L1_ffn_b1, L1_ffn_W2, L1_ffn_b2)
    return h

_drawn_inputs = setup_inputs


def setup_inputs(seed=0):
    import zlib

    import numpy as np

    out = dict(_drawn_inputs(seed))
    spreads = {'L0_tok_pixel_masks': (1.0, 0.2),
     'L0_tok_la_ln_q_g': (1.0, 0.6),
     'L0_tok_la_ln_q_b': (0.0, 0.8),
     'L0_tok_la_ln_kv_g': (1.0, 0.6),
     'L0_tok_la_ln_kv_b': (0.0, 0.1),
     'L0_tok_la_proj_b': (0.0, 0.1),
     'L0_tok_ga_ln_q_g': (1.0, 0.6),
     'L0_tok_ga_ln_q_b': (0.0, 0.8),
     'L0_tok_ga_ln_kv_g': (1.0, 0.6),
     'L0_tok_ga_ln_kv_b': (0.0, 0.319),
     'L0_tok_ga_proj_b': (0.0, 0.1),
     'L0_tok_mod_b': (0.0, 0.1),
     'L0_attn_gate_bias': (0.0, 0.1),
     'L0_attn_head_importance_bias': (0.0, 0.1),
     'L0_ffn_g1': (1.0, 0.6),
     'L0_ffn_g2': (1.0, 0.6),
     'L0_ffn_expert_bias': (0.0, 0.8),
     'L1_attn_gn_weight': (1.0, 0.6),
     'L1_attn_gn_bias': (0.0, 2.0)}
    factors = {'L0_tok_la_wq': 8.0,
     'L0_tok_ga_wq': 8.0,
     'L0_attn_W_q': 8.0,
     'L0_attn_W_k': 8.0,
     'L0_ffn_Wq': 8.0,
     'L0_ffn_Wkc': 8.0,
     'L0_ffn_Wr': 5.075,
     'L0_ffn_sW1': 3.263,
     'L0_ffn_sW2': 3.092,
     'L0_ffn_sW3': 3.287,
     'L0_ffn_eW1': 4.809,
     'L0_ffn_eW2': 4.499,
     'L0_ffn_eW3': 4.987,
     'L1_attn_W_Q': 8.0,
     'L1_attn_W_K': 8.0,
     'L1_attn_W_V': 8.0,
     'L1_attn_W_G': 8.0,
     'L1_attn_W_O': 8.0,
     'L1_ffn_b1': 21.935,
     'L1_ffn_b2': 64.0}
    for name, (base, spread) in spreads.items():
        noise = np.random.default_rng([zlib.crc32(name.encode()), seed]).standard_normal(out[name].shape)
        drawn = base * np.exp(spread * noise) if base else spread * noise
        out[name] = jnp.asarray(drawn.astype(out[name].dtype))
    for name, factor in factors.items():
        out[name] = (out[name] * factor).astype(out[name].dtype)
    return out
```

```python
from contextlib import ExitStack

import numpy as np
import concourse.bass as bass
from concourse import mybir

F32 = mybir.dt.float32
ALU = mybir.AluOpType
ACT = mybir.ActivationFunctionType
AX = mybir.AxisListType

P = 128
B = 64
T = 17
HW = 16
C = 256
PATCH_K = 588
K_REST = PATCH_K - 4 * P
NJ = 9
ITERS = 8
XC = NJ * P
CONV_N = 384
NCG = XC // CONV_N
NT = B * T
NW = B * HW
CH = NT // 4
LC = NW // 4
NEXP = 8
KVN = C + 1
KVS = KVN + 1
EPS_LN = 1e-5
EPS_RMS = 1e-6
MASKED = -1e30

VEC = [("la_ln_q_g", 2), ("la_ln_q_b", 2), ("la_ln_kv_g", 2), ("la_ln_kv_b", 2), ("la_proj_b", 2),
       ("ga_ln_q_g", 2), ("ga_ln_q_b", 2), ("ga_ln_kv_g", 2), ("ga_ln_kv_b", 2), ("ga_proj_b", 2),
       ("mod_b", 2), ("class_emb", 2), ("g1", 2), ("g2", 2), ("gn_weight", 2), ("gn_bias", 2),
       ("b1", 8), ("b2", 2)]
VCOL = {}
_n = 0
for _name, _k in VEC:
    VCOL[_name] = _n
    _n += _k
NVEC = _n


def causal_sizes():
    return [t + 1 for t in range(T)]


def build(nc, a, out):
    ctx = ExitStack()
    with ctx:
        def sb(name, shape):
            return ctx.enter_context(nc.sbuf_tensor(name, shape, F32))

        sems = {}

        def sem(name):
            if name not in sems:
                sems[name] = ctx.enter_context(nc.semaphore(name))
            return sems[name]

        ps = ctx.enter_context(nc.psum_tensor("ps", [P, 8, 512], F32))

        hbuf = sb("hbuf", [P, 2 * XC])
        xbuf = sb("xbuf", [P, 2 * XC])
        tbuf = sb("tbuf", [P, 2 * XC])
        ybuf = sb("ybuf", [P, 2 * NT])
        obuf = sb("obuf", [P, 2 * NT])
        lnv = sb("lnv", [P, NT])

        def chan(buf, n=NT):
            return buf[:, 0:2 * n].rearrange("p (m n) -> p m n", m=2)

        hT, xT, yT, oT, tT = chan(hbuf), chan(xbuf), chan(ybuf), chan(obuf), chan(tbuf)
        xW, yW, tW = chan(xbuf, NW), chan(ybuf, NW), chan(tbuf, NW)
        patch_emb = [hbuf[:, :].rearrange("p (m n) -> p m n", m=2),
                     xbuf[:, :].rearrange("p (m n) -> p m n", m=2)]
        patch_sq = tbuf[:, :].rearrange("p (m n) -> p m n", m=2)
        aggW = obuf[:, 0:ITERS * C].rearrange("p (i c) -> p i c", i=ITERS)

        vec = sb("vec", [P, NVEC])
        ident = sb("ident", [P, P])
        avg = sb("avg", [P, P])
        small = sb("small", [P, 512])
        wtok = sb("wtok", [P, 6 * 512])
        wattn = sb("wattn", [P, 2048 + 1024])

        def v(name, i=0):
            return vec[:, VCOL[name] + i:VCOL[name] + i + 1]

        def w2(ap, n=C):
            return ap.rearrange("p (k n) -> p k n", k=2)

        w_proj, w_mod = w2(wtok[:, 0:512]), w2(wtok[:, 512:1024])
        w_gkv = wtok[:, 1024:2048].rearrange("p (k h n) -> p k h n", k=2, h=2)
        w_gq = wtok[:, 2048:2560].rearrange("p (k h n) -> p k h n", k=2, h=2)
        w_gproj = w2(wtok[:, 2560:3072])
        w_l1qkv = wtok[:, 0:1536].rearrange("p (k h n) -> p k h n", k=2, h=2)
        w_l1g, w_l1o = w2(wtok[:, 1536:2048]), w2(wtok[:, 2048:2560])
        w_qkvg = wattn[:, 0:2048].rearrange("p (k h n) -> p k h n", k=2, h=2)
        w_go, w_o = w2(wattn[:, 2048:2560]), w2(wattn[:, 2560:3072])

        ARENA = 30892
        arena = sb("arena", [P, ARENA])
        at = [0]

        def take(n):
            at[0] += n
            assert at[0] <= ARENA, at[0]
            return arena[:, at[0] - n:at[0]]

        x_main = [take(4 * XC).rearrange("p (k n) -> p k n", k=4) for _ in range(2)]
        x_rest = [take(XC) for _ in range(2)]
        w_conv = take(4 * C).rearrange("p (k n) -> p k n", k=4)
        w_convr = take(C)
        kv_raw = take(NJ * 2 * KVS).rearrange("p (j s n) -> p j s n", j=NJ, s=2)
        prodW = take(NJ * C)
        sq_sum = take(XC)
        red = take(C).rearrange("p (m n) -> p m n", m=2)
        red_sq = take(C).rearrange("p (m n) -> p m n", m=2)
        rsq_sum = take(P)
        w_kv = take(1024).rearrange("p (k n) -> p k n", k=2)
        w_kvc = take(2 * 2 * KVS).rearrange("p (k s n) -> p k s n", k=2, s=2)
        w_lq = take(512).rearrange("p (k n) -> p k n", k=2)
        w_lqc = take(2 * KVS).rearrange("p (k n) -> p k n", k=2)
        q_win = take(C)
        qk_tmp = take(C)
        bias_row = take(3 * C)
        bcol = take(2 * P).rearrange("p (k n) -> p k n", k=2)
        sc = take(NJ * 8)
        sm8 = take(8)
        qb8 = take(8)
        st10 = take(10)
        mean10 = take(10)

        at[0] = 0
        w_exp = take(9 * 3 * 512).rearrange("p (e w k n) -> p e w k n", e=9, w=3, k=2)
        qkv_flat = take(T * 512)
        prodA = take(T * P)
        S = take(T * T * 8)
        tab = take(2 * T * 16 + 4 * T * 32)
        decay = take(T * T * 4)
        prodB = tbuf[:, 0:T * P]
        ffn_w = sb("ffn_w", [P, 1024 + 512 + 16])
        w_mqa = ffn_w[:, 0:1024].rearrange("p (k h n) -> p k h n", k=2, h=2)
        w_mo = w2(ffn_w[:, 1024:1536])
        w_r = ffn_w[:, 1536:1552].rearrange("p (k n) -> p k n", k=2)
        ebias = sb("ebias", [P, NEXP])
        lower = sb("lower", [P, NEXP * NEXP])
        sel = tbuf[0:NEXP, 0:NEXP * P]
        cmbT = lnv[0:NEXP, :]
        rope_c = tab[:, 0:T * 16].rearrange("p (t d) -> p t d", t=T)
        rope_s = tab[:, T * 16:2 * T * 16].rearrange("p (t d) -> p t d", t=T)
        xpos = tab[:, 2 * T * 16:].rearrange("p (f t d) -> p f t d", f=4, t=T)
        w_f1 = arena[:, 0:2048].rearrange("p (k n) -> p k n", k=2)
        w_f2 = arena[:, 2048:4096].rearrange("p (k n) -> p k n", k=8)
        tern = arena[:, 4096:8192]
        w_t1 = arena[:, 4096:6144].rearrange("p (k n) -> p k n", k=2)
        w_t2 = arena[:, 6144:8192].rearrange("p (k n) -> p k n", k=8)
        gam = small[:, 400:410]
        eh = [arena[:, 13824 + 272 * i:13824 + 272 * (i + 1)] for i in range(3)]
        esil = [arena[:, 13824 + 272 * (3 + i):13824 + 272 * (4 + i)] for i in range(2)]
        emul = [arena[:, 13824 + 272 * (5 + i):13824 + 272 * (6 + i)] for i in range(2)]
        hid = arena[:, 13824:13824 + 16 * CH].rearrange("p (u k n) -> p u k n", u=2, k=8)

        def qkv(n):
            return qkv_flat[:, 0:T * n].rearrange("p (t n) -> p t n", t=T)

        def after(eng, s, value):
            if not (isinstance(value, int) and value <= 0):
                eng.wait_ge(sem(s), value)

        norms = ["lnga", "ln0", "ln1", "rms1", "rms2", "ln2", "ln3"]

        def norm(name, step, n):
            before = [x for x in norms[:norms.index(name)] if step != "mu2" or not x.startswith("rms")]
            return "norm_" + step, 4 * len(before) + n

        block = ctx.enter_context(nc.Block())

        @block.sync
        def _(sp):
            def load(dst, src, s):
                sp.dma_start(dst, src).then_inc(sem(s), 16)

            def load_x(i, u):
                load(x_main[u], a["x_main"][i], f"x_in{u}")
                load(x_rest[u][0:K_REST, :], a["x_rest"][i], f"x_in{u}")

            load(w_conv, a["w_conv"], "w_conv_in")
            load(w_convr[0:K_REST, :], a["w_convr"], "w_conv_in")
            load_x(0, 0)
            load(vec[:, :], a["vec"], "w_first_in")
            load(ident[:, :], a["ident"], "w_first_in")
            load(w_kv, a["la_wkv"], "w_first_in")
            load(w_lq, a["la_wq"], "w_first_in")
            load(wtok[:, 0:512], a["la_proj_w"], "w_tok_in")
            load(wtok[:, 512:1024], a["mod_w"], "w_tok_in")
            load(wtok[:, 1024:2048], a["ga_wkv"], "w_tok_in")
            load(wtok[:, 2048:2560], a["ga_wq"], "w_tok_in")
            load(wtok[:, 2560:3072], a["ga_proj_w"], "w_tok_in")
            load_x(1, 1)
            load(wattn[:, 0:2048], a["attn_qkvg"], "w_attn_in")
            load(wattn[:, 2048:2560], a["attn_go"], "w_attn_in")
            load(wattn[:, 2560:3072], a["attn_o"], "w_attn_in")
            load(ffn_w[:, 0:1024], a["ffn_qkv"], "w_ffn_in")
            load(ffn_w[:, 1024:1536], a["ffn_o"], "w_ffn_in")
            load(ffn_w[:, 1536:1552], a["ffn_r"], "w_ffn_in")
            load(ebias[:, :], a["ebias"].partition_broadcast(P), "w_ffn_in")
            load(lower[:, :], a["lower"].partition_broadcast(P), "w_ffn_in")
            with sp.Fori(1, ITERS // 2) as k:
                for u in range(2):
                    sp.wait_ge(sem("conv_evac"), 12 * k + 6 * (u - 1))
                    load_x(2 * k + u, u)
            sp.wait_ge(sem("win_done"), ITERS)
            load(tab[:, 0:2 * T * 16], a["rope"].partition_broadcast(P), "tab_in")
            load(tab[:, 2 * T * 16:], a["xpos"].partition_broadcast(P), "tab_in")
            for h in range(2):
                load(decay[64 * h:64 * h + 64, :], a["decay"][h].partition_broadcast(64), "tab_in")
            for e in range(9):
                load(w_exp[:, e], a["experts"][:, e], "w_exp_in")
            sp.wait_ge(sem("gproj_ready"), 2)
            load(wtok[:, 0:1536], a["l1_qkv"], "w_l1_in")
            load(wtok[:, 1536:2048], a["l1_g"], "w_l1_in")
            load(wtok[:, 2048:2560], a["l1_o"], "w_l1_in")
            after(sp, *norm("rms2", "out", 4))
            load(sel, a["sel"], "sel_in")
            sp.wait_ge(sem("edown"), 72)
            load(w_f1, a["w1"], "w_f_in")
            load(w_f2, a["w2"], "w_f_in")
            for c in range(4):
                sp.wait_ge(sem("final"), 2 * c + 2)
                load(out[:, :, c * CH:(c + 1) * CH], hT[:, :, c * CH:(c + 1) * CH], "out_done")
            sp.wait_ge(sem("out_done"), 64)

        @block.tensor
        def _(pe):
            mm = nc.tensor.matmul

            pe.wait_ge(sem("const_set"), 1)
            pe.wait_ge(sem("w_scaled"), 1)
            for k in range(2):
                mm(ps[:, 2, :].rearrange("p (s n) -> p s n", s=2), avg[:, :], w_kvc[:, k, :, 0:C], start=(k == 0), stop=(k == 1))
            for k in range(2):
                last = mm(ps[:, 3, 0:C], avg[:, :], w_lqc[:, k, 0:C], start=(k == 0), stop=(k == 1))
            last.then_inc(sem("w_means"), 1)
            pe.wait_ge(sem("kv_bcol"), 1)
            for k in range(2):
                last = mm(ps[:, 4, :], bcol[:, k, :], w_kv[:, k, :], start=(k == 0), stop=(k == 1))
            last.then_inc(sem("kv_brow"), 1)
            pe.wait_ge(sem("q_bcol"), 1)
            for k in range(2):
                last = mm(ps[:, 5, 0:C], bcol[:, k, :], w_lq[:, k, :], start=(k == 0), stop=(k == 1))
            last.then_inc(sem("q_brow"), 1)
            pe.wait_ge(sem("w_kv_ready"), 1)
            pe.wait_ge(sem("w_conv_in"), 32)

            def window_tile(i, k, u):
                pe.wait_ge(sem(f"x_in{u}"), 32 * (k + 1) if isinstance(k, int) else k * 32 + 32)
                for g in range(2 * NCG):
                    c, m = g // 2, g % 2
                    after(pe, "conv_evac", 6 * i + (g - 1))
                    cols = slice(c * CONV_N, (c + 1) * CONV_N)
                    for kk in range(4):
                        mm(ps[:, g % 2, 0:CONV_N], w_conv[:, kk, m * P:(m + 1) * P],
                           x_main[u][:, kk, cols], start=(kk == 0), stop=False)
                    last = mm(ps[:, g % 2, 0:CONV_N], w_convr[0:K_REST, m * P:(m + 1) * P],
                              x_rest[u][0:K_REST, cols], start=False, stop=True)
                    last.then_inc(sem("conv_ready"), 1)
                pe.wait_ge(sem("conv_evac"), 6 * i + 6)
                for j in range(NJ):
                    b = 2 + 2 * ((u + j) % 2)
                    after(pe, "kv_evac", 9 * i + (j - 1))
                    for s in range(2):
                        for kk in range(2):
                            last = mm(ps[:, b + s, 0:KVN], patch_emb[u][:, kk, j * P:(j + 1) * P],
                                      w_kvc[:, kk, s, 0:KVN], start=(kk == 0), stop=(kk == 1))
                    last.then_inc(sem("kv_ready"), 1)
                pe.wait_ge(sem("sums_ready"), 1 * i + 1)
                after(pe, "win_done", 1 * i - 1)
                sb_ = ps[:, 6 + u, :]
                for j in range(NJ):
                    mm(sb_[:, 300 + j:301 + j], sq_sum[:, j * P:(j + 1) * P], avg[:, 0:1], start=True, stop=True)
                mm(sb_[:, 309:310], rsq_sum[:, :], avg[:, 0:1], start=True, stop=True)
                for kk in range(2):
                    last = mm(sb_[:, 0:KVN], red[:, kk, :], w_lqc[:, kk, 0:KVN], start=(kk == 0), stop=(kk == 1))
                last.then_inc(sem("stat_ready"), 1)

            for u in range(2):
                window_tile(u, 0, u)
            with pe.Fori(1, ITERS // 2) as k:
                for u in range(2):
                    window_tile(2 * k + u, k, u)

            pe.wait_ge(sem("kv_evac"), 9 * ITERS)
            for g in range(4):
                pe.wait_ge(sem("win_done"), 2 * g + 2)
                for i in range(2):
                    for m in range(2):
                        last = nc.tensor.transpose(ps[:, g, (2 * i + m) * P:(2 * i + m + 1) * P],
                                                   aggW[:, 2 * g + i, m * P:(m + 1) * P], ident[:, :])
                last.then_inc(sem("aggT_ready"), 1)

            def linear(name, w, src, n, banks, src_ready, drained=(), used=None):
                for s, value in drained:
                    pe.wait_ge(sem(s), value)
                for c in range(4):
                    for s, value in src_ready(c):
                        pe.wait_ge(sem(s), value)
                    for m in range(2):
                        after(pe, used or name + "_used", 2 * c + m - 3)
                        for k in range(2):
                            last = mm(ps[:, banks + (2 * c + m) % 4, 0:n], w[:, k, m * P:(m + 1) * P],
                                      src[:, k, c * n:(c + 1) * n], start=(k == 0), stop=(k == 1))
                        last.then_inc(sem(name + "_ready"), 1)

            def norm_stats(name, src, n, banks, src_ready, mean=True, drained=()):
                for s, value in drained:
                    pe.wait_ge(sem(s), value)
                for c in range(4):
                    b = banks + 2 * (c % 2)
                    cols = slice(c * n, (c + 1) * n)
                    for s, value in src_ready(c):
                        pe.wait_ge(sem(s), value)
                    after(pe, *norm(name, "out", c - 1))
                    if mean:
                        for k in range(2):
                            mm(ps[:, b, 0:n], avg[:, :], src[:, k, cols], start=(k == 0), stop=(k == 1))
                    after(pe, *norm(name, "sq", c + 1))
                    for k in range(2):
                        last = mm(ps[:, b + 1, 0:n], avg[:, :], chan(tbuf, 4 * n)[:, k, cols],
                                  start=(k == 0), stop=(k == 1))
                    last.then_inc(sem("norm_stat"), 1)

            def to_images(name, w, src, n, nt, banks, src_ready, drained=()):
                for s, value in drained:
                    pe.wait_ge(sem(s), value)
                for t in range(nt):
                    for s, value in src_ready(t):
                        pe.wait_ge(sem(s), value)
                    after(pe, name + "_used", t - 3)
                    for h in range(2):
                        for k in range(2):
                            last = mm(ps[64 * h:64 * h + 64, banks + t % 4, 0:n],
                                      src[:, k, t * B:(t + 1) * B], w[:, k, h, 0:n],
                                      start=(k == 0), stop=(k == 1))
                    last.then_inc(sem(name + "_ready"), 1)

            def to_channels(name, src, banks, ready, drained=()):
                for s, value in drained:
                    pe.wait_ge(sem(s), value)
                pe.wait_ge(sem(ready), 1)
                for g in range(5):
                    after(pe, name + "_used", g - 3)
                    for t in range(4 * g, min(4 * g + 4, T)):
                        last = nc.tensor.transpose(ps[:, banks + g % 4, (t % 4) * P:(t % 4 + 1) * P],
                                                   src[:, t, 0:P], ident[:, :])
                    last.then_inc(sem(name + "_ready"), 1)

            linear("proj", w_proj, xW, LC, 4, lambda c: [("aggT_used", c + 1)],
                   [("w_tok_in", 80), ("win_done", ITERS)], used="local_out")
            linear("mod", w_mod, yW, LC, 0, lambda c: [("local_out", 2 * c + 2)], [("aggT_used", 4)],
                   used="h_tok")
            norm_stats("lnga", yW, LC, 4, lambda c: [("local_out", 2 * c + 2)], drained=[("local_out", 8)])

            pe.wait_ge(sem("h_tok"), 8)
            pe.wait_ge(sem("cls_cols"), 1)
            for k in range(2):
                last = mm(ps[:, 0, 0:2], avg[:, :], small[:, 2 * k:2 * k + 2], start=(k == 0), stop=(k == 1))
            last.then_inc(sem("cls_stat"), 1)
            pe.wait_ge(sem("cls_bcast"), 1)
            for h in range(2):
                for k in range(2):
                    last = mm(ps[64 * h:64 * h + 64, 1, 0:P], small[:, 16 + 64 * k:16 + 64 * k + 64],
                              w_gq[:, k, h, :], start=(k == 0), stop=(k == 1))
            last.then_inc(sem("gq_ready"), 1)
            pe.wait_ge(sem("gq_used"), 1)
            to_images("gkv", w_gkv, xW, 256, HW, 0, lambda t: [("lnga_aff", t // 4 + 1)])
            pe.wait_ge(sem("gatt_done"), 1)
            after(pe, *norm("lnga", "out", 4))
            nc.tensor.transpose(ps[:, 4, 0:P], small[:, 272:400], ident[:, :]).then_inc(sem("gaggT_ready"), 1)
            pe.wait_ge(sem("gaggT_used"), 1)
            for m in range(2):
                for k in range(2):
                    last = mm(ps[:, 5 + m, 0:B], w_gproj[:, k, m * P:(m + 1) * P],
                              oT[:, k, 0:B], start=(k == 0), stop=(k == 1))
                last.then_inc(sem("gproj_ready"), 1)

            h0 = lambda c: [("h_tok", 2 * c + 2)] if c < 3 else [("h_tok", 8), ("h_cls", 2)]
            norm_stats("ln0", hT, CH, 0, h0, drained=[("gkv_used", HW)])
            full = lambda name, total: (lambda c: [(name, total)])
            to_images("qkv0", w_qkvg, xT, 512, T, 4, lambda t: [norm("ln0", "out", min(4, (t * B + B - 1) // CH + 1))],
                      [("w_attn_in", 48), ("gaggT_used", 1), ("h_cls", 2)])
            linear("go", w_go, xT, CH, 0, lambda c: [norm("ln0", "out", 4)])
            to_channels("att0", qkv(512), 4, "att0_done", [("qkv0_used", T)])
            linear("wo", w_o, oT, CH, 0, lambda c: [("att0_gated", c + 1)], [("go_used", 8)])

            norm_stats("ln1", hT, CH, 4, lambda c: [("wo_used", 2 * c + 2)], drained=[("att0_used", 5)])
            norm_stats("rms1", xT, CH, 0, lambda c: [norm("ln1", "out", c + 1)], mean=False, drained=[("wo_used", 8)])
            to_images("qkv1", w_mqa, yT, 256, T, 4, lambda t: [norm("rms1", "out", min(4, (t * B + B - 1) // CH + 1))],
                      [("w_ffn_in", 80), norm("ln1", "out", 4)])
            to_channels("att1", qkv(256), 0, "att1_done", [norm("rms1", "out", 4)])
            linear("mo", w_mo, oT, CH, 4, lambda c: [("att1_used", 5)], [("qkv1_used", T)])
            norm_stats("rms2", xT, CH, 0, lambda c: [("mo_used", 2 * c + 2)], mean=False,
                       drained=[("att1_used", 5)])

            after(pe, *norm("rms2", "out", 4))
            pe.wait_ge(sem("mo_used"), 8)
            for t in range(9):
                n = P if t < 8 else NT - 8 * P
                for k in range(2):
                    last = mm(ps[0:n, 4, t * NEXP:(t + 1) * NEXP], yT[:, k, t * P:t * P + n], w_r[:, k, :],
                              start=(k == 0), stop=(k == 1))
            last.then_inc(sem("logits_ready"), 1)
            pe.wait_ge(sem("combine_done"), 1)
            cw = small[:, 0:72].rearrange("p (t e) -> p t e", t=9)
            for t in range(9):
                n = P if t < 8 else NT - 8 * P
                last = nc.tensor.transpose(ps[0:NEXP, 5 + t // 4, (t % 4) * P:(t % 4) * P + n],
                                           cw[0:n, t, :], ident[0:n, 0:n])
            last.then_inc(sem("cmb_ready"), 1)
            pe.wait_ge(sem("cmb_used"), 1)
            pe.wait_ge(sem("w_exp_in"), 16 * 9)
            pe.wait_ge(sem("sel_in"), 16)

            with pe.Fori(0, 4) as c:
                for n in range(18 + 2):
                    if n < 18:
                        e, m = n // 2, n % 2
                        pe.wait_ge(sem("eh_ready"), c * 18 + max(n - 1, 0))
                        for w in range(2):
                            for k in range(2):
                                last = mm(ps[:, 2 + 2 * (n % 2) + w, 0:CH],
                                          w_exp[:, e, w, k, m * P:(m + 1) * P],
                                          yT[:, k, bass.ts(c, CH)], start=(k == 0), stop=(k == 1))
                            if w == 0 and m == 0 and e < NEXP:
                                mm(ps[:, 6 + e % 2, 0:CH], sel[:, e * P:(e + 1) * P],
                                   cmbT[:, bass.ts(c, CH)], start=True, stop=True)
                        last.then_inc(sem("eup_ready"), 1)
                    if n >= 2:
                        d = n - 2
                        e, k = d // 2, d % 2
                        pe.wait_ge(sem("eh_ready"), c * 18 + (d + 1))
                        if d == 0:
                            pe.wait_ge(sem("moe_used"), c * 2)
                        for m in range(2):
                            last = mm(ps[:, m, 0:CH], w_exp[:, e, 2, k, m * P:(m + 1) * P], eh[d % 3],
                                      start=(d == 0), stop=(d == 17))
                        last.then_inc(sem("edown"), 1)

            norm_stats("ln2", hT, CH, 2, lambda c: [("moe_used", 8)])
            to_images("qkv2", w_l1qkv, xT, 384, T, 4,
                      lambda t: [norm("ln2", "out", min(4, (t * B + B - 1) // CH + 1))], [("w_l1_in", 48), norm("ln2", "out", 4)])
            linear("g", w_l1g, xT, CH, 0, lambda c: [norm("ln2", "out", 4)])
            to_channels("att2", qkv(384), 4, "att2_done", [("qkv2_used", T)])
            pe.wait_ge(sem("att2_used"), 5)
            pe.wait_ge(sem("gam_sum"), 1)
            mm(ps[:, 4, 0:2], avg[:, :], gam[:, 0:2], start=True, stop=True).then_inc(sem("gam_ready"), 1)
            linear("l1o", w_l1o, oT, CH, 0, lambda c: [("att2_gated", c + 1)], [("g_used", 8)])

            pe.wait_ge(sem("tern_done"), 1)
            norm_stats("ln3", hT, CH, 4, lambda c: [("l1o_used", 2 * c + 2)], drained=[("l1o_used", 8)])
            for c in range(4):
                after(pe, *norm("ln3", "out", c + 1))
                for f in range(8):
                    after(pe, "hid_done", 8 * c + f - 3)
                    for k in range(2):
                        last = mm(ps[:, f % 4, 0:CH], w_t1[:, k, f * P:(f + 1) * P],
                                  xT[:, k, c * CH:(c + 1) * CH], start=(k == 0), stop=(k == 1))
                    last.then_inc(sem("fc1_ready"), 1)
                pe.wait_ge(sem("hid_done"), 8 * c + 8)
                if c == 0:
                    after(pe, *norm("ln3", "out", 4))
                for m in range(2):
                    after(pe, "final", 2 * c + m - 3)
                    for f in range(8):
                        last = mm(ps[:, 4 + (2 * c + m) % 4, 0:CH], w_t2[:, f, m * P:(m + 1) * P],
                                  hid[:, c % 2, f, :], start=(f == 0), stop=(f == 7))
                    last.then_inc(sem("fc2_ready"), 1)

        @block.scalar
        def _(act):
            A = nc.scalar.activation

            def rstd_of(i):
                act.wait_ge(sem("var10"), 1 * i + 1)
                A(st10, st10, ACT.Ln).then_inc(sem("ln10"), 1)
                act.wait_ge(sem("ln10"), 1 * i + 1)
                A(st10, st10, ACT.Exp, scale=-0.5).then_inc(sem("rstd10"), 1)

            def exp_of(i):
                act.wait_ge(sem("sc_max"), 1 * i + 1)
                A(sc, sc, ACT.Exp, scale=C ** -0.5).then_inc(sem("sc_exp"), 1)

            def window_tile(i, u, first=False):
                for g in range(2 * NCG):
                    c, m = g // 2, g % 2
                    cols = slice(c * CONV_N, (c + 1) * CONV_N)
                    act.wait_ge(sem("conv_ready"), 6 * i + (g + 1))
                    if g == 0:
                        after(act, "sums_ready", 1 * i)
                        after(act, "kv_ready", 9 * i - 9)
                    A(patch_emb[u][:, m, cols], ps[:, g % 2, 0:CONV_N], ACT.Copy)
                    A(patch_sq[:, m, cols], ps[:, g % 2, 0:CONV_N], ACT.Square).then_inc(sem("conv_evac"), 1)
                    if g == 0 and not first:
                        rstd_of(i - 1)
                    if g == 3 and not first:
                        exp_of(i - 1)
                after(act, "win_done", 1 * i)
                for j in range(NJ):
                    act.wait_ge(sem("kv_ready"), 9 * i + (j + 1))
                    b = 2 + 2 * ((u + j) % 2)
                    A(kv_raw[:, j, :, 0:KVN], ps[:, b:b + 2, 0:KVN], ACT.Copy).then_inc(sem("kv_evac"), 1)

            act.wait_ge(sem("w_first_in"), 64)
            for u in range(2):
                window_tile(u, u, first=(u == 0))
            with act.Fori(1, ITERS // 2) as k:
                for u in range(2):
                    window_tile(2 * k + u, u)
            rstd_of(ITERS - 1)
            exp_of(ITERS - 1)

            for g in range(4):
                act.wait_ge(sem("aggT_ready"), g + 1)
                if g == 0:
                    act.wait_ge(sem("stat_ready"), ITERS)
                    act.wait_ge(sem("kv_ready"), 9 * ITERS)
                A(xW[:, :, 2 * g * P:(2 * g + 2) * P].rearrange("p m (i n) -> p m i n", i=2),
                  ps[:, g, :].rearrange("p (i m n) -> p m i n", i=2, m=2), ACT.Copy).then_inc(sem("aggT_used"), 1)

            def norm_act(name, src, n, src_ready, mean=True, drained=()):
                sq = chan(tbuf, 4 * n)
                for s, value in drained:
                    act.wait_ge(sem(s), value)

                def squares(c):
                    cols = slice(c * n, (c + 1) * n)
                    for s, value in src_ready(c):
                        act.wait_ge(sem(s), value)
                    A(sq[:, :, cols], src[:, :, cols], ACT.Square).then_inc(sem("norm_sq"), 1)

                def mean_sq(c):
                    b = name_banks[name] + 2 * (c % 2)
                    after(act, *norm(name, "stat", c + 1))
                    A(lnv[:, c * n:(c + 1) * n], ps[:, b, 0:n], ACT.Square).then_inc(sem("norm_mu2"), 1)

                def rstd(c):
                    cols = slice(c * n, (c + 1) * n)
                    after(act, *norm(name, "var", c + 1))
                    A(lnv[:, cols], lnv[:, cols], ACT.Ln).then_inc(sem("norm_ln"), 1)
                    after(act, *norm(name, "ln", c + 1))
                    A(lnv[:, cols], lnv[:, cols], ACT.Exp, scale=-0.5).then_inc(sem("norm_rstd"), 1)

                for c in range(4 + 2):
                    if c < 4:
                        squares(c)
                    if mean and 1 <= c < 5:
                        mean_sq(c - 1)
                    if c >= 2:
                        rstd(c - 2)

            name_banks = {"lnga": 4, "ln0": 0, "ln1": 4, "rms1": 0, "rms2": 0, "ln2": 2, "ln3": 4}

            act.wait_ge(sem("w_tok_in"), 80)
            for c in range(4):
                for m in range(2):
                    act.wait_ge(sem("mod_ready"), 2 * c + m + 1)
                    A(hT[:, m, c * LC:(c + 1) * LC], ps[:, (2 * c + m) % 4, 0:LC], ACT.Identity,
                      bias=v("mod_b", m)).then_inc(sem("h_tok"), 1)
            norm_act("lnga", yW, LC, lambda c: [("local_out", 2 * c + 2)])
            for c in range(4):
                after(act, *norm("lnga", "out", c + 1))
                for m in range(2):
                    last = A(xW[:, m, c * LC:(c + 1) * LC], xW[:, m, c * LC:(c + 1) * LC], ACT.Identity,
                             bias=v("ga_ln_kv_b", m), scale=v("ga_ln_kv_g", m))
                last.then_inc(sem("lnga_aff"), 1)
            act.wait_ge(sem("cls_var"), 1)
            A(small[:, 8:9], small[:, 8:9], ACT.Ln).then_inc(sem("cls_ln"), 1)
            act.wait_ge(sem("cls_ln"), 1)
            A(small[:, 8:9], small[:, 8:9], ACT.Exp, scale=-0.5).then_inc(sem("cls_rstd"), 1)
            gkv = qkv_flat[:, 0:HW * 256].rearrange("p (t n) -> p t n", t=HW)
            for t in range(HW):
                act.wait_ge(sem("gkv_ready"), t + 1)
                A(gkv[:, t, :], ps[:, t % 4, 0:256], ACT.Copy).then_inc(sem("gkv_used"), 1)
            act.wait_ge(sem("gsc_max"), 1)
            A(S[:, 0:64], S[:, 0:64], ACT.Exp, scale=C ** -0.5).then_inc(sem("gsc_exp"), 1)

            norm_act("ln0", hT, CH, lambda c: [("h_tok", 8), ("h_cls", 2)])
            for t in range(T):
                act.wait_ge(sem("qkv0_ready"), t + 1)
                if t == 0:
                    act.wait_ge(sem("gatt_done"), 1)
                A(qkv(512)[:, t, 0:384], ps[:, 4 + t % 4, 0:384], ACT.Copy)
                A(qkv(512)[:, t, 384:512], ps[:, 4 + t % 4, 384:512], ACT.Sigmoid).then_inc(sem("qkv0_used"), 1)
            for c in range(4):
                for m in range(2):
                    act.wait_ge(sem("go_ready"), 2 * c + m + 1)
                    A(yT[:, m, c * CH:(c + 1) * CH], ps[:, (2 * c + m) % 4, 0:CH],
                      ACT.Sigmoid).then_inc(sem("go_used"), 1)
            act.wait_ge(sem("att0_max"), 1)
            A(S, S, ACT.Exp, scale=16 ** -0.5).then_inc(sem("att0_exp"), 1)

            def from_images(name, banks):
                for g in range(5):
                    n = min(4, T - 4 * g)
                    act.wait_ge(sem(name + "_ready"), g + 1)
                    A(oT[:, :, 4 * g * B:(4 * g + n) * B].rearrange("p m (t b) -> p m t b", t=n),
                      ps[:, banks + g % 4, 0:n * P].rearrange("p (t m b) -> p m t b", t=n, m=2),
                      ACT.Copy).then_inc(sem(name + "_used"), 1)

            from_images("att0", 4)

            norm_act("ln1", hT, CH, lambda c: [("wo_used", 2 * c + 2)], drained=[("att0_done", 1)])
            norm_act("rms1", xT, CH, lambda c: [norm("ln1", "out", c + 1)], mean=False)
            for t in range(T):
                act.wait_ge(sem("qkv1_ready"), t + 1)
                if t == 0:
                    act.wait_ge(sem("att0_ready"), 5)
                A(qkv(256)[:, t, :], ps[:, 4 + t % 4, 0:256], ACT.Copy).then_inc(sem("qkv1_used"), 1)
            act.wait_ge(sem("att1_max"), 1)
            A(S[:, 0:T * T * 2], S[:, 0:T * T * 2], ACT.Exp, scale=64 ** -0.5).then_inc(sem("att1_exp"), 1)
            from_images("att1", 0)
            norm_act("rms2", xT, CH, lambda c: [("mo_used", 2 * c + 2)], mean=False, drained=[("att1_done", 1)])
            act.wait_ge(sem("lg_max"), 1)
            A(small[:, 0:72], small[:, 0:72], ACT.Exp).then_inc(sem("lg_exp"), 1)
            act.wait_ge(sem("rw_max"), 1)
            A(small[:, 72:144], small[:, 72:144], ACT.Exp).then_inc(sem("rw_exp"), 1)
            act.wait_ge(sem("cmb_ready"), 1)
            A(cmbT[:, 0:512], ps[0:NEXP, 5, :], ACT.Copy)
            A(cmbT[:, 512:1024], ps[0:NEXP, 6, :], ACT.Copy)
            A(cmbT[:, 1024:NT], ps[0:NEXP, 7, 0:NT - 1024], ACT.Copy).then_inc(sem("cmb_used"), 1)
            with act.Fori(0, 4) as c:
                for n in range(18):
                    act.wait_ge(sem("eup_ready"), c * 18 + (n + 1))
                    act.wait_ge(sem("eh_ready"), c * 18 + max(n - 1, 0))
                    A(esil[n % 2], ps[:, 2 + 2 * (n % 2), 0:CH], ACT.Silu).then_inc(sem("esil_ready"), 1)

            norm_act("ln2", hT, CH, lambda c: [("moe_used", 8)])
            for t in range(T):
                act.wait_ge(sem("qkv2_ready"), t + 1)
                A(qkv(384)[:, t, :], ps[:, 4 + t % 4, 0:384], ACT.Copy).then_inc(sem("qkv2_used"), 1)
            for c in range(4):
                for m in range(2):
                    act.wait_ge(sem("g_ready"), 2 * c + m + 1)
                    A(yT[:, m, c * CH:(c + 1) * CH], ps[:, (2 * c + m) % 4, 0:CH],
                      ACT.Silu).then_inc(sem("g_used"), 1)
            act.wait_ge(sem("gn_var"), 1)
            A(S[:, 0:68], S[:, 0:68], ACT.Ln).then_inc(sem("gn_ln"), 1)
            act.wait_ge(sem("gn_ln"), 1)
            A(S[:, 0:68], S[:, 0:68], ACT.Exp, scale=-0.5).then_inc(sem("gn_rstd"), 1)
            from_images("att2", 4)

            norm_act("ln3", hT, CH, lambda c: [("l1o_used", 2 * c + 2)], drained=[("att2_done", 1)])
            for c in range(4):
                for f in range(8):
                    act.wait_ge(sem("fc1_ready"), 8 * c + f + 1)
                    if f == 0:
                        after(act, "fc2_ready", 2 * c - 2)
                        act.wait_ge(sem("att2_ready"), 5)
                    A(hid[:, c % 2, f, :], ps[:, f % 4, 0:CH], ACT.Relu,
                      bias=v("b1", f)).then_inc(sem("hid_done"), 1)

        @block.vector
        def _(dve):
            V = nc.vector
            steps = [0]

            def mark(ins):
                steps[0] += 1
                ins.then_inc(sem("dve_step"), 1)
                return steps[0]

            def need(count):
                dve.wait_ge(sem("dve_step"), count)

            def link(ins):
                need(mark(ins))

            def bc(ap, shape):
                return ap.to_broadcast(shape)

            V.memset(avg[:, :], 1.0 / C).then_inc(sem("const_set"), 1)
            dve.wait_ge(sem("w_first_in"), 64)
            for k in range(2):
                V.tensor_scalar(w_kvc[:, k, :, 0:C], w_kv[:, k, :].rearrange("p (s n) -> p s n", s=2),
                                v("la_ln_kv_g", k), None, ALU.mult)
                last = V.tensor_scalar(w_lqc[:, k, 0:C], w_lq[:, k, :], v("la_ln_q_g", k), None, ALU.mult)
            link(last)
            link(V.memset(sm8, 0.0))
            V.memset(sm8, 0.0).then_inc(sem("w_scaled"), 1)
            V.memset(w_kvc[:, :, :, C:KVS], 1.0 / C)
            link(V.memset(w_lqc[:, :, C:KVS], 1.0 / C))
            for k in range(2):
                last = V.tensor_scalar(bcol[:, k, :], avg[:, :], v("la_ln_kv_b", k), float(C), ALU.mult, ALU.mult)
            last.then_inc(sem("kv_bcol"), 1)
            dve.wait_ge(sem("w_means"), 1)
            for k in range(2):
                V.tensor_tensor(w_kvc[:, k, :, 0:C], w_kvc[:, k, :, 0:C],
                                ps[:, 2, :].rearrange("p (s n) -> p s n", s=2), ALU.subtract)
                last = V.tensor_tensor(w_lqc[:, k, 0:C], w_lqc[:, k, 0:C], ps[:, 3, 0:C], ALU.subtract)
            link(last)
            dve.wait_ge(sem("kv_brow"), 1)
            link(V.tensor_copy(bias_row[:, 0:2 * C], ps[:, 4, :]))
            for k in range(2):
                last = V.tensor_scalar(bcol[:, k, :], avg[:, :], v("la_ln_q_b", k), float(C), ALU.mult, ALU.mult)
            last.then_inc(sem("q_bcol"), 1)
            dve.wait_ge(sem("q_brow"), 1)
            V.tensor_copy(bias_row[:, 2 * C:3 * C], ps[:, 5, 0:C]).then_inc(sem("w_kv_ready"), 1)
            dve.wait_ge(sem("w_kv_ready"), 1)

            NSTEP = 19
            sc3 = sc.rearrange("p (j h) -> p j h", j=NJ)

            def window_tile(i, u):
                base = [0]

                def wlink(ins):
                    base[0] += 1
                    ins.then_inc(sem("win_step"), 1)
                    dve.wait_ge(sem("win_step"), NSTEP * i + base[0])

                dve.wait_ge(sem("conv_evac"), 6 * i + 6)
                after(dve, "stat_ready", 1 * i)
                wlink(V.tensor_reduce(red_sq, patch_emb[u].rearrange("p m (j n) -> p m n j", j=NJ), AX.X, ALU.add))
                wlink(V.tensor_scalar(red, red_sq, 1.0 / NJ, None, ALU.mult))
                V.tensor_copy(yW[:, :, bass.ts(i, P)] if not isinstance(i, int) else yW[:, :, i * P:(i + 1) * P], red)
                wlink(V.tensor_tensor(red_sq, red, red, ALU.mult))
                wlink(V.tensor_tensor(rsq_sum, red_sq[:, 0, :], red_sq[:, 1, :], ALU.add))
                V.tensor_tensor(sq_sum, patch_sq[:, 0, :], patch_sq[:, 1, :], ALU.add).then_inc(sem("sums_ready"), 1)

                dve.wait_ge(sem("stat_ready"), 1 * i + 1)
                dve.wait_ge(sem("kv_evac"), 9 * i + 9)
                st = ps[:, 6 + u, :]
                V.tensor_copy(mean10[:, 0:NJ], kv_raw[:, :, 0, C])
                wlink(V.tensor_copy(mean10[:, NJ:NJ + 1], st[:, C:C + 1]))
                wlink(V.tensor_tensor(mean10, mean10, mean10, ALU.mult))
                wlink(V.tensor_tensor(st10, st[:, 300:310], mean10, ALU.subtract))
                V.tensor_scalar(st10, st10, 0.0, EPS_LN, ALU.max, ALU.add).then_inc(sem("var10"), 1)
                dve.wait_ge(sem("rstd10"), 1 * i + 1)
                wlink(V.scalar_tensor_tensor(out=q_win, in0=st[:, 0:C], scalar=st10[:, NJ:NJ + 1],
                                             in1=bias_row[:, 2 * C:3 * C], op0=ALU.mult, op1=ALU.add))
                prod3 = prodW.rearrange("p (j n) -> p j n", j=NJ)
                V.tensor_tensor(qk_tmp, q_win, bias_row[:, 0:C], ALU.mult)
                wlink(V.tensor_tensor(prod3, kv_raw[:, :, 0, 0:C],
                                      q_win.unsqueeze(1).to_broadcast([P, NJ, C]), ALU.mult))
                V.tensor_reduce(qb8, qk_tmp.rearrange("p (h d) -> p h d", h=8), AX.X, ALU.add)
                wlink(V.tensor_reduce(sc, prodW.rearrange("p (a d) -> p a d", d=32), AX.X, ALU.add))
                r9 = st10[:, 0:NJ].unsqueeze(2).to_broadcast([P, NJ, 8])
                wlink(V.tensor_tensor(sc3, sc3, r9, ALU.mult))
                wlink(V.tensor_tensor(sc3, sc3, qb8.unsqueeze(1).to_broadcast([P, NJ, 8]), ALU.add))
                wlink(V.tensor_reduce(sm8, sc.rearrange("p (j h) -> p h j", j=NJ), AX.X, ALU.max))
                V.tensor_tensor(sc3, sc3, sm8.unsqueeze(1).to_broadcast([P, NJ, 8]),
                                ALU.subtract).then_inc(sem("sc_max"), 1)
                dve.wait_ge(sem("sc_exp"), 1 * i + 1)
                wlink(V.tensor_reduce(sm8, sc.rearrange("p (j h) -> p h j", j=NJ), AX.X, ALU.add))
                wlink(V.reciprocal(qb8, sm8))
                wlink(V.tensor_tensor(sc3, sc3, qb8.unsqueeze(1).to_broadcast([P, NJ, 8]), ALU.mult))
                wlink(V.tensor_tensor(sc3, sc3, r9, ALU.mult))
                wlink(V.tensor_tensor(prodW.rearrange("p (j h d) -> p j h d", j=NJ, h=8),
                                      kv_raw[:, :, 1, 0:C].rearrange("p j (h d) -> p j h d", h=8),
                                      sc3.unsqueeze(3).to_broadcast([P, NJ, 8, 32]), ALU.mult))
                wlink(V.tensor_reduce(qk_tmp, prodW.rearrange("p (j n) -> p n j", j=NJ), AX.X, ALU.add))
                dst = aggW[:, i, :] if isinstance(i, int) else obuf[:, bass.ts(i, C)]
                V.tensor_tensor(dst, qk_tmp, bias_row[:, C:2 * C], ALU.add).then_inc(sem("win_done"), 1)
                dve.wait_ge(sem("win_done"), 1 * i + 1)
                assert base[0] == NSTEP, base[0]

            for u in range(2):
                window_tile(u, u)
            with dve.Fori(1, ITERS // 2) as k:
                for u in range(2):
                    window_tile(2 * k + u, u)

            for c in range(4):
                for m in range(2):
                    dve.wait_ge(sem("proj_ready"), 2 * c + m + 1)
                    y = yW[:, m, c * LC:(c + 1) * LC]
                    V.scalar_tensor_tensor(out=y, in0=ps[:, 4 + (2 * c + m) % 4, 0:LC], scalar=v("la_proj_b", m),
                                           in1=y, op0=ALU.add, op1=ALU.add).then_inc(sem("local_out"), 1)

            def norm_dve(name, src, dst, n, banks, eps, mean=True, gain=None, drained=()):
                for s, value in drained:
                    dve.wait_ge(sem(s), value)

                def variance(c):
                    b = banks + 2 * (c % 2)
                    cols = slice(c * n, (c + 1) * n)
                    after(dve, *norm(name, "stat", c + 1))
                    if mean:
                        after(dve, *norm(name, "mu2", c + 1))
                        link(V.tensor_tensor(lnv[:, cols], ps[:, b + 1, 0:n], lnv[:, cols], ALU.subtract))
                        V.tensor_scalar(lnv[:, cols], lnv[:, cols], 0.0, eps, ALU.max,
                                        ALU.add).then_inc(sem("norm_var"), 1)
                        x = mark(V.tensor_tensor(dst[:, :, cols], src[:, :, cols],
                                                 ps[:, b, 0:n].unsqueeze(1).to_broadcast([P, 2, n]), ALU.subtract))
                        return x
                    V.tensor_scalar(lnv[:, cols], ps[:, b + 1, 0:n], eps, None,
                                    ALU.add).then_inc(sem("norm_var"), 1)
                    return None

                def scale(c, x):
                    cols = slice(c * n, (c + 1) * n)
                    after(dve, *norm(name, "rstd", c + 1))
                    if mean:
                        need(x)
                        V.tensor_tensor(dst[:, :, cols], dst[:, :, cols],
                                        lnv[:, cols].unsqueeze(1).to_broadcast([P, 2, n]),
                                        ALU.mult).then_inc(sem("norm_out"), 1)
                    else:
                        for m in range(2):
                            last = V.scalar_tensor_tensor(out=dst[:, m, cols], in0=src[:, m, cols],
                                                          scalar=v(gain, m), in1=lnv[:, cols],
                                                          op0=ALU.mult, op1=ALU.mult)
                        last.then_inc(sem("norm_out"), 1)

                x = variance(0)
                for c in range(4):
                    nxt = variance(c + 1) if c < 3 else None
                    scale(c, x)
                    x = nxt

            norm_dve("lnga", yW, xW, LC, 4, EPS_LN, drained=[("proj_ready", 8)])

            for k in range(2):
                V.tensor_copy(small[:, 2 * k:2 * k + 1], v("class_emb", k))
                last = V.tensor_tensor(small[:, 2 * k + 1:2 * k + 2], v("class_emb", k), v("class_emb", k), ALU.mult)
            last.then_inc(sem("cls_cols"), 1)
            dve.wait_ge(sem("cls_cols"), 1)
            dve.wait_ge(sem("cls_stat"), 1)
            link(V.tensor_copy(small[:, 6:8], ps[:, 0, 0:2]))
            link(V.tensor_tensor(small[:, 5:6], small[:, 6:7], small[:, 6:7], ALU.mult))
            link(V.tensor_tensor(small[:, 8:9], small[:, 7:8], small[:, 5:6], ALU.subtract))
            V.tensor_scalar(small[:, 8:9], small[:, 8:9], 0.0, EPS_LN, ALU.max, ALU.add).then_inc(sem("cls_var"), 1)
            dve.wait_ge(sem("cls_rstd"), 1)
            for k in range(2):
                link(V.tensor_scalar(small[:, 10 + k:11 + k], v("class_emb", k), small[:, 6:7], small[:, 8:9],
                                     ALU.subtract, ALU.mult))
                link(V.scalar_tensor_tensor(out=small[:, 12 + k:13 + k], in0=small[:, 10 + k:11 + k],
                                            scalar=v("ga_ln_q_g", k), in1=v("ga_ln_q_b", k),
                                            op0=ALU.mult, op1=ALU.add))
            for k in range(2):
                last = V.tensor_scalar(small[:, 16 + 64 * k:80 + 64 * k], avg[:, 0:64], small[:, 12 + k:13 + k],
                                       float(C), ALU.mult, ALU.mult)
            last.then_inc(sem("cls_bcast"), 1)
            dve.wait_ge(sem("gq_ready"), 1)
            gq = small[:, 144:144 + P]
            V.tensor_copy(gq, ps[:, 1, 0:P]).then_inc(sem("gq_used"), 1)
            dve.wait_ge(sem("gq_used"), 1)

            gkv = qkv_flat[:, 0:HW * 256].rearrange("p (t n) -> p t n", t=HW)
            dve.wait_ge(sem("gkv_used"), HW)
            pa = prodA[:, 0:HW * P]
            gs = S[:, 0:64]
            gs3 = gs.rearrange("p (t h) -> p t h", t=HW)
            g4 = S[:, 64:68]
            link(V.tensor_tensor(pa.rearrange("p (t n) -> p t n", t=HW), gkv[:, :, 0:P],
                                 gq.unsqueeze(1).to_broadcast([P, HW, P]), ALU.mult))
            link(V.tensor_reduce(gs, pa.rearrange("p (a d) -> p a d", d=32), AX.X, ALU.add))
            link(V.tensor_reduce(g4, gs.rearrange("p (t h) -> p h t", t=HW), AX.X, ALU.max))
            V.tensor_tensor(gs3, gs3, g4.unsqueeze(1).to_broadcast([P, HW, 4]),
                            ALU.subtract).then_inc(sem("gsc_max"), 1)
            dve.wait_ge(sem("gsc_exp"), 1)
            link(V.tensor_reduce(g4, gs.rearrange("p (t h) -> p h t", t=HW), AX.X, ALU.add))
            link(V.reciprocal(S[:, 68:72], g4))
            link(V.tensor_tensor(gs3, gs3, S[:, 68:72].unsqueeze(1).to_broadcast([P, HW, 4]), ALU.mult))
            link(V.tensor_tensor(pa.rearrange("p (t h d) -> p t h d", t=HW, h=4),
                                 gkv[:, :, P:2 * P].rearrange("p t (h d) -> p t h d", h=4),
                                 gs3.unsqueeze(3).to_broadcast([P, HW, 4, 32]), ALU.mult))
            gagg = small[:, 272:400]
            V.tensor_reduce(gagg, pa.rearrange("p (t n) -> p n t", t=HW), AX.X, ALU.add).then_inc(sem("gatt_done"), 1)
            dve.wait_ge(sem("gaggT_ready"), 1)
            V.tensor_copy(oT[:, :, 0:B], ps[:, 4, 0:P].rearrange("p (m b) -> p m b", m=2)).then_inc(sem("gaggT_used"), 1)
            link(V.tensor_tensor(small[:, 4:6], vec[:, VCOL["class_emb"]:VCOL["class_emb"] + 2],
                                 vec[:, VCOL["ga_proj_b"]:VCOL["ga_proj_b"] + 2], ALU.add))
            for m in range(2):
                dve.wait_ge(sem("gproj_ready"), m + 1)
                V.tensor_scalar(hT[:, m, NW:NT], ps[:, 5 + m, 0:B], small[:, 4 + m:5 + m], None,
                                ALU.add).then_inc(sem("h_cls"), 1)

            def rotate(x, nh, d, cs, sn):
                shape = [P, T, nh, d]
                xv = x.rearrange("p t (h d) -> p t h d", h=nh)
                pv = prodA.rearrange("p (t h d) -> p t h d", t=T, h=nh)
                c_ = cs.unsqueeze(2).to_broadcast(shape)
                h_ = d // 2
                half = [P, T, nh, h_]
                V.tensor_tensor(pv[:, :, :, 0:h_], xv[:, :, :, h_:d],
                                sn[:, :, 0:h_].unsqueeze(2).to_broadcast(half), ALU.mult)
                link(V.tensor_tensor(pv[:, :, :, h_:d], xv[:, :, :, 0:h_],
                                     sn[:, :, h_:d].unsqueeze(2).to_broadcast(half), ALU.mult))
                link(V.tensor_tensor(xv, xv, c_, ALU.mult))
                link(V.tensor_tensor(xv, xv, pv, ALU.add))

            prods = [prodA, prodB]

            def scores(q, k_, nh, d, sizes, shared=False):
                width = nh * d
                s_done, p_done = [], []

                def product(t):
                    n = sizes[t]
                    if t >= 2:
                        need(s_done[t - 2])
                    o = prods[t % 2][:, 0:n * width]
                    if shared:
                        p_done.append(mark(V.tensor_tensor(
                            o.rearrange("p (k h d) -> p k h d", k=n, h=nh),
                            k_[:, 0:n, :].unsqueeze(2).to_broadcast([P, n, nh, d]),
                            q[:, t, :].rearrange("p (h d) -> p h d", h=nh).unsqueeze(1).to_broadcast([P, n, nh, d]),
                            ALU.mult)))
                    else:
                        p_done.append(mark(V.tensor_tensor(
                            o.rearrange("p (k c) -> p k c", k=n), k_[:, 0:n, :],
                            q[:, t, :].unsqueeze(1).to_broadcast([P, n, width]), ALU.mult)))

                product(0)
                for t in range(T):
                    if t + 1 < T:
                        product(t + 1)
                    need(p_done[t])
                    n = sizes[t]
                    s_done.append(mark(V.tensor_reduce(
                        S[:, t * T * nh:t * T * nh + n * nh],
                        prods[t % 2][:, 0:n * width].rearrange("p (a d) -> p a d", d=d), AX.X, ALU.add)))
                need(s_done[-1])

            def weigh(v_, o_, nh, d, sizes, shared=False):
                width = nh * d
                s_done, p_done = [], []

                def product(t):
                    n = sizes[t]
                    if t >= 2:
                        need(s_done[t - 2])
                    vv = (v_[:, 0:n, :].unsqueeze(2).to_broadcast([P, n, nh, d]) if shared
                          else v_[:, 0:n, :].rearrange("p k (h d) -> p k h d", h=nh))
                    p_done.append(mark(V.tensor_tensor(
                        prods[t % 2][:, 0:n * width].rearrange("p (k h d) -> p k h d", k=n, h=nh), vv,
                        S[:, t * T * nh:t * T * nh + n * nh].rearrange("p (k h) -> p k h", k=n)
                        .unsqueeze(3).to_broadcast([P, n, nh, d]), ALU.mult)))

                product(0)
                for t in range(T):
                    if t + 1 < T:
                        product(t + 1)
                    need(p_done[t])
                    n = sizes[t]
                    s_done.append(mark(V.tensor_reduce(
                        o_[:, t, :], prods[t % 2][:, 0:n * width].rearrange("p (k c) -> p c k", k=n),
                        AX.X, ALU.add)))
                need(s_done[-1])

            def softmax(name, nh):
                s4 = S[:, 0:T * T * nh].rearrange("p (t k h) -> p t k h", t=T, k=T)
                byk = S[:, 0:T * T * nh].rearrange("p (t k h) -> p t h k", t=T, k=T)
                mx = prodA[:, 0:T * nh].rearrange("p (t h) -> p t h", t=T)
                ri = prodA[:, T * nh:2 * T * nh]
                shape = [P, T, T, nh]
                link(V.tensor_reduce(mx, byk, AX.X, ALU.max))
                V.tensor_tensor(s4, s4, mx.unsqueeze(2).to_broadcast(shape),
                                ALU.subtract).then_inc(sem(name + "_max"), 1)
                dve.wait_ge(sem(name + "_exp"), 1)
                link(V.tensor_reduce(mx, byk, AX.X, ALU.add))
                link(V.reciprocal(ri, prodA[:, 0:T * nh]))
                link(V.tensor_tensor(s4, s4, ri.rearrange("p (t h) -> p t h", t=T).unsqueeze(2).to_broadcast(shape),
                                     ALU.mult))

            norm_dve("ln0", hT, xT, CH, 0, EPS_LN, drained=[("gkv_ready", HW)])
            q5 = qkv(512)
            link(V.memset(S, MASKED))
            dve.wait_ge(sem("tab_in"), 64)
            dve.wait_ge(sem("qkv0_used"), T)
            link(V.tensor_tensor(q5[:, :, 256:384], q5[:, :, 256:384], q5[:, :, 384:512], ALU.mult))
            rotate(q5[:, :, 0:128], 8, 16, rope_c, rope_s)
            rotate(q5[:, :, 128:256], 8, 16, rope_c, rope_s)
            after(dve, *norm("ln0", "stat", 4))
            scores(q5[:, :, 0:128], q5[:, :, 128:256], 8, 16, causal_sizes())
            softmax("att0", 8)
            weigh(q5[:, :, 256:384], q5[:, :, 0:128], 8, 16, causal_sizes())
            V.memset(prodA[:, 0:1], 0.0).then_inc(sem("att0_done"), 1)
            for c in range(4):
                dve.wait_ge(sem("att0_used"), min(5, ((c + 1) * CH - 1) // 256 + 1))
                dve.wait_ge(sem("go_used"), 8)
                cols = slice(c * CH, (c + 1) * CH)
                V.tensor_tensor(oT[:, :, cols], oT[:, :, cols], yT[:, :, cols],
                                ALU.mult).then_inc(sem("att0_gated"), 1)

            def add_to(dst, name, banks, n=CH):
                for c in range(4):
                    for m in range(2):
                        cols = slice(c * n, (c + 1) * n)
                        dve.wait_ge(sem(name + "_ready"), 2 * c + m + 1)
                        V.tensor_tensor(dst[:, m, cols], dst[:, m, cols], ps[:, banks + (2 * c + m) % 4, 0:n],
                                        ALU.add).then_inc(sem(name + "_used"), 1)

            add_to(hT, "wo", 0)

            norm_dve("ln1", hT, xT, CH, 4, EPS_LN, drained=[("go_ready", 8), ("qkv0_ready", T)])
            for c in range(4):
                cols = slice(c * CH, (c + 1) * CH)
                after(dve, *norm("ln1", "out", c + 1))
                after(dve, *norm("ln1", "sq", c + 1))
                link(V.tensor_tensor(hT[:, :, cols], hT[:, :, cols], xT[:, :, cols], ALU.add))
            norm_dve("rms1", xT, yT, CH, 0, EPS_RMS, mean=False, gain="g1")
            q2 = qkv(256)
            dve.wait_ge(sem("qkv1_used"), T)
            after(dve, *norm("rms1", "stat", 4))
            whole = [T] * T
            scores(q2[:, :, 0:128], q2[:, :, 128:192], 2, 64, whole, shared=True)
            softmax("att1", 2)
            weigh(q2[:, :, 192:256], q2[:, :, 0:128], 2, 64, whole, shared=True)
            V.memset(prodA[:, 0:1], 0.0).then_inc(sem("att1_done"), 1)
            for c in range(4):
                for m in range(2):
                    cols = slice(c * CH, (c + 1) * CH)
                    pb = ps[:, 4 + (2 * c + m) % 4, 0:CH]
                    dve.wait_ge(sem("mo_ready"), 2 * c + m + 1)
                    V.tensor_tensor(hT[:, m, cols], hT[:, m, cols], pb, ALU.add)
                    V.tensor_tensor(xT[:, m, cols], xT[:, m, cols], pb, ALU.add).then_inc(sem("mo_used"), 1)
            norm_dve("rms2", xT, yT, CH, 0, EPS_RMS, mean=False, gain="g2", drained=[("qkv1_ready", T)])

            rw = small[:, 0:72]
            rw3 = rw.rearrange("p (t e) -> p t e", t=9)
            w3 = small[:, 72:144].rearrange("p (t e) -> p t e", t=9)
            r9_ = small[:, 144:153]
            cmpA = prodA[:, 0:576].rearrange("p (t e j) -> p t e j", t=9, e=8)
            cmpB = prodA[:, 576:1152].rearrange("p (t e j) -> p t e j", t=9, e=8)
            rank = prodA[:, 1152:1224].rearrange("p (t e) -> p t e", t=9)
            s98 = [P, 9, 8]
            s988 = [P, 9, 8, 8]
            link(V.memset(small[:, 0:160], 0.0))
            dve.wait_ge(sem("w_ffn_in"), 80)
            dve.wait_ge(sem("logits_ready"), 1)
            V.tensor_copy(small[64:128, 0:64], ps[64:128, 4, 0:64])
            link(V.tensor_copy(small[0:64, 0:72], ps[0:64, 4, 0:72]))
            link(V.tensor_tensor(rw3, rw3, ebias[:, :].unsqueeze(1).to_broadcast(s98), ALU.add))
            link(V.tensor_reduce(r9_, rw3, AX.X, ALU.max))
            V.tensor_tensor(rw3, rw3, r9_.unsqueeze(2).to_broadcast(s98), ALU.subtract).then_inc(sem("lg_max"), 1)
            dve.wait_ge(sem("lg_exp"), 1)
            link(V.tensor_reduce(r9_, rw3, AX.X, ALU.add))
            link(V.reciprocal(small[:, 153:162], r9_))
            link(V.tensor_tensor(rw3, rw3, small[:, 153:162].unsqueeze(2).to_broadcast(s98), ALU.mult))
            V.tensor_tensor(cmpA, rw3.unsqueeze(2).to_broadcast(s988), rw3.unsqueeze(3).to_broadcast(s988), ALU.is_gt)
            link(V.tensor_tensor(cmpB, rw3.unsqueeze(2).to_broadcast(s988), rw3.unsqueeze(3).to_broadcast(s988),
                                 ALU.is_equal))
            low = lower[:, :].rearrange("p (e j) -> p e j", e=8).unsqueeze(1).to_broadcast(s988)
            link(V.tensor_tensor(cmpB, cmpB, low, ALU.mult))
            link(V.tensor_tensor(cmpA, cmpA, cmpB, ALU.add))
            link(V.tensor_reduce(rank, cmpA, AX.X, ALU.add))
            link(V.tensor_scalar(rank, rank, 2.0, None, ALU.is_lt))
            link(V.tensor_reduce(r9_, rw3, AX.X, ALU.max))
            V.tensor_tensor(w3, rw3, r9_.unsqueeze(2).to_broadcast(s98), ALU.subtract).then_inc(sem("rw_max"), 1)
            dve.wait_ge(sem("rw_exp"), 1)
            link(V.tensor_tensor(w3, w3, rank, ALU.mult))
            link(V.tensor_reduce(r9_, w3, AX.X, ALU.add))
            link(V.reciprocal(small[:, 153:162], r9_))
            V.tensor_tensor(rw3, w3, small[:, 153:162].unsqueeze(2).to_broadcast(s98),
                            ALU.mult).then_inc(sem("combine_done"), 1)

            with dve.Fori(0, 4) as c:
                for n in range(18):
                    e = n // 2
                    up = ps[:, 3 + 2 * (n % 2), 0:CH]
                    dve.wait_ge(sem("esil_ready"), c * 18 + (n + 1))
                    dve.wait_ge(sem("edown"), c * 18 + max(n - 2, 0))
                    dve.wait_ge(sem("eh_ready"), c * 18 + max(n - 1, 0))
                    if e < NEXP:
                        V.tensor_tensor(emul[n % 2], esil[n % 2], up, ALU.mult).then_inc(sem("emul_done"), 1)
                        dve.wait_ge(sem("emul_done"), c * 16 + (n + 1))
                        V.tensor_tensor(eh[n % 3], emul[n % 2], ps[:, 6 + e % 2, 0:CH],
                                        ALU.mult).then_inc(sem("eh_ready"), 1)
                    else:
                        V.tensor_tensor(eh[n % 3], esil[n % 2], up, ALU.mult).then_inc(sem("eh_ready"), 1)
                dve.wait_ge(sem("edown"), c * 18 + 18)
                for m in range(2):
                    dst = hbuf[:, bass.ds(c * CH + m * NT, CH)]
                    V.tensor_tensor(dst, dst, ps[:, m, 0:CH], ALU.add).then_inc(sem("moe_used"), 1)

            dve.wait_ge(sem("moe_used"), 8)
            norm_dve("ln2", hT, xT, CH, 2, EPS_LN)
            q3 = qkv(384)
            dve.wait_ge(sem("qkv2_used"), T)
            after(dve, *norm("ln2", "stat", 4))
            rotate(q3[:, :, 0:128], 4, 32, xpos[:, 0], xpos[:, 1])
            rotate(q3[:, :, 128:256], 4, 32, xpos[:, 2], xpos[:, 3])
            scores(q3[:, :, 0:128], q3[:, :, 128:256], 4, 32, causal_sizes())
            for t in range(T):
                n = (t + 1) * 4
                last = V.tensor_tensor(S[:, t * T * 4:t * T * 4 + n], S[:, t * T * 4:t * T * 4 + n],
                                       decay[:, t * T * 4:t * T * 4 + n], ALU.mult)
            link(last)
            weigh(q3[:, :, 256:384], q3[:, :, 0:128], 4, 32, causal_sizes())
            y4 = q3[:, :, 0:128].rearrange("p t (h d) -> p t h d", h=4)
            shape = [P, T, 4, 32]
            gm = S[:, 100:168].rearrange("p (t h) -> p t h", t=T)
            gv = S[:, 0:68].rearrange("p (t h) -> p t h", t=T)
            p4 = prodA.rearrange("p (t h d) -> p t h d", t=T, h=4)
            link(V.tensor_reduce(gm, y4, AX.X, ALU.add))
            link(V.tensor_scalar(gm, gm, 1.0 / 32, None, ALU.mult))
            link(V.tensor_tensor(y4, y4, gm.unsqueeze(3).to_broadcast(shape), ALU.subtract))
            link(V.tensor_tensor(p4, y4, y4, ALU.mult))
            link(V.tensor_reduce(gv, p4, AX.X, ALU.add))
            V.tensor_scalar(S[:, 0:68], S[:, 0:68], 1.0 / 32, EPS_LN, ALU.mult, ALU.add).then_inc(sem("gn_var"), 1)
            dve.wait_ge(sem("gn_rstd"), 1)
            V.tensor_tensor(y4, y4, gv.unsqueeze(3).to_broadcast(shape), ALU.mult).then_inc(sem("att2_done"), 1)
            dve.wait_ge(sem("w_f_in"), 32)
            V.tensor_reduce(gam[:, 0:1], arena[:, 0:2048], AX.X, ALU.add, apply_absolute_value=True)
            V.tensor_reduce(gam[:, 1:2], arena[:, 2048:4096], AX.X, ALU.add,
                            apply_absolute_value=True).then_inc(sem("gam_sum"), 1)
            for c in range(4):
                cols = slice(c * CH, (c + 1) * CH)
                dve.wait_ge(sem("att2_used"), min(5, ((c + 1) * CH - 1) // 256 + 1))
                dve.wait_ge(sem("g_used"), 8)
                for m in range(2):
                    last = V.tensor_scalar(oT[:, m, cols], oT[:, m, cols], v("gn_weight", m), v("gn_bias", m),
                                           ALU.mult, ALU.add)
                link(last)
                V.tensor_tensor(oT[:, :, cols], oT[:, :, cols], yT[:, :, cols],
                                ALU.mult).then_inc(sem("att2_gated"), 1)
            add_to(hT, "l1o", 0)
            dve.wait_ge(sem("gam_ready"), 1)
            link(V.tensor_scalar(gam[:, 2:4], ps[:, 4, 0:2], 1.0 / 1024, EPS_LN, ALU.mult, ALU.add))
            link(V.tensor_scalar(gam[:, 4:6], gam[:, 2:4], 0.5, None, ALU.mult))
            link(V.tensor_scalar(gam[:, 6:8], gam[:, 2:4], -0.5, None, ALU.mult))
            for w in range(2):
                link(V.tensor_scalar(tern[:, 2048 * w:2048 * (w + 1)], arena[:, 2048 * w:2048 * (w + 1)],
                                     gam[:, 6 + w:7 + w], None, ALU.is_lt))
                last = V.scalar_tensor_tensor(out=tern[:, 2048 * w:2048 * (w + 1)],
                                              in0=arena[:, 2048 * w:2048 * (w + 1)], scalar=gam[:, 4 + w:5 + w],
                                              in1=tern[:, 2048 * w:2048 * (w + 1)], op0=ALU.is_gt,
                                              op1=ALU.subtract)
            last.then_inc(sem("tern_done"), 1)

            norm_dve("ln3", hT, xT, CH, 4, EPS_LN)
            for c in range(4):
                for m in range(2):
                    cols = slice(c * CH, (c + 1) * CH)
                    dve.wait_ge(sem("fc2_ready"), 2 * c + m + 1)
                    V.scalar_tensor_tensor(out=hT[:, m, cols], in0=ps[:, 4 + (2 * c + m) % 4, 0:CH],
                                           scalar=v("b2", m), in1=hT[:, m, cols],
                                           op0=ALU.add, op1=ALU.add).then_inc(sem("final"), 1)


def fold(w):
    k = w.shape[0] // P
    return w.reshape(k, P, -1).transpose(1, 0, 2).reshape(P, -1)


def pair_order(w, heads, d):
    return w.reshape(w.shape[0], heads, d // 2, 2).transpose(0, 1, 3, 2).reshape(w.shape[0], heads * d)


def by_half(*ws):
    return np.concatenate([w.reshape(w.shape[0], 2, -1) for w in ws], axis=2)


def shape_tables():
    f = np.float32
    pos = np.arange(T, dtype=f)
    inv = (1.0 / np.power(f(2500), np.arange(0, 16, 2, dtype=f) / f(16))).astype(f)
    emb = np.outer(pos, inv).astype(f)
    emb = np.concatenate([emb, emb], -1)
    cs, sn = np.cos(emb)[:, ::2].astype(f), np.sin(emb)[:, ::2].astype(f)
    rope = np.stack([np.concatenate([cs, cs], -1), np.concatenate([-sn, sn], -1)])
    base = ((np.arange(0, 32, 2, dtype=f) + f(0.4 * 32)) / f(1.4 * 32)).astype(f)
    scale = np.power(base[None, :], pos[:, None] / f(512.0)).astype(f)
    ang = (pos[:, None] * (1.0 / np.power(f(10000.0), np.arange(16, dtype=f) / f(16)))[None, :]).astype(f)
    tabs = []
    for s in (scale, (1.0 / scale).astype(f)):
        c_, s_ = np.cos(ang) * s, np.sin(ang) * s
        tabs += [np.concatenate([c_, c_], -1), np.concatenate([-s_, s_], -1)]
    gammas = 1.0 - np.exp(np.linspace(np.log(1 / 32.0), np.log(1 / 512.0), 8)).astype(f)
    expo = (np.arange(T)[:, None] - np.arange(T)[None, :]).astype(f)
    d = np.where(expo[None] >= 0, np.exp(expo[None] * np.log(gammas)[:, None, None]), 0.0)
    decay = d.reshape(2, 4, T, T).transpose(0, 2, 3, 1).reshape(2, 1, T * T * 4)
    sel = np.repeat(np.eye(NEXP), P, axis=1)
    lower = (np.arange(8)[None, :] < np.arange(8)[:, None]).astype(f).reshape(1, 64)
    return {k: np.ascontiguousarray(x, dtype=f) for k, x in dict(
        rope=rope.reshape(1, -1), xpos=np.stack(tabs).reshape(1, -1), decay=decay, sel=sel, lower=lower,
        ident=np.eye(P)).items()}


def lay_out(i):
    g = {k: np.asarray(x) for k, x in i.items()}
    t = lambda n: g["L0_tok_" + n]
    at = lambda n: g["L0_attn_" + n].T
    ff = lambda n: g["L0_ffn_" + n]
    l1 = lambda n: g["L1_attn_" + n]
    x = g["x"].reshape(B, 3, 4, 3, 14, 2, 2, 3, 14).transpose(2, 5, 1, 4, 8, 3, 7, 6, 0)
    x = x.reshape(ITERS, PATCH_K, XC)
    wc = t("conv_w").reshape(C, PATCH_K).T
    a = {
        "x_main": x[:, 0:512].reshape(ITERS, 4, P, XC).transpose(0, 2, 1, 3),
        "x_rest": x[:, 512:],
        "w_conv": wc[0:512].reshape(4, P, C).transpose(1, 0, 2),
        "w_convr": wc[512:],
        "la_wkv": t("la_wkv").reshape(2, P, 512).transpose(1, 0, 2),
        "la_wq": t("la_wq").reshape(2, P, C).transpose(1, 0, 2),
        "la_proj_w": fold(t("la_proj_w")), "mod_w": fold(t("mod_w")),
        "ga_wkv": fold(by_half(t("ga_wkv")[:, 0:C], t("ga_wkv")[:, C:]).reshape(C, -1)),
        "ga_wq": fold(t("ga_wq")), "ga_proj_w": fold(t("ga_proj_w")),
        "attn_qkvg": fold(by_half(pair_order(at("W_q"), 16, 16), pair_order(at("W_k"), 16, 16),
                                  at("W_v"), at("W_gv")).reshape(C, -1)),
        "attn_go": fold(at("W_go")), "attn_o": fold(at("W_o")),
        "ffn_o": fold(ff("Wo").T), "ffn_r": fold(ff("Wr").T), "ebias": ff("expert_bias").reshape(1, NEXP),
        "l1_g": fold(l1("W_G")), "l1_o": fold(l1("W_O")),
        "w1": fold(g["L1_ffn_W1"].T).reshape(P, 2, 1024), "w2": fold(g["L1_ffn_W2"].T).reshape(P, 8, C),
    }
    kc, vc = ff("Wkc").T, ff("Wvc").T
    q = ff("Wq").T.reshape(C, 2, P)
    a["ffn_qkv"] = fold(np.concatenate([q, np.stack([kc, kc], 1), np.stack([vc, vc], 1)], 2).reshape(C, -1))
    heads = lambda n: l1(n).transpose(1, 0, 2).reshape(C, C)
    a["l1_qkv"] = fold(by_half(pair_order(heads("W_Q"), 8, 32), pair_order(heads("W_K"), 8, 32),
                               heads("W_V")).reshape(C, -1))
    ex = [np.stack([fold(w.T) for w in (ff("eW1")[e], ff("eW3")[e], ff("eW2")[e])], 1) for e in range(NEXP)]
    ex.append(np.stack([fold(w.T) for w in (ff("sW1"), ff("sW3"), ff("sW2"))], 1))
    a["experts"] = np.stack(ex, 1).reshape(P, 9, 3, 2, C)
    src = {"class_emb": t("class_emb"), "g1": ff("g1"), "g2": ff("g2"), "gn_weight": l1("gn_weight"),
           "gn_bias": l1("gn_bias"), "b1": g["L1_ffn_b1"], "b2": g["L1_ffn_b2"]}
    a["vec"] = np.concatenate([(src[n] if n in src else t(n)).reshape(k, P).T for n, k in VEC], axis=1)
    return {k: np.ascontiguousarray(x) for k, x in a.items()}


def kernel(**inputs):
    import concourse.bacc as _bacc
    from concourse.bass_utils import run_bass_kernel_spmd as _run

    nc = _bacc.Bacc("TRN2", target_bir_lowering=False, num_devices=1)
    arrays = {**lay_out(inputs), **shape_tables()}
    aps = {n: nc.dram_tensor(n + "_dram", x.shape, F32, kind="ExternalInput").ap() for n, x in arrays.items()}
    out = nc.dram_tensor("out_dram", (P, 2, NT), F32, kind="ExternalOutput").ap()
    build(nc, aps, out)
    r = _run(nc, [{n + "_dram": x for n, x in arrays.items()}], core_ids=[0])
    got = r.results[0]["out_dram"]
    return np.ascontiguousarray(got.reshape(P, 2, T, B).transpose(3, 2, 1, 0).reshape(B, T, C))
```

```python
from contextlib import ExitStack

import numpy as np
import concourse.bass as bass
from concourse import mybir

F32 = mybir.dt.float32
ALU = mybir.AluOpType
ACT = mybir.ActivationFunctionType
AX = mybir.AxisListType

P = 128
B = 64
HB = B // 2
T = 17
HW = 16
C = 256
PATCH_K = 588
K_REST = PATCH_K - 4 * P
NJ = 9
ITERS = 8
XC = NJ * P
CONV_N = 384
NCG = XC // CONV_N
XRING = 4
NT = B * T
NH = HB * T
NWH = HB * HW
CH = NH // 2
LC = NWH // 2
QC = C // 4
FIXED = T * 256 + T * T * 4 + NJ * C + 2 * T * 16
LATER = 24900
NEXP = 8
KVN = C + 1
KVS = KVN + 1
EPS_LN = 1e-5
EPS_RMS = 1e-6
MASKED = -1e30

VEC = [("la_ln_q_g", 2), ("la_ln_q_b", 2), ("la_ln_kv_g", 2), ("la_ln_kv_b", 2), ("la_proj_b", 2),
       ("ga_ln_q_g", 2), ("ga_ln_q_b", 2), ("ga_ln_kv_g", 2), ("ga_ln_kv_b", 2), ("ga_proj_b", 2),
       ("mod_b", 2), ("class_emb", 2), ("g1", 2), ("g2", 2), ("gn_weight", 2), ("gn_bias", 2),
       ("b1", 8), ("b2", 2)]
VCOL = {}
_n = 0
for _name, _k in VEC:
    VCOL[_name] = _n
    _n += _k
NVEC = _n


CUT_SCORES, CUT_WEIGH = 8, 12
CAUSAL = [t + 1 for t in range(T)]


def build(nc, a, out):
    ctx = ExitStack()
    with ctx:
        def sb(name, shape):
            return ctx.enter_context(nc.sbuf_tensor(name, shape, F32))

        sems = {}

        def sem(name):
            if name not in sems:
                sems[name] = ctx.enter_context(nc.semaphore(name))
            return sems[name]

        ps = ctx.enter_context(nc.psum_tensor("ps", [P, 8, 512], F32))

        hT, xT, yT, oT = (sb(n, [P, 2, NT]) for n in ("hT", "xT", "yT", "oT"))
        sqb = sb("sqb", [P, 2, 2, CH])
        lnv = sb("lnv", [P, 2, CH])
        vec = sb("vec", [P, NVEC])
        ident = sb("ident", [P, P])
        avg = sb("avg", [P, P])
        small = sb("small", [P, 512])
        ebias = sb("ebias", [P, NEXP])
        lower = sb("lower", [P, NEXP * NEXP])
        wtok = sb("wtok", [P, 6 * 512])
        wattn = sb("wattn", [P, 6 * 512])

        def v(name, i=0):
            return vec[:, VCOL[name] + i:VCOL[name] + i + 1]

        def w2(ap):
            return ap.rearrange("p (k n) -> p k n", k=2)

        def wq4(ap):
            return ap.rearrange("p (k q n) -> p k q n", k=2, q=4)

        w_proj, w_mod = w2(wtok[:, 0:512]), w2(wtok[:, 512:1024])
        w_gkv, w_gq, w_gproj = wq4(wtok[:, 1024:2048]), wq4(wtok[:, 2048:2560]), w2(wtok[:, 2560:3072])
        w_l1qkv, w_l1g, w_l1o = wq4(wtok[:, 0:1536]), w2(wtok[:, 1536:2048]), w2(wtok[:, 2048:2560])
        w_qkvg, w_go, w_o = wq4(wattn[:, 0:2048]), w2(wattn[:, 2048:2560]), w2(wattn[:, 2560:3072])

        ARENA = FIXED + LATER
        arena = sb("arena", [P, ARENA])
        at = [0]

        def take(n):
            at[0] += n
            assert at[0] <= ARENA, at[0]
            return arena[:, at[0] - n:at[0]]

        qkv_of = [take(T * 256), None]
        S = take(T * T * 4)
        prodW = take(NJ * C)
        prods = [prodW[:, 0:T * QC], prodW[:, T * QC:2 * T * QC]]
        rope = take(2 * T * 16).rearrange("p (f t d) -> p f t d", f=2, t=T)
        assert at[0] == FIXED, at[0]
        x_main = [take(4 * CONV_N).rearrange("p (k n) -> p k n", k=4) for _ in range(XRING)]
        x_rest = [take(CONV_N) for _ in range(XRING)]
        w_conv = take(4 * C).rearrange("p (k n) -> p k n", k=4)
        w_convr = take(C)
        patch_emb = take(2 * XC).rearrange("p (m n) -> p m n", m=2)
        patch_sq = take(2 * XC).rearrange("p (m n) -> p m n", m=2)
        kv_flat = take(NJ * 2 * KVS)
        kv_raw = kv_flat.rearrange("p (j s n) -> p j s n", j=NJ, s=2)
        w_kv = kv_flat[:, 0:1024].rearrange("p (k n) -> p k n", k=2)
        w_lq = kv_flat[:, 1024:1536].rearrange("p (k n) -> p k n", k=2)
        bcol = kv_flat[:, 1536:1792].rearrange("p (k n) -> p k n", k=2)
        sq_sum = take(XC)
        red = take(C).rearrange("p (m n) -> p m n", m=2)
        red_sq = take(C).rearrange("p (m n) -> p m n", m=2)
        rsq_sum = take(P)
        w_kvc = take(2 * 2 * KVS).rearrange("p (k s n) -> p k s n", k=2, s=2)
        w_lqc = take(2 * KVS).rearrange("p (k n) -> p k n", k=2)
        q_win = take(C)
        qk_tmp = take(C)
        bias_row = take(3 * C)
        sc = take(NJ * 8)
        sm8 = take(8)
        qb8 = take(8)
        st10 = take(10)
        mean10 = take(10)
        aggW = take(4 * C).rearrange("p (i c) -> p i c", i=4)
        at[0] = FIXED
        exp_flat = take(9 * 3 * 512)
        w_exp = exp_flat.rearrange("p (e w k n) -> p e w k n", e=9, w=3, k=2)
        qkv_of[1] = take(T * 256)
        eh = [take(CH) for _ in range(3)]
        esil = [take(CH) for _ in range(2)]
        emul = [take(CH) for _ in range(2)]
        w_mqa_flat, w_mo_flat, w_r_flat = take(2 * (C + P + QC)), take(512), take(16)
        w_mqa, w_mo = w2(w_mqa_flat), w2(w_mo_flat)
        w_mq, w_mk, w_mv = w_mqa[:, :, 0:C], w_mqa[:, :, C:C + P], w_mqa[:, :, C + P:C + P + QC]
        w_r = w_r_flat.rearrange("p (k n) -> p k n", k=2)
        xpos_flat = take(4 * T * 32)
        xpos = xpos_flat.rearrange("p (f t d) -> p f t d", f=4, t=T)
        decay = take(T * T * 2)
        sel = sb("sel", [NEXP, NEXP * P])
        cmbT = sb("cmbT", [NEXP, NH])
        w_f1 = exp_flat[:, 0:2048].rearrange("p (k n) -> p k n", k=2)
        w_f2 = exp_flat[:, 2048:4096].rearrange("p (k n) -> p k n", k=8)
        tern = exp_flat[:, 4096:8192]
        w_t1 = tern[:, 0:2048].rearrange("p (k n) -> p k n", k=2)
        w_t2 = tern[:, 2048:4096].rearrange("p (k n) -> p k n", k=8)
        gam = small[:, 400:410]
        hid = qkv_of[0][:, 0:16 * CH].rearrange("p (u k n) -> p u k n", u=2, k=8)

        class Mqa:
            def __init__(self, s):
                at_ = [0]

                def part(n):
                    at_[0] += n
                    return qkv_of[s][:, at_[0] - n:at_[0]]

                self.q = part(2 * NH).rearrange("p (m n) -> p m n", m=2)
                self.k = part(NH)
                self.v_flat = part(8 * QC)
                self.v = self.v_flat.rearrange("p (g d) -> p g d", g=8)
                self.p = part(HB * 32)
                self.p3 = self.p.rearrange("p (i k) -> p i k", k=32)
                self.pT = part(8 * P).rearrange("p (g n) -> p g n", g=8)
                self.top, self.inv = part(HB), part(HB)

        mqa_of = [Mqa(0), Mqa(1)]

        def qkv(s, n):
            return qkv_of[s][:, 0:T * n].rearrange("p (t n) -> p t n", t=T)

        X4 = [2, 3, 4, 5]
        Y4 = [6, 7, 0, 1]

        def cols(s, c, n=CH):
            return slice(s * NH + c * n, s * NH + (c + 1) * n)

        def after(eng, s, value):
            if value > 0:
                eng.wait_ge(sem(s), value)

        NORMS = [("lnga", 0), ("ln0", 0), ("lnga", 1), ("ln1", 0), ("rms1", 0), ("ln0", 1), ("rms2", 0),
                 ("ln2", 0), ("ln1", 1), ("rms1", 1), ("rms2", 1), ("ln2", 1), ("ln3", 0), ("ln3", 1)]
        NORM_BANKS = {"lnga": X4, "ln0": X4, "ln1": Y4, "rms1": Y4, "rms2": Y4, "ln2": X4, "ln3": X4}

        def norm(name, s, step, n):
            none = {"mu2": ("rms1", "rms2"), "sq": ("rms1",), "stat": ("rms1",)}.get(step, ())
            before = [x for x in NORMS[:NORMS.index((name, s))] if x[0] not in none]
            return "norm_" + step, 2 * len(before) + n

        def spot(name, s, c):
            return 2 * NORMS.index((name, s)) + c

        block = ctx.enter_context(nc.Block())

        @block.sync
        def _(sp):
            def load(dst, src, s):
                sp.dma_start(dst, src).then_inc(sem(s), 16)

            def load_x(g):
                load(x_main[g % XRING], a["x_main"][g], f"x_in{g % XRING}")
                load(x_rest[g % XRING][0:K_REST, :], a["x_rest"][g], f"x_in{g % XRING}")

            load(w_conv, a["w_conv"], "w_conv_in")
            load(w_convr[0:K_REST, :], a["w_convr"], "w_conv_in")
            load_x(0)
            load(vec[:, :], a["vec"], "w_first_in")
            load(ident[:, :], a["ident"], "w_first_in")
            load(w_kv, a["la_wkv"], "w_first_in")
            load(w_lq, a["la_wq"], "w_first_in")
            for g in range(1, XRING):
                load_x(g)
            load(wtok[:, 0:512], a["la_proj_w"], "w_tok_in")
            load(wtok[:, 512:1024], a["mod_w"], "w_tok_in")
            load(wtok[:, 1024:2048], a["ga_wkv"], "w_tok_in")
            load(wtok[:, 2048:2560], a["ga_wq"], "w_tok_in")
            load(wtok[:, 2560:3072], a["ga_proj_w"], "w_tok_in")
            load(wattn[:, 0:2048], a["attn_qkvg"], "w_attn_in")
            load(wattn[:, 2048:2560], a["attn_go"], "w_attn_in")
            load(wattn[:, 2560:3072], a["attn_o"], "w_attn_in")
            load(ebias[:, :], a["ebias"].partition_broadcast(P), "tab_in")
            load(lower[:, :], a["lower"].partition_broadcast(P), "tab_in")
            load(sel[:, :], a["sel"], "tab_in")
            load(rope, a["rope"].partition_broadcast(P), "tab_in")
            for g in range(XRING, ITERS * NCG):
                sp.wait_ge(sem("conv_evac"), 2 * (g - XRING) + 2)
                load_x(g)
            sp.wait_ge(sem("win_done"), ITERS)
            load(w_mqa_flat, a["ffn_qkv"], "w_ffn_in")
            load(w_mo_flat, a["ffn_o"], "w_ffn_in")
            load(w_r_flat, a["ffn_r"], "w_ffn_in")
            for e in range(9):
                load(w_exp[:, e], a["experts"][:, e], "w_exp_in")
            sp.wait_ge(sem("aggT_ready"), 4)
            load(xpos_flat, a["xpos"].partition_broadcast(P), "w_l1_in")
            for q in range(4):
                load(decay[32 * q:32 * q + 32, :], a["decay"][q].partition_broadcast(32), "w_l1_in")
            sp.wait_ge(sem("gproj_ready"), 4)
            load(wtok[:, 0:1536], a["l1_qkv"], "w_l1_in")
            load(wtok[:, 1536:2048], a["l1_g"], "w_l1_in")
            load(wtok[:, 2048:2560], a["l1_o"], "w_l1_in")
            sp.wait_ge(sem("edown"), 54 + 6)
            load(w_f1, a["w1"], "w_f_in")
            load(w_f2, a["w2"], "w_f_in")
            for s in range(2):
                for c in range(2):
                    sp.wait_ge(sem("final"), 4 * s + 2 * c + 2)
                    load(out[:, :, cols(s, c)], hT[:, :, cols(s, c)], "out_done")
            sp.wait_ge(sem("out_done"), 64)

        @block.tensor
        def _(pe):
            mm = nc.tensor.matmul

            def waits(pairs):
                for s, value in pairs:
                    after(pe, s, value)

            pe.wait_ge(sem("w_scaled"), 1)
            for k in range(2):
                mm(ps[:, 2, :].rearrange("p (s n) -> p s n", s=2), avg[:, :], w_kvc[:, k, :, 0:C],
                   start=(k == 0), stop=(k == 1))
            for k in range(2):
                last = mm(ps[:, 3, 0:C], avg[:, :], w_lqc[:, k, 0:C], start=(k == 0), stop=(k == 1))
            last.then_inc(sem("w_means"), 1)
            pe.wait_ge(sem("kv_bcol"), 1)
            for k in range(2):
                last = mm(ps[:, 4, :], bcol[:, k, :], w_kv[:, k, :], start=(k == 0), stop=(k == 1))
            last.then_inc(sem("kv_brow"), 1)
            pe.wait_ge(sem("q_bcol"), 1)
            for k in range(2):
                last = mm(ps[:, 5, 0:C], bcol[:, k, :], w_lq[:, k, :], start=(k == 0), stop=(k == 1))
            last.then_inc(sem("q_brow"), 1)
            pe.wait_ge(sem("w_kv_ready"), 1)
            pe.wait_ge(sem("w_conv_in"), 32)

            def conv(i):
                for g in range(2 * NCG):
                    c, m = g // 2, g % 2
                    r = (NCG * i + c) % XRING
                    if m == 0:
                        pe.wait_ge(sem(f"x_in{r}"), 32 * ((NCG * i + c) // XRING + 1))
                    after(pe, "conv_evac", 6 * i + g - 1)
                    for kk in range(4):
                        mm(ps[:, g % 2, 0:CONV_N], w_conv[:, kk, m * P:(m + 1) * P],
                           x_main[r][:, kk, :], start=(kk == 0), stop=False)
                    mm(ps[:, g % 2, 0:CONV_N], w_convr[0:K_REST, m * P:(m + 1) * P],
                       x_rest[r][0:K_REST, :], start=False, stop=True).then_inc(sem("conv_ready"), 1)

            def window_kv(i, drained=()):
                pe.wait_ge(sem("conv_evac"), 6 * i + 6)
                waits(drained)
                for j in range(NJ):
                    b = 2 + 2 * (j % 2)
                    after(pe, "kv_evac", 9 * i + j - 1)
                    for s in range(2):
                        for kk in range(2):
                            last = mm(ps[:, b + s, 0:KVN], patch_emb[:, kk, j * P:(j + 1) * P],
                                      w_kvc[:, kk, s, 0:KVN], start=(kk == 0), stop=(kk == 1))
                    last.then_inc(sem("kv_ready"), 1)
                pe.wait_ge(sem("sums_ready"), i + 1)
                after(pe, "win_done", i - 1)
                st = ps[:, 6 + i % 2, :]
                for j in range(NJ):
                    mm(st[:, 300 + j:301 + j], sq_sum[:, j * P:(j + 1) * P], avg[:, 0:1], start=True, stop=True)
                mm(st[:, 309:310], rsq_sum, avg[:, 0:1], start=True, stop=True)
                for kk in range(2):
                    last = mm(st[:, 0:KVN], red[:, kk, :], w_lqc[:, kk, 0:KVN], start=(kk == 0), stop=(kk == 1))
                last.then_inc(sem("stat_ready"), 1)

            def agg_transposes(s):
                pe.wait_ge(sem("kv_evac"), 9 * 4 * (s + 1))
                for g in range(2):
                    pe.wait_ge(sem("win_done"), 4 * s + 2 * g + 2)
                    for i in range(2):
                        for m in range(2):
                            last = nc.tensor.transpose(ps[:, X4[g], (2 * i + m) * P:(2 * i + m + 1) * P],
                                                       aggW[:, 2 * g + i, m * P:(m + 1) * P], ident[:, :])
                    last.then_inc(sem("aggT_ready"), 1)

            def linear(name, s, w, src, n, banks, src_ready, drained=(), used=None):
                waits(drained)
                for c in range(2):
                    waits(src_ready(c))
                    for m in range(2):
                        for k in range(2):
                            last = mm(ps[:, banks[2 * c + m], 0:n], w[:, k, m * P:(m + 1) * P],
                                      src[:, k, cols(s, c, n)], start=(k == 0), stop=(k == 1))
                        last.then_inc(sem(name + "_ready"), 1)

            def norm_stats(name, s, src, n, src_ready, drained=()):
                banks = NORM_BANKS[name]
                waits(drained)
                for c in range(2):
                    waits(src_ready(c))
                    if not name.startswith("rms"):
                        for k in range(2):
                            mm(ps[:, banks[2 * c], 0:n], avg[:, :], src[:, k, cols(s, c, n)],
                               start=(k == 0), stop=(k == 1))
                    after(pe, *norm(name, s, "sq", c + 1))
                    for k in range(2):
                        last = mm(ps[:, banks[2 * c + 1], 0:n], avg[:, :], sqb[:, spot(name, s, c) % 2, k, 0:n],
                                  start=(k == 0), stop=(k == 1))
                    last.then_inc(sem("norm_stat"), 1)

            def to_images(name, s, w, src, n, nt, banks, src_ready, drained=()):
                groups = (nt + 1) // 2
                waits(drained)
                for g in range(groups):
                    if g >= 4:
                        after(pe, name + "_used", groups * s + g - 3)
                    for t in range(2 * g, min(2 * g + 2, nt)):
                        waits(src_ready(t))
                        for k in range(2):
                            for q in range(4):
                                last = mm(ps[32 * q:32 * q + 32, banks[g % 4], (t % 2) * n:(t % 2 + 1) * n],
                                          src[:, k, s * NH + t * HB:s * NH + (t + 1) * HB], w[:, k, q, :],
                                          start=(k == 0), stop=(k == 1), skip_group_check=True)
                    last.then_inc(sem(name + "_ready"), 1)

            spread = ident[:, :].rearrange("p (m r b) -> p r m b", m=2, r=2)

            def to_channels(name, s, src, nt, banks, ready, drained=()):
                waits(drained)
                pe.wait_ge(sem(ready), s + 1)
                for g in range((nt + 7) // 8):
                    for t in range(8 * g, min(8 * g + 8, nt)):
                        for r in range(2):
                            last = mm(ps[64 * r:64 * r + 64, banks[g], (t % 8) * QC:(t % 8 + 1) * QC]
                                      .rearrange("p (m b) -> p m b", m=2),
                                      src[:, t, 0:QC], spread[:, r], start=True, stop=True, skip_group_check=True)
                    last.then_inc(sem(name + "_ready"), 1)

            def token_ready(name, s, n=CH):
                return lambda t: [norm(name, s, "out", min(2, ((t + 1) * HB - 1) // n + 1))]

            def local_output(s):
                agg_transposes(s)
                linear("proj", s, w_proj, xT, LC, X4, lambda c: [("aggT_used", 2 * s + c + 1)],
                       [("w_tok_in", 80), ("aggT_used", 2 * s + 2)])

            def patch_output(s):
                linear("mod", s, w_mod, yT, LC, X4, lambda c: [("local_out", 4 * s + 2 * c + 2)],
                       [("local_out", 4 * s + 4)])
                norm_stats("lnga", s, yT, LC, lambda c: [], [("h_tok", 4 * s + 4)])

            def global_kv(s):
                if s == 0:
                    after(pe, *norm("lnga", 0, "out", 2))
                    pe.wait_ge(sem("cls_cols"), 1)
                    for k in range(2):
                        last = mm(ps[:, 2, 0:2], avg[:, :], small[:, 2 * k:2 * k + 2], start=(k == 0), stop=(k == 1))
                    last.then_inc(sem("cls_stat"), 1)
                    pe.wait_ge(sem("cls_bcast"), 1)
                    for q in range(4):
                        for k in range(2):
                            last = mm(ps[32 * q:32 * q + 32, 3, 0:QC], small[:, 16 + 64 * k:16 + 64 * k + 32],
                                      w_gq[:, k, q, :], start=(k == 0), stop=(k == 1))
                    last.then_inc(sem("gq_ready"), 1)
                    pe.wait_ge(sem("gq_used"), 1)
                to_images("gkv", s, w_gkv, xT, 128, HW, X4, lambda t: [("lnga_aff", 2 * s + t // 8 + 1)],
                          [norm("lnga", s, "out", 2)])

            def class_output(s):
                to_channels("gagg", s, small[:, 272:336].unsqueeze(1), 1, X4, "gatt_done", [("gkv_used", 8 * s + 8)])
                pe.wait_ge(sem("gagg_used"), s + 1)
                for m in range(2):
                    for k in range(2):
                        last = mm(ps[:, 3 + m, 0:HB], w_gproj[:, k, m * P:(m + 1) * P],
                                  oT[:, k, s * NH:s * NH + HB], start=(k == 0), stop=(k == 1))
                    last.then_inc(sem("gproj_ready"), 1)
                norm_stats("ln0", s, hT, CH, lambda c: [], [("h_tok", 4 * s + 4), ("h_cls", 2 * s + 2)])

            def att0_qkv(s):
                to_images("qkv0", s, w_qkvg, xT, 256, T, X4, token_ready("ln0", s),
                          [("w_attn_in", 48), norm("ln0", s, "out", 2)])

            def att0_gate(s):
                linear("go", s, w_go, xT, CH, X4, lambda c: [], [("qkv0_used", 9 * s + 9)])

            def of_tokens(ap, i):
                return ap.rearrange("p (t b) -> p b t", b=HB)[:, i, :]

            def att0_channels(s):
                to_channels("att0", s, qkv(s, 256), T, Y4, "att0_done", [("win_done", ITERS), ("moe_used", 4 * s)])

            def att0_output(s):
                linear("wo", s, w_o, oT, CH, Y4, lambda c: [("att0_gated", 2 * s + c + 1)], [("att0_used", 3 * s + 3)])
                norm_stats("ln1", s, hT, CH, lambda c: [("wo_used", 4 * s + 2 * c + 2)], [("wo_used", 4 * s + 4)])

            def mqa_scores(s):
                t_ = mqa_of[s]
                linear("mq", s, w_mq, yT, CH, Y4, lambda c: [norm("rms1", s, "out", c + 1)],
                       [norm("ln1", s, "out", 2), ("w_ffn_in", 48)])
                pe.wait_ge(sem("mq_used"), 4 * s + 3)
                for c in range(2):
                    for k in range(2):
                        last = mm(ps[:, Y4[c], 0:CH], w_mk[:, k, :], yT[:, k, cols(s, c)],
                                  start=(k == 0), stop=(k == 1))
                    last.then_inc(sem("mk_ready"), 1)
                for g in range(8):
                    for k in range(2):
                        for j in range(4):
                            last = mm(ps[32 * j:32 * j + T, Y4[2], g * QC:(g + 1) * QC],
                                      of_tokens(yT[:, k, s * NH:(s + 1) * NH], 4 * g + j), w_mv[:, k, :],
                                      start=(k == 0), stop=(k == 1), skip_group_check=True)
                last.then_inc(sem("mv_ready"), 1)
                pe.wait_ge(sem("mk_used"), 2 * s + 2)
                for i in range(HB):
                    for h in range(4):
                        r = 64 * (h % 2)
                        last = mm(ps[32 * h:32 * h + T, Y4[i // 16], (i % 16) * T:(i % 16 + 1) * T],
                                  of_tokens(t_.q[r:r + 64, h // 2, :], i), of_tokens(t_.k[r:r + 64, :], i),
                                  start=True, stop=True, skip_group_check=True)
                    if i % 16 == 15:
                        last.then_inc(sem("msc_ready"), 1)

            def mqa_weigh(s):
                t_ = mqa_of[s]
                pe.wait_ge(sem("mq_used"), 4 * s + 4)
                pe.wait_ge(sem("mv_used"), s + 1)
                pe.wait_ge(sem("msc_done"), s + 1)
                for g in range(8):
                    last = nc.tensor.transpose(ps[:, Y4[2 + g // 4], (g % 4) * P:(g % 4 + 1) * P],
                                               t_.p[:, g * P:(g + 1) * P], ident[:, :])
                    if g % 4 == 3:
                        last.then_inc(sem("mpT_ready"), 1)
                pe.wait_ge(sem("mpT_used"), 2 * s + 2)
                for g in range(8):
                    for j in range(4):
                        w_ = t_.pT[32 * j:32 * j + T, g, :].rearrange("p (m r t) -> p r m t", m=2, r=2)
                        for r in range(2):
                            last = mm(ps[64 * r:64 * r + 64, Y4[j], 2 * T * g:2 * T * (g + 1)]
                                      .rearrange("p (m t) -> p m t", m=2),
                                      t_.v[32 * j:32 * j + T, g, :], w_[:, r, :, 0:T],
                                      start=True, stop=True, skip_group_check=True)
                        if g == 7:
                            last.then_inc(sem("att1_ready"), 1)

            def att1_output(s):
                linear("mo", s, w_mo, oT, CH, Y4, lambda c: [("att1_used", 4 * s + 4)])
                norm_stats("rms2", s, xT, CH, lambda c: [("mo_used", 4 * s + 2 * c + 2)], [("mo_used", 4 * s + 4)])

            def router(s):
                after(pe, *norm("rms2", s, "out", 2))
                for t in range(5):
                    n = min(P, NH - t * P)
                    for k in range(2):
                        c0 = s * NH + t * P
                        last = mm(ps[0:n, Y4[0], t * NEXP:(t + 1) * NEXP], yT[:, k, c0:c0 + n], w_r[:, k, :],
                                  start=(k == 0), stop=(k == 1))
                last.then_inc(sem("logits_ready"), 1)

            def combine(s):
                pe.wait_ge(sem("combine_done"), s + 1)
                cw = small[:, 0:40].rearrange("p (t e) -> p t e", t=5)
                for t in range(5):
                    n = min(P, NH - t * P)
                    last = nc.tensor.transpose(ps[0:NEXP, Y4[1 + t // 4], (t % 4) * P:(t % 4) * P + n],
                                               cw[0:n, t, :], ident[0:n, 0:n])
                last.then_inc(sem("cmb_ready"), 1)
                pe.wait_ge(sem("cmb_used"), s + 1)
                pe.wait_ge(sem("w_exp_in"), 16 * 9)
                pe.wait_ge(sem("tab_in"), 64)
                waits([("go_used", 8), ("qkv2_used", 9 * s), ("g_used", 4 * s)])

            def experts(s, c, drained=()):
                base = 36 * s + 18 * c
                waits(drained)
                after(pe, "moe_used", 4 * s + 2 * c)
                for n in range(18 + 2):
                    if n < 18:
                        e, m = n // 2, n % 2
                        if n >= 2:
                            pe.wait_ge(sem("eh_ready"), base + n - 1)
                        for w in range(2):
                            for k in range(2):
                                last = mm(ps[:, 2 + 2 * (n % 2) + w, 0:CH], w_exp[:, e, w, k, m * P:(m + 1) * P],
                                          yT[:, k, cols(s, c)], start=(k == 0), stop=(k == 1))
                            if w == 0 and m == 0 and e < NEXP:
                                mm(ps[:, 6 + e % 2, 0:CH], sel[:, e * P:(e + 1) * P],
                                   cmbT[:, c * CH:(c + 1) * CH], start=True, stop=True)
                        last.then_inc(sem("eup_ready"), 1)
                    if n >= 2:
                        d = n - 2
                        e, k = d // 2, d % 2
                        pe.wait_ge(sem("eh_ready"), base + d + 1)
                        for m in range(2):
                            last = mm(ps[:, m, 0:CH], w_exp[:, e, 2, k, m * P:(m + 1) * P], eh[d % 3],
                                      start=(d == 0), stop=(d == 17))
                        last.then_inc(sem("edown"), 1)

            def retention_stats(s):
                norm_stats("ln2", s, hT, CH, lambda c: [("moe_used", 4 * s + 2 * c + 2)])

            def retention_qkv(s):
                to_images("qkv2", s, w_l1qkv, xT, 192, T, X4, token_ready("ln2", s),
                          [("w_l1_in", 128), norm("ln2", s, "out", 2)])

            def retention_gate(s):
                linear("g", s, w_l1g, xT, CH, X4, lambda c: [], [("qkv2_used", 9 * s + 9)])

            def att2_channels(s):
                to_channels("att2", s, qkv(s, 192), T, Y4, "att2_done", [("moe_used", 8)])
                if s == 0:
                    pe.wait_ge(sem("gam_sum"), 1)
                    mm(ps[:, Y4[3], 0:2], avg[:, :], gam[:, 0:2], start=True, stop=True).then_inc(sem("gam_ready"), 1)

            def att2_output(s):
                linear("l1o", s, w_l1o, oT, CH, Y4, lambda c: [("att2_gated", 2 * s + c + 1)],
                       [("att2_used", 3 * s + 3), ("gam_used", 1)])

            def mlp(s):
                pe.wait_ge(sem("tern_done"), 1)
                norm_stats("ln3", s, hT, CH, lambda c: [("l1o_used", 4 * s + 2 * c + 2)],
                           [("qkv2_used", 18), ("g_used", 8), ("l1o_used", 4 * s + 4)])
                after(pe, *norm("ln3", s, "out", 2))
                for c in range(2):
                    k0 = 2 * s + c
                    for f in range(8):
                        after(pe, "hid_done", 8 * k0 + f - 3)
                        for k in range(2):
                            last = mm(ps[:, Y4[f % 4], 0:CH], w_t1[:, k, f * P:(f + 1) * P],
                                      xT[:, k, cols(s, c)], start=(k == 0), stop=(k == 1))
                        last.then_inc(sem("fc1_ready"), 1)
                    pe.wait_ge(sem("hid_done"), 8 * k0 + 8)
                    for m in range(2):
                        for f in range(8):
                            last = mm(ps[:, X4[2 * c + m], 0:CH], w_t2[:, f, m * P:(m + 1) * P],
                                      hid[:, c, f, :], start=(f == 0), stop=(f == 7))
                        last.then_inc(sem("fc2_ready"), 1)

            for i in range(4):
                conv(i)
                window_kv(i)
            conv(4)
            local_output(0)
            patch_output(0)
            global_kv(0)
            window_kv(4, [("gkv_used", 8)])
            conv(5)
            class_output(0)
            att0_qkv(0)
            att0_gate(0)
            window_kv(5, [("go_used", 4)])
            for i in range(6, ITERS):
                conv(i)
                window_kv(i)
            local_output(1)
            att0_channels(0)
            patch_output(1)
            att0_output(0)
            global_kv(1)
            mqa_scores(0)
            class_output(1)
            mqa_weigh(0)
            att1_output(0)
            att0_qkv(1)
            router(0)
            att0_gate(1)
            combine(0)
            experts(0, 0)
            experts(0, 1)
            att0_channels(1)
            retention_stats(0)
            att0_output(1)
            retention_qkv(0)
            mqa_scores(1)
            retention_gate(0)
            mqa_weigh(1)
            att1_output(1)
            router(1)
            combine(1)
            experts(1, 0)
            experts(1, 1)
            retention_stats(1)
            att2_channels(0)
            retention_qkv(1)
            att2_output(0)
            retention_gate(1)
            mlp(0)
            att2_channels(1)
            att2_output(1)
            mlp(1)

        @block.scalar
        def _(act):
            A = nc.scalar.activation

            def waits(pairs):
                for s, value in pairs:
                    after(act, s, value)

            def window_rstd(i):
                act.wait_ge(sem("var10"), i + 1)
                A(st10, st10, ACT.Ln).then_inc(sem("ln10"), 1)
                act.wait_ge(sem("ln10"), i + 1)
                A(st10, st10, ACT.Exp, scale=-0.5).then_inc(sem("rstd10"), 1)

            def window_exp(i):
                act.wait_ge(sem("sc_max"), i + 1)
                A(sc, sc, ACT.Exp, scale=C ** -0.5).then_inc(sem("sc_exp"), 1)

            def conv_evac(i):
                for g in range(2 * NCG):
                    c, m = g // 2, g % 2
                    pc = slice(c * CONV_N, (c + 1) * CONV_N)
                    act.wait_ge(sem("conv_ready"), 6 * i + g + 1)
                    if g == 0:
                        after(act, "sums_ready", i)
                    A(patch_emb[:, m, pc], ps[:, g % 2, 0:CONV_N], ACT.Copy)
                    A(patch_sq[:, m, pc], ps[:, g % 2, 0:CONV_N], ACT.Square).then_inc(sem("conv_evac"), 1)
                    if g == 0 and i > 0:
                        window_rstd(i - 1)
                    if g == 3 and i > 0:
                        window_exp(i - 1)

            def kv_evac(i):
                after(act, "win_done", i)
                for j in range(NJ):
                    act.wait_ge(sem("kv_ready"), 9 * i + j + 1)
                    b = 2 + 2 * (j % 2)
                    A(kv_raw[:, j, :, 0:KVN], ps[:, b:b + 2, 0:KVN], ACT.Copy).then_inc(sem("kv_evac"), 1)

            def norm_act(name, s, src, n, src_ready, drained=()):
                banks = NORM_BANKS[name]
                waits(drained)
                for c in range(2) if name != "rms1" else ():
                    waits(src_ready(c))
                    after(act, "norm_stat", norm(name, s, "stat", c + 1)[1] - 2)
                    A(sqb[:, spot(name, s, c) % 2, :, 0:n], src[:, :, cols(s, c, n)],
                      ACT.Square).then_inc(sem("norm_sq"), 1)
                if not name.startswith("rms"):
                    for c in range(2):
                        after(act, *norm(name, s, "stat", c + 1))
                        after(act, "norm_out", spot(name, s, c) - 1)
                        A(lnv[:, spot(name, s, c) % 2, 0:n], ps[:, banks[2 * c], 0:n],
                          ACT.Square).then_inc(sem("norm_mu2"), 1)
                for c in range(2):
                    r = lnv[:, spot(name, s, c) % 2, 0:n]
                    after(act, *norm(name, s, "var", c + 1))
                    A(r, r, ACT.Ln).then_inc(sem("norm_ln"), 1)
                    after(act, *norm(name, s, "ln", c + 1))
                    A(r, r, ACT.Exp, scale=-0.5).then_inc(sem("norm_rstd"), 1)

            def images_evac(name, s, dst, n, nt, banks, gate=False):
                for g in range((nt + 1) // 2):
                    k = min(2, nt - 2 * g)
                    act.wait_ge(sem(name + "_ready"), (nt + 1) // 2 * s + g + 1)
                    src = ps[:, banks[g % 4], 0:k * n].rearrange("p (t n) -> p t n", t=k)
                    to = dst[:, 2 * g:2 * g + k, :]
                    if gate:
                        A(to[:, :, 0:3 * QC], src[:, :, 0:3 * QC], ACT.Copy)
                        last = A(to[:, :, 3 * QC:4 * QC], src[:, :, 3 * QC:4 * QC], ACT.Sigmoid)
                    else:
                        last = A(to, src, ACT.Copy)
                    last.then_inc(sem(name + "_used"), 1)

            def channels_evac(name, s, banks):
                for g in range(3):
                    n = min(8, T - 8 * g)
                    act.wait_ge(sem(name + "_ready"), 3 * s + g + 1)
                    c0 = s * NH + 8 * g * HB
                    A(oT[:, :, c0:c0 + n * HB].rearrange("p m (t b) -> p m t b", t=n),
                      ps[:, banks[g], 0:n * QC].rearrange("p (t m b) -> p m t b", t=n, m=2),
                      ACT.Copy).then_inc(sem(name + "_used"), 1)

            def local_output(s):
                for g in range(2):
                    act.wait_ge(sem("aggT_ready"), 2 * s + g + 1)
                    c0 = s * NH + 2 * g * P
                    A(xT[:, :, c0:c0 + 2 * P].rearrange("p m (i n) -> p m i n", i=2),
                      ps[:, X4[g], :].rearrange("p (i m n) -> p m i n", i=2, m=2),
                      ACT.Copy).then_inc(sem("aggT_used"), 1)

            def patch_output(s):
                for c in range(2):
                    for m in range(2):
                        act.wait_ge(sem("mod_ready"), 4 * s + 2 * c + m + 1)
                        A(hT[:, m, cols(s, c, LC)], ps[:, X4[2 * c + m], 0:LC], ACT.Identity,
                          bias=v("mod_b", m)).then_inc(sem("h_tok"), 1)
                norm_act("lnga", s, yT, LC, lambda c: [("local_out", 4 * s + 2 * c + 2)])
                for c in range(2):
                    after(act, *norm("lnga", s, "out", c + 1))
                    for m in range(2):
                        y = xT[:, m, cols(s, c, LC)]
                        last = A(y, y, ACT.Identity, bias=v("ga_ln_kv_b", m), scale=v("ga_ln_kv_g", m))
                    last.then_inc(sem("lnga_aff"), 1)

            def class_norm():
                act.wait_ge(sem("cls_var"), 1)
                A(small[:, 8:9], small[:, 8:9], ACT.Ln).then_inc(sem("cls_ln"), 1)
                act.wait_ge(sem("cls_ln"), 1)
                A(small[:, 8:9], small[:, 8:9], ACT.Exp, scale=-0.5).then_inc(sem("cls_rstd"), 1)

            def global_kv(s):
                if s == 1:
                    act.wait_ge(sem("win_done"), ITERS)
                images_evac("gkv", s, qkv(s, 128), 128, HW, X4)

            def ga_exp(s):
                act.wait_ge(sem("gsc_max"), s + 1)
                A(S[:, 0:32], S[:, 0:32], ACT.Exp, scale=C ** -0.5).then_inc(sem("gsc_exp"), 1)

            def class_output(s):
                act.wait_ge(sem("gagg_ready"), s + 1)
                A(oT[:, :, s * NH:s * NH + HB], ps[:, 2, 0:QC].rearrange("p (m b) -> p m b", m=2),
                  ACT.Copy).then_inc(sem("gagg_used"), 1)
                norm_act("ln0", s, hT, CH, lambda c: [("h_tok", 4 * s + 4), ("h_cls", 2 * s + 2)])

            def att0_qkv(s):
                act.wait_ge(sem("gatt_done"), s + 1)
                images_evac("qkv0", s, qkv(s, 256), 256, T, X4, gate=True)

            def att0_gate(s):
                for c in range(2):
                    for m in range(2):
                        act.wait_ge(sem("go_ready"), 4 * s + 2 * c + m + 1)
                        A(yT[:, m, cols(s, c)], ps[:, X4[2 * c + m], 0:CH], ACT.Sigmoid).then_inc(sem("go_used"), 1)

            def att_exp(name, s, nh, scale):
                act.wait_ge(sem(name + "_max"), s + 1)
                A(S[:, 0:T * T * nh], S[:, 0:T * T * nh], ACT.Exp, scale=scale).then_inc(sem(name + "_exp"), 1)

            def att0_channels(s):
                channels_evac("att0", s, Y4)

            def att0_output(s):
                norm_act("ln1", s, hT, CH, lambda c: [("wo_used", 4 * s + 2 * c + 2)])
                norm_act("rms1", s, xT, CH, lambda c: [])

            def mqa_scores(s):
                t_ = mqa_of[s]
                for c in range(2):
                    for m in range(2):
                        act.wait_ge(sem("mq_ready"), 4 * s + 2 * c + m + 1)
                        A(t_.q[:, m, c * CH:(c + 1) * CH], ps[:, Y4[2 * c + m], 0:CH],
                          ACT.Copy).then_inc(sem("mq_used"), 1)
                for c in range(2):
                    act.wait_ge(sem("mk_ready"), 2 * s + c + 1)
                    A(t_.k[:, c * CH:(c + 1) * CH], ps[:, Y4[c], 0:CH], ACT.Copy).then_inc(sem("mk_used"), 1)
                act.wait_ge(sem("mv_ready"), s + 1)
                A(t_.v_flat, ps[:, Y4[2], :], ACT.Copy).then_inc(sem("mv_used"), 1)

            def mqa_exp(s):
                t_ = mqa_of[s]
                act.wait_ge(sem("att1_max"), s + 1)
                A(t_.p3[:, :, 0:T], t_.p3[:, :, 0:T], ACT.Exp, scale=QC ** -0.5).then_inc(sem("att1_exp"), 1)

            def mqa_weigh(s):
                t_ = mqa_of[s]
                for b in range(2):
                    act.wait_ge(sem("mpT_ready"), 2 * s + b + 1)
                    A(t_.pT[:, 4 * b:4 * b + 4, :], ps[:, Y4[2 + b], :].rearrange("p (g n) -> p g n", g=4),
                      ACT.Copy).then_inc(sem("mpT_used"), 1)
                for b in range(4):
                    act.wait_ge(sem("att1_ready"), 4 * s + b + 1)
                    to = oT[:, :, s * NH:(s + 1) * NH].rearrange("p m (t g j) -> p m t g j", g=8, j=4)
                    A(to[:, :, :, :, b],
                      ps[:, Y4[b], 0:8 * 2 * T].rearrange("p (b m t) -> p m t b", b=8, m=2),
                      ACT.Copy).then_inc(sem("att1_used"), 1)

            def att1_output(s):
                norm_act("rms2", s, xT, CH, lambda c: [("mo_used", 4 * s + 2 * c + 2)])

            def router(s):
                act.wait_ge(sem("lg_max"), s + 1)
                A(small[:, 0:40], small[:, 0:40], ACT.Exp).then_inc(sem("lg_exp"), 1)
                act.wait_ge(sem("rw_max"), s + 1)
                A(small[:, 40:80], small[:, 40:80], ACT.Exp).then_inc(sem("rw_exp"), 1)

            def combine(s):
                act.wait_ge(sem("cmb_ready"), s + 1)
                A(cmbT[:, 0:512], ps[0:NEXP, Y4[1], :], ACT.Copy)
                A(cmbT[:, 512:NH], ps[0:NEXP, Y4[2], 0:NH - 512], ACT.Copy).then_inc(sem("cmb_used"), 1)

            def experts(s, c, exp_at=None, exp=None):
                base = 36 * s + 18 * c
                for n in range(18):
                    act.wait_ge(sem("eup_ready"), base + n + 1)
                    after(act, "eh_ready", base + n - 1)
                    A(esil[n % 2], ps[:, 2 + 2 * (n % 2), 0:CH], ACT.Silu).then_inc(sem("esil_ready"), 1)
                    if n == exp_at:
                        exp()

            def retention_stats(s):
                norm_act("ln2", s, hT, CH, lambda c: [("moe_used", 4 * s + 2 * c + 2)])

            def retention_qkv(s):
                images_evac("qkv2", s, qkv(s, 192), 192, T, X4)

            def retention_gate(s):
                for c in range(2):
                    for m in range(2):
                        act.wait_ge(sem("g_ready"), 4 * s + 2 * c + m + 1)
                        A(yT[:, m, cols(s, c)], ps[:, X4[2 * c + m], 0:CH], ACT.Silu).then_inc(sem("g_used"), 1)

            def group_norm(s):
                act.wait_ge(sem("gn_var"), s + 1)
                A(S[:, 0:34], S[:, 0:34], ACT.Ln).then_inc(sem("gn_ln"), 1)
                act.wait_ge(sem("gn_ln"), s + 1)
                A(S[:, 0:34], S[:, 0:34], ACT.Exp, scale=-0.5).then_inc(sem("gn_rstd"), 1)

            def mlp(s):
                norm_act("ln3", s, hT, CH, lambda c: [("l1o_used", 4 * s + 2 * c + 2)])
                for c in range(2):
                    k0 = 2 * s + c
                    for f in range(8):
                        act.wait_ge(sem("fc1_ready"), 8 * k0 + f + 1)
                        if f == 0:
                            after(act, "fc2_ready", 2 * k0 - 2)
                        A(hid[:, c, f, :], ps[:, Y4[f % 4], 0:CH], ACT.Relu,
                          bias=v("b1", f)).then_inc(sem("hid_done"), 1)

            def ln_exp_table():
                nc.scalar.preload_act_table_set("natural_log_exp_and_others")

            ln_exp_table()
            act.wait_ge(sem("w_first_in"), 64)
            for i in range(4):
                conv_evac(i)
                kv_evac(i)
            conv_evac(4)
            local_output(0)
            patch_output(0)
            class_norm()
            global_kv(0)
            ga_exp(0)
            kv_evac(4)
            conv_evac(5)
            class_output(0)
            att0_qkv(0)
            att0_gate(0)
            ln_exp_table()
            kv_evac(5)
            conv_evac(6)
            kv_evac(6)
            att_exp("att0", 0, 4, 16 ** -0.5)
            conv_evac(7)
            kv_evac(7)
            window_rstd(7)
            window_exp(7)
            local_output(1)
            att0_channels(0)
            patch_output(1)
            att0_output(0)
            global_kv(1)
            mqa_scores(0)
            ga_exp(1)
            mqa_exp(0)
            class_output(1)
            mqa_weigh(0)
            att1_output(0)
            att0_qkv(1)
            ln_exp_table()
            router(0)
            att0_gate(1)
            combine(0)
            experts(0, 0, 17, lambda: att_exp("att0", 1, 4, 16 ** -0.5))
            experts(0, 1)
            ln_exp_table()
            att0_channels(1)
            retention_stats(0)
            att0_output(1)
            retention_qkv(0)
            mqa_scores(1)
            mqa_exp(1)
            mqa_weigh(1)
            att1_output(1)
            router(1)
            combine(1)
            retention_gate(0)
            experts(1, 0)
            experts(1, 1)
            ln_exp_table()
            group_norm(0)
            retention_stats(1)
            channels_evac("att2", 0, Y4)
            retention_qkv(1)
            retention_gate(1)
            ln_exp_table()
            mlp(0)
            group_norm(1)
            channels_evac("att2", 1, Y4)
            mlp(1)

        @block.vector
        def _(dve):
            V = nc.vector
            steps = [0]

            def waits(pairs):
                for s, value in pairs:
                    after(dve, s, value)

            def mark(ins):
                steps[0] += 1
                ins.then_inc(sem("dve_step"), 1)
                return steps[0]

            def need(count):
                dve.wait_ge(sem("dve_step"), count)

            def link(ins):
                need(mark(ins))

            V.memset(ps[:, Y4[2], :], 0.0)
            link(V.memset(avg[:, :], 1.0 / C))
            dve.wait_ge(sem("w_first_in"), 64)
            for k in range(2):
                V.tensor_scalar(w_kvc[:, k, :, 0:C], w_kv[:, k, :].rearrange("p (s n) -> p s n", s=2),
                                v("la_ln_kv_g", k), None, ALU.mult)
                V.tensor_scalar(w_lqc[:, k, 0:C], w_lq[:, k, :], v("la_ln_q_g", k), None, ALU.mult)
            V.memset(w_kvc[:, :, :, C:KVS], 1.0 / C)
            V.memset(w_lqc[:, :, C:KVS], 1.0 / C).then_inc(sem("w_scaled"), 1)
            for k in range(2):
                last = V.tensor_scalar(bcol[:, k, :], avg[:, :], v("la_ln_kv_b", k), float(C), ALU.mult, ALU.mult)
            last.then_inc(sem("kv_bcol"), 1)
            dve.wait_ge(sem("w_means"), 1)
            for k in range(2):
                V.tensor_tensor(w_kvc[:, k, :, 0:C], w_kvc[:, k, :, 0:C],
                                ps[:, 2, :].rearrange("p (s n) -> p s n", s=2), ALU.subtract)
                last = V.tensor_tensor(w_lqc[:, k, 0:C], w_lqc[:, k, 0:C], ps[:, 3, 0:C], ALU.subtract)
            link(last)
            dve.wait_ge(sem("kv_brow"), 1)
            link(V.tensor_copy(bias_row[:, 0:2 * C], ps[:, 4, :]))
            for k in range(2):
                last = V.tensor_scalar(bcol[:, k, :], avg[:, :], v("la_ln_q_b", k), float(C), ALU.mult, ALU.mult)
            last.then_inc(sem("q_bcol"), 1)
            dve.wait_ge(sem("q_brow"), 1)
            V.tensor_copy(bias_row[:, 2 * C:3 * C], ps[:, 5, 0:C]).then_inc(sem("w_kv_ready"), 1)
            dve.wait_ge(sem("w_kv_ready"), 1)

            sc3 = sc.rearrange("p (j h) -> p j h", j=NJ)

            def window_sums(i):
                s, r = i // 4, i % 4
                dve.wait_ge(sem("conv_evac"), 6 * i + 6)
                after(dve, "stat_ready", i)
                link(V.tensor_reduce(red_sq, patch_emb.rearrange("p m (j n) -> p m n j", j=NJ), AX.X, ALU.add))
                link(V.tensor_scalar(red, red_sq, 1.0 / NJ, None, ALU.mult))
                V.tensor_copy(yT[:, :, s * NH + r * P:s * NH + (r + 1) * P], red)
                link(V.tensor_tensor(red_sq, red, red, ALU.mult))
                link(V.tensor_tensor(rsq_sum, red_sq[:, 0, :], red_sq[:, 1, :], ALU.add))
                V.tensor_tensor(sq_sum, patch_sq[:, 0, :], patch_sq[:, 1, :], ALU.add).then_inc(sem("sums_ready"), 1)

            def window_attention(i):
                dve.wait_ge(sem("stat_ready"), i + 1)
                dve.wait_ge(sem("kv_evac"), 9 * i + 9)
                st = ps[:, 6 + i % 2, :]
                V.tensor_copy(mean10[:, 0:NJ], kv_raw[:, :, 0, C])
                link(V.tensor_copy(mean10[:, NJ:NJ + 1], st[:, C:C + 1]))
                link(V.tensor_tensor(mean10, mean10, mean10, ALU.mult))
                link(V.tensor_tensor(st10, st[:, 300:310], mean10, ALU.subtract))
                V.tensor_scalar(st10, st10, 0.0, EPS_LN, ALU.max, ALU.add).then_inc(sem("var10"), 1)
                dve.wait_ge(sem("rstd10"), i + 1)
                link(V.scalar_tensor_tensor(out=q_win, in0=st[:, 0:C], scalar=st10[:, NJ:NJ + 1],
                                            in1=bias_row[:, 2 * C:3 * C], op0=ALU.mult, op1=ALU.add))
                prod3 = prodW.rearrange("p (j n) -> p j n", j=NJ)
                V.tensor_tensor(qk_tmp, q_win, bias_row[:, 0:C], ALU.mult)
                link(V.tensor_tensor(prod3, kv_raw[:, :, 0, 0:C],
                                     q_win.unsqueeze(1).to_broadcast([P, NJ, C]), ALU.mult))
                V.tensor_reduce(qb8, qk_tmp.rearrange("p (h d) -> p h d", h=8), AX.X, ALU.add)
                link(V.tensor_reduce(sc, prodW.rearrange("p (a d) -> p a d", d=32), AX.X, ALU.add))
                r9 = st10[:, 0:NJ].unsqueeze(2).to_broadcast([P, NJ, 8])
                link(V.tensor_tensor(sc3, sc3, r9, ALU.mult))
                link(V.tensor_tensor(sc3, sc3, qb8.unsqueeze(1).to_broadcast([P, NJ, 8]), ALU.add))
                link(V.tensor_reduce(sm8, sc.rearrange("p (j h) -> p h j", j=NJ), AX.X, ALU.max))
                V.tensor_tensor(sc3, sc3, sm8.unsqueeze(1).to_broadcast([P, NJ, 8]),
                                ALU.subtract).then_inc(sem("sc_max"), 1)
                dve.wait_ge(sem("sc_exp"), i + 1)
                link(V.tensor_reduce(sm8, sc.rearrange("p (j h) -> p h j", j=NJ), AX.X, ALU.add))
                link(V.reciprocal(qb8, sm8))
                link(V.tensor_tensor(sc3, sc3, qb8.unsqueeze(1).to_broadcast([P, NJ, 8]), ALU.mult))
                link(V.tensor_tensor(sc3, sc3, r9, ALU.mult))
                link(V.tensor_tensor(prodW.rearrange("p (j h d) -> p j h d", j=NJ, h=8),
                                     kv_raw[:, :, 1, 0:C].rearrange("p j (h d) -> p j h d", h=8),
                                     sc3.unsqueeze(3).to_broadcast([P, NJ, 8, 32]), ALU.mult))
                link(V.tensor_reduce(qk_tmp, prodW.rearrange("p (j n) -> p n j", j=NJ), AX.X, ALU.add))
                V.tensor_tensor(aggW[:, i % 4, :], qk_tmp, bias_row[:, C:2 * C], ALU.add).then_inc(sem("win_done"), 1)
                dve.wait_ge(sem("win_done"), i + 1)

            def norm_dve(name, s, src, dst, n, eps, gain=None, drained=()):
                banks = NORM_BANKS[name]
                centred = not name.startswith("rms")
                waits(drained)
                x = []
                for c in range(2):
                    r = lnv[:, spot(name, s, c) % 2, 0:n]
                    cc = cols(s, c, n)
                    if name != "rms1":
                        after(dve, *norm(name, s, "stat", c + 1))
                    if name == "rms1":
                        after(dve, "norm_out", spot(name, s, c) - 1)
                        link(V.tensor_tensor(r, r, r, ALU.mult))
                        link(V.tensor_tensor(r, r, sqb[:, c, 0, 0:n], ALU.mult))
                        V.tensor_scalar(r, r, eps, None, ALU.add).then_inc(sem("norm_var"), 1)
                    elif centred:
                        after(dve, *norm(name, s, "mu2", c + 1))
                        link(V.tensor_tensor(r, ps[:, banks[2 * c + 1], 0:n], r, ALU.subtract))
                        if name == "ln1":
                            V.tensor_scalar(sqb[:, c, 0, 0:n], r, 0.0, None, ALU.max)
                        V.tensor_scalar(r, r, 0.0, eps, ALU.max, ALU.add).then_inc(sem("norm_var"), 1)
                        x.append(mark(V.tensor_tensor(
                            dst[:, :, cc], src[:, :, cc],
                            ps[:, banks[2 * c], 0:n].unsqueeze(1).to_broadcast([P, 2, n]), ALU.subtract)))
                    else:
                        after(dve, "norm_out", spot(name, s, c) - 1)
                        V.tensor_scalar(r, ps[:, banks[2 * c + 1], 0:n], eps, None,
                                        ALU.add).then_inc(sem("norm_var"), 1)
                for c in range(2):
                    r = lnv[:, spot(name, s, c) % 2, 0:n]
                    cc = cols(s, c, n)
                    after(dve, *norm(name, s, "rstd", c + 1))
                    if centred:
                        need(x[c])
                        last = V.tensor_tensor(dst[:, :, cc], dst[:, :, cc],
                                               r.unsqueeze(1).to_broadcast([P, 2, n]), ALU.mult)
                    else:
                        for m in range(2):
                            last = V.scalar_tensor_tensor(out=dst[:, m, cc], in0=src[:, m, cc], scalar=v(gain, m),
                                                          in1=r, op0=ALU.mult, op1=ALU.mult)
                    last.then_inc(sem("norm_out"), 1)

            gq = small[:, 144:144 + QC]

            def class_query():
                for k in range(2):
                    V.tensor_copy(small[:, 2 * k:2 * k + 1], v("class_emb", k))
                    last = V.tensor_tensor(small[:, 2 * k + 1:2 * k + 2], v("class_emb", k), v("class_emb", k),
                                           ALU.mult)
                last.then_inc(sem("cls_cols"), 1)
                dve.wait_ge(sem("cls_stat"), 1)
                link(V.tensor_copy(small[:, 6:8], ps[:, 2, 0:2]))
                link(V.tensor_tensor(small[:, 5:6], small[:, 6:7], small[:, 6:7], ALU.mult))
                link(V.tensor_tensor(small[:, 8:9], small[:, 7:8], small[:, 5:6], ALU.subtract))
                V.tensor_scalar(small[:, 8:9], small[:, 8:9], 0.0, EPS_LN, ALU.max, ALU.add).then_inc(sem("cls_var"), 1)
                dve.wait_ge(sem("cls_rstd"), 1)
                for k in range(2):
                    link(V.tensor_scalar(small[:, 10 + k:11 + k], v("class_emb", k), small[:, 6:7], small[:, 8:9],
                                         ALU.subtract, ALU.mult))
                    link(V.scalar_tensor_tensor(out=small[:, 12 + k:13 + k], in0=small[:, 10 + k:11 + k],
                                                scalar=v("ga_ln_q_g", k), in1=v("ga_ln_q_b", k),
                                                op0=ALU.mult, op1=ALU.add))
                for k in range(2):
                    last = V.tensor_scalar(small[:, 16 + 64 * k:48 + 64 * k], avg[:, 0:32], small[:, 12 + k:13 + k],
                                           float(C), ALU.mult, ALU.mult)
                last.then_inc(sem("cls_bcast"), 1)
                dve.wait_ge(sem("gq_ready"), 1)
                V.tensor_copy(gq, ps[:, 3, 0:QC]).then_inc(sem("gq_used"), 1)
                dve.wait_ge(sem("gq_used"), 1)
                link(V.tensor_tensor(small[:, 4:6], vec[:, VCOL["class_emb"]:VCOL["class_emb"] + 2],
                                     vec[:, VCOL["ga_proj_b"]:VCOL["ga_proj_b"] + 2], ALU.add))

            def local_out(s):
                for c in range(2):
                    for m in range(2):
                        dve.wait_ge(sem("proj_ready"), 4 * s + 2 * c + m + 1)
                        y = yT[:, m, cols(s, c, LC)]
                        V.scalar_tensor_tensor(out=y, in0=ps[:, X4[2 * c + m], 0:LC], scalar=v("la_proj_b", m),
                                               in1=y, op0=ALU.add, op1=ALU.add).then_inc(sem("local_out"), 1)

            def global_attention(s):
                gkv = qkv(s, 128)[:, 0:HW, :]
                dve.wait_ge(sem("gkv_used"), 8 * s + 8)
                pa = prods[0][:, 0:HW * QC]
                gs = S[:, 0:32]
                gs3 = gs.rearrange("p (t h) -> p t h", t=HW)
                g2, gi = S[:, 64:66], S[:, 66:68]
                link(V.tensor_tensor(pa.rearrange("p (t n) -> p t n", t=HW), gkv[:, :, 0:QC],
                                     gq.unsqueeze(1).to_broadcast([P, HW, QC]), ALU.mult))
                link(V.tensor_reduce(gs, pa.rearrange("p (a d) -> p a d", d=32), AX.X, ALU.add))
                link(V.tensor_reduce(g2, gs.rearrange("p (t h) -> p h t", t=HW), AX.X, ALU.max))
                V.tensor_tensor(gs3, gs3, g2.unsqueeze(1).to_broadcast([P, HW, 2]),
                                ALU.subtract).then_inc(sem("gsc_max"), 1)
                dve.wait_ge(sem("gsc_exp"), s + 1)
                link(V.tensor_reduce(g2, gs.rearrange("p (t h) -> p h t", t=HW), AX.X, ALU.add))
                link(V.reciprocal(gi, g2))
                link(V.tensor_tensor(gs3, gs3, gi.unsqueeze(1).to_broadcast([P, HW, 2]), ALU.mult))
                link(V.tensor_tensor(pa.rearrange("p (t h d) -> p t h d", t=HW, h=2),
                                     gkv[:, :, QC:2 * QC].rearrange("p t (h d) -> p t h d", h=2),
                                     gs3.unsqueeze(3).to_broadcast([P, HW, 2, 32]), ALU.mult))
                V.tensor_reduce(small[:, 272:336], pa.rearrange("p (t n) -> p n t", t=HW), AX.X,
                                ALU.add).then_inc(sem("gatt_done"), 1)

            def class_token(s):
                for m in range(2):
                    dve.wait_ge(sem("gproj_ready"), 2 * s + m + 1)
                    V.tensor_scalar(hT[:, m, s * NH + NWH:(s + 1) * NH], ps[:, 3 + m, 0:HB], small[:, 4 + m:5 + m],
                                    None, ALU.add).then_inc(sem("h_cls"), 1)

            def rotate(x, nh, d, cs, sn):
                xv = x.rearrange("p t (h d) -> p t h d", h=nh)
                pv = prods[0].rearrange("p (t h d) -> p t h d", t=T, h=nh)
                h_ = d // 2
                half = [P, T, nh, h_]
                V.tensor_tensor(pv[:, :, :, 0:h_], xv[:, :, :, h_:d],
                                sn[:, :, 0:h_].unsqueeze(2).to_broadcast(half), ALU.mult)
                link(V.tensor_tensor(pv[:, :, :, h_:d], xv[:, :, :, 0:h_],
                                     sn[:, :, h_:d].unsqueeze(2).to_broadcast(half), ALU.mult))
                link(V.tensor_tensor(xv, xv, cs.unsqueeze(2).to_broadcast([P, T, nh, d]), ALU.mult))
                link(V.tensor_tensor(xv, xv, pv, ALU.add))

            def weighted(product, reduce, cut):
                for first, end in ((0, cut), (cut, T)):
                    p_done, s_done = [], []
                    for t in range(end - first + 1):
                        if t < end - first:
                            if t >= 2:
                                need(s_done[t - 2])
                            p_done.append(mark(product(first + t)))
                        if t >= 1:
                            need(p_done[t - 1])
                            s_done.append(mark(reduce(first + t - 1)))
                            if t == end - first:
                                need(s_done[-1])
                            yield

            def scores(q, k_, nh, sizes, cut=T):
                d = QC // nh
                return weighted(
                    lambda t: V.tensor_tensor(
                        prods[t % 2][:, 0:sizes[t] * QC].rearrange("p (k c) -> p k c", c=QC), k_[:, 0:sizes[t], :],
                        q[:, t, :].unsqueeze(1).to_broadcast([P, sizes[t], QC]), ALU.mult),
                    lambda t: V.tensor_reduce(
                        S[:, t * T * nh:t * T * nh + sizes[t] * nh],
                        prods[t % 2][:, 0:sizes[t] * QC].rearrange("p (a d) -> p a d", d=d), AX.X, ALU.add), cut)

            def weigh(v_, o_, nh, sizes, cut=T):
                d = QC // nh
                return weighted(
                    lambda t: V.tensor_tensor(
                        prods[t % 2][:, 0:sizes[t] * QC].rearrange("p (k h d) -> p k h d", h=nh, d=d),
                        v_[:, 0:sizes[t], :].rearrange("p k (h d) -> p k h d", h=nh),
                        S[:, t * T * nh:t * T * nh + sizes[t] * nh].rearrange("p (k h) -> p k h", h=nh)
                        .unsqueeze(3).to_broadcast([P, sizes[t], nh, d]), ALU.mult),
                    lambda t: V.tensor_reduce(
                        o_[:, t, :], prods[t % 2][:, 0:sizes[t] * QC].rearrange("p (k c) -> p c k", c=QC),
                        AX.X, ALU.add), cut)

            def softmax_shift(name, nh):
                s4 = S[:, 0:T * T * nh].rearrange("p (t k h) -> p t k h", t=T, k=T)
                mx = prods[0][:, 0:T * nh].rearrange("p (t h) -> p t h", t=T)
                link(V.tensor_reduce(mx, S[:, 0:T * T * nh].rearrange("p (t k h) -> p t h k", t=T, k=T),
                                     AX.X, ALU.max))
                V.tensor_tensor(s4, s4, mx.unsqueeze(2).to_broadcast([P, T, T, nh]),
                                ALU.subtract).then_inc(sem(name + "_max"), 1)

            def softmax_scale(name, s, nh):
                s4 = S[:, 0:T * T * nh].rearrange("p (t k h) -> p t k h", t=T, k=T)
                ri = prods[0][:, T * nh:2 * T * nh]
                dve.wait_ge(sem(name + "_exp"), s + 1)
                link(V.tensor_reduce(prods[0][:, 0:T * nh].rearrange("p (t h) -> p t h", t=T),
                                     S[:, 0:T * T * nh].rearrange("p (t k h) -> p t h k", t=T, k=T), AX.X, ALU.add))
                link(V.reciprocal(ri, prods[0][:, 0:T * nh]))
                link(V.tensor_tensor(s4, s4, ri.rearrange("p (t h) -> p t h", t=T).unsqueeze(2)
                                     .to_broadcast([P, T, T, nh]), ALU.mult))

            def att0_scores(s):
                q = qkv(s, 256)
                link(V.memset(S, MASKED))
                dve.wait_ge(sem("tab_in"), 64)
                dve.wait_ge(sem("qkv0_used"), 9 * s + 9)
                link(V.tensor_tensor(q[:, :, 128:192], q[:, :, 128:192], q[:, :, 192:256], ALU.mult))
                rotate(q[:, :, 0:64], 4, 16, rope[:, 0], rope[:, 1])
                yield
                rotate(q[:, :, 64:128], 4, 16, rope[:, 0], rope[:, 1])
                yield
                yield from scores(q[:, :, 0:64], q[:, :, 64:128], 4, CAUSAL, cut=CUT_SCORES)

            def att0_weigh(s):
                q = qkv(s, 256)
                yield from weigh(q[:, :, 128:192], q[:, :, 0:64], 4, CAUSAL, cut=CUT_WEIGH)

            def mqa_softmax(s):
                t_ = mqa_of[s]
                link(V.memset(t_.p, 0.0))
                for b in range(2):
                    dve.wait_ge(sem("msc_ready"), 2 * s + b + 1)
                    half = slice(16 * b, 16 * b + 16)
                    sc_ = ps[:, Y4[b], 0:16 * T].rearrange("p (i k) -> p i k", k=T)
                    link(V.tensor_reduce(t_.top[:, half], sc_, AX.X, ALU.max))
                    last = V.tensor_tensor(t_.p3[:, half, 0:T], sc_,
                                           t_.top[:, half].unsqueeze(2).to_broadcast([P, 16, T]), ALU.subtract)
                last.then_inc(sem("att1_max"), 1)
                dve.wait_ge(sem("att1_exp"), s + 1)
                link(V.tensor_reduce(t_.top, t_.p3[:, :, 0:T], AX.X, ALU.add))
                link(V.reciprocal(t_.inv, t_.top))
                V.tensor_tensor(t_.p3[:, :, 0:T], t_.p3[:, :, 0:T], t_.inv.unsqueeze(2).to_broadcast([P, HB, T]),
                                ALU.mult).then_inc(sem("msc_done"), 1)

            def att2_scores(s):
                q = qkv(s, 192)
                dve.wait_ge(sem("w_l1_in"), 128)
                dve.wait_ge(sem("qkv2_used"), 9 * s + 9)
                rotate(q[:, :, 0:64], 2, 32, xpos[:, 0], xpos[:, 1])
                yield
                rotate(q[:, :, 64:128], 2, 32, xpos[:, 2], xpos[:, 3])
                yield
                yield from scores(q[:, :, 0:64], q[:, :, 64:128], 2, CAUSAL)
                for t in range(T):
                    w = slice(t * T * 2, t * T * 2 + (t + 1) * 2)
                    last = V.tensor_tensor(S[:, w], S[:, w], decay[:, w], ALU.mult)
                link(last)

            def att2_weigh(s):
                q = qkv(s, 192)
                yield from weigh(q[:, :, 128:192], q[:, :, 0:64], 2, CAUSAL)

            def done(name):
                V.memset(prods[0][:, 0:1], 0.0).then_inc(sem(name + "_done"), 1)

            def run(steps_, n=None):
                for i, _ in enumerate(steps_):
                    if n is not None and i + 1 >= n:
                        return

            def att0_gated(s):
                for c in range(2):
                    dve.wait_ge(sem("att0_used"), 3 * s + min(3, ((c + 1) * CH - 1) // 256 + 1))
                    dve.wait_ge(sem("go_used"), 4 * s + 4)
                    V.tensor_tensor(oT[:, :, cols(s, c)], oT[:, :, cols(s, c)], yT[:, :, cols(s, c)],
                                    ALU.mult).then_inc(sem("att0_gated"), 1)

            def add_to_h(name, s, banks):
                for c in range(2):
                    for m in range(2):
                        y = hT[:, m, cols(s, c)]
                        dve.wait_ge(sem(name + "_ready"), 4 * s + 2 * c + m + 1)
                        V.tensor_tensor(y, y, ps[:, banks[2 * c + m], 0:CH], ALU.add).then_inc(sem(name + "_used"), 1)

            def att0_output(s):
                add_to_h("wo", s, Y4)
                norm_dve("ln1", s, hT, xT, CH, EPS_LN)
                for c in range(2):
                    after(dve, *norm("ln1", s, "out", c + 1))
                    link(V.tensor_tensor(hT[:, :, cols(s, c)], hT[:, :, cols(s, c)], xT[:, :, cols(s, c)], ALU.add))
                norm_dve("rms1", s, xT, yT, CH, EPS_RMS, gain="g1")

            def att1_output(s):
                for c in range(2):
                    for m in range(2):
                        pb = ps[:, Y4[2 * c + m], 0:CH]
                        dve.wait_ge(sem("mo_ready"), 4 * s + 2 * c + m + 1)
                        V.tensor_tensor(hT[:, m, cols(s, c)], hT[:, m, cols(s, c)], pb, ALU.add)
                        V.tensor_tensor(xT[:, m, cols(s, c)], xT[:, m, cols(s, c)], pb,
                                        ALU.add).then_inc(sem("mo_used"), 1)
                norm_dve("rms2", s, xT, yT, CH, EPS_RMS, gain="g2")

            def router(s):
                rw = small[:, 0:40]
                rw3 = rw.rearrange("p (t e) -> p t e", t=5)
                w3 = small[:, 40:80].rearrange("p (t e) -> p t e", t=5)
                top, inv = small[:, 144:149], small[:, 153:158]
                cmpA = prods[0][:, 0:320].rearrange("p (t e j) -> p t e j", t=5, e=8)
                cmpB = prods[0][:, 320:640].rearrange("p (t e j) -> p t e j", t=5, e=8)
                rank = prods[0][:, 640:680].rearrange("p (t e) -> p t e", t=5)
                s58, s588 = [P, 5, 8], [P, 5, 8, 8]
                link(V.memset(small[:, 0:160], 0.0))
                dve.wait_ge(sem("logits_ready"), s + 1)
                V.tensor_copy(small[0:32, 0:40], ps[0:32, Y4[0], 0:40])
                V.tensor_copy(small[32:64, 0:32], ps[32:64, Y4[0], 0:32])
                link(V.tensor_copy(small[64:128, 0:32], ps[64:128, Y4[0], 0:32]))
                link(V.tensor_tensor(rw3, rw3, ebias[:, :].unsqueeze(1).to_broadcast(s58), ALU.add))
                link(V.tensor_reduce(top, rw3, AX.X, ALU.max))
                V.tensor_tensor(rw3, rw3, top.unsqueeze(2).to_broadcast(s58), ALU.subtract).then_inc(sem("lg_max"), 1)
                dve.wait_ge(sem("lg_exp"), s + 1)
                link(V.tensor_reduce(top, rw3, AX.X, ALU.add))
                link(V.reciprocal(inv, top))
                link(V.tensor_tensor(rw3, rw3, inv.unsqueeze(2).to_broadcast(s58), ALU.mult))
                V.tensor_tensor(cmpA, rw3.unsqueeze(2).to_broadcast(s588), rw3.unsqueeze(3).to_broadcast(s588),
                                ALU.is_gt)
                link(V.tensor_tensor(cmpB, rw3.unsqueeze(2).to_broadcast(s588), rw3.unsqueeze(3).to_broadcast(s588),
                                     ALU.is_equal))
                low = lower[:, :].rearrange("p (e j) -> p e j", e=8).unsqueeze(1).to_broadcast(s588)
                link(V.tensor_tensor(cmpB, cmpB, low, ALU.mult))
                link(V.tensor_tensor(cmpA, cmpA, cmpB, ALU.add))
                link(V.tensor_reduce(rank, cmpA, AX.X, ALU.add))
                link(V.tensor_scalar(rank, rank, 2.0, None, ALU.is_lt))
                link(V.tensor_reduce(top, rw3, AX.X, ALU.max))
                V.tensor_tensor(w3, rw3, top.unsqueeze(2).to_broadcast(s58), ALU.subtract).then_inc(sem("rw_max"), 1)
                dve.wait_ge(sem("rw_exp"), s + 1)
                link(V.tensor_tensor(w3, w3, rank, ALU.mult))
                link(V.tensor_reduce(top, w3, AX.X, ALU.add))
                link(V.reciprocal(inv, top))
                V.tensor_tensor(rw3, w3, inv.unsqueeze(2).to_broadcast(s58), ALU.mult).then_inc(sem("combine_done"), 1)
                dve.wait_ge(sem("combine_done"), s + 1)

            def experts(s, c, between):
                base = 36 * s + 18 * c
                for n in range(18):
                    e = n // 2
                    up = ps[:, 3 + 2 * (n % 2), 0:CH]
                    dve.wait_ge(sem("esil_ready"), base + n + 1)
                    after(dve, "edown", base + n - 2)
                    if e < NEXP:
                        link(V.tensor_tensor(emul[n % 2], esil[n % 2], up, ALU.mult))
                        V.tensor_tensor(eh[n % 3], emul[n % 2], ps[:, 6 + e % 2, 0:CH],
                                        ALU.mult).then_inc(sem("eh_ready"), 1)
                    else:
                        V.tensor_tensor(eh[n % 3], esil[n % 2], up, ALU.mult).then_inc(sem("eh_ready"), 1)
                    between(n)
                dve.wait_ge(sem("edown"), base + 18)
                for m in range(2):
                    y = hT[:, m, cols(s, c)]
                    V.tensor_tensor(y, y, ps[:, m, 0:CH], ALU.add).then_inc(sem("moe_used"), 1)

            def att2_out(s):
                q = qkv(s, 192)
                y4 = q[:, :, 0:64].rearrange("p t (h d) -> p t h d", h=2)
                shape = [P, T, 2, 32]
                gm = S[:, 100:134].rearrange("p (t h) -> p t h", t=T)
                gv = S[:, 0:34].rearrange("p (t h) -> p t h", t=T)
                p4 = prods[0].rearrange("p (t h d) -> p t h d", t=T, h=2)
                link(V.tensor_reduce(gm, y4, AX.X, ALU.add))
                link(V.tensor_scalar(gm, gm, 1.0 / 32, None, ALU.mult))
                link(V.tensor_tensor(y4, y4, gm.unsqueeze(3).to_broadcast(shape), ALU.subtract))
                link(V.tensor_tensor(p4, y4, y4, ALU.mult))
                link(V.tensor_reduce(gv, p4, AX.X, ALU.add))
                V.tensor_scalar(S[:, 0:34], S[:, 0:34], 1.0 / 32, EPS_LN, ALU.mult, ALU.add).then_inc(sem("gn_var"), 1)
                dve.wait_ge(sem("gn_rstd"), s + 1)
                V.tensor_tensor(y4, y4, gv.unsqueeze(3).to_broadcast(shape), ALU.mult).then_inc(sem("att2_done"), 1)
                dve.wait_ge(sem("att2_done"), s + 1)

            def att2_gated(s):
                for c in range(2):
                    dve.wait_ge(sem("att2_used"), 3 * s + min(3, ((c + 1) * CH - 1) // 256 + 1))
                    dve.wait_ge(sem("g_used"), 4 * s + 4)
                    for m in range(2):
                        y = oT[:, m, cols(s, c)]
                        last = V.tensor_scalar(y, y, v("gn_weight", m), v("gn_bias", m), ALU.mult, ALU.add)
                    link(last)
                    V.tensor_tensor(oT[:, :, cols(s, c)], oT[:, :, cols(s, c)], yT[:, :, cols(s, c)],
                                    ALU.mult).then_inc(sem("att2_gated"), 1)

            def ternary_mean():
                dve.wait_ge(sem("w_f_in"), 32)
                for w in range(2):
                    last = V.tensor_reduce(gam[:, w:w + 1], exp_flat[:, 2048 * w:2048 * (w + 1)], AX.X, ALU.add,
                                           apply_absolute_value=True)
                last.then_inc(sem("gam_sum"), 1)

            def ternary_weights():
                dve.wait_ge(sem("gam_ready"), 1)
                V.tensor_scalar(gam[:, 2:4], ps[:, Y4[3], 0:2], 1.0 / 1024, EPS_LN, ALU.mult,
                                ALU.add).then_inc(sem("gam_used"), 1)
                dve.wait_ge(sem("gam_used"), 1)
                link(V.tensor_scalar(gam[:, 4:6], gam[:, 2:4], 0.5, None, ALU.mult))
                link(V.tensor_scalar(gam[:, 6:8], gam[:, 2:4], -0.5, None, ALU.mult))
                for w in range(2):
                    raw, t_ = exp_flat[:, 2048 * w:2048 * (w + 1)], tern[:, 2048 * w:2048 * (w + 1)]
                    link(V.tensor_scalar(t_, raw, gam[:, 6 + w:7 + w], None, ALU.is_lt))
                    last = V.scalar_tensor_tensor(out=t_, in0=raw, scalar=gam[:, 4 + w:5 + w], in1=t_,
                                                  op0=ALU.is_gt, op1=ALU.subtract)
                last.then_inc(sem("tern_done"), 1)

            def final(s, c, m):
                y = hT[:, m, cols(s, c)]
                dve.wait_ge(sem("fc2_ready"), 4 * s + 2 * c + m + 1)
                V.scalar_tensor_tensor(out=y, in0=ps[:, X4[2 * c + m], 0:CH], scalar=v("b2", m), in1=y,
                                       op0=ALU.add, op1=ALU.add).then_inc(sem("final"), 1)

            for i in range(4):
                window_sums(i)
                window_attention(i)
            window_sums(4)
            local_out(0)
            norm_dve("lnga", 0, yT, xT, LC, EPS_LN, drained=[("proj_ready", 4)])
            class_query()
            global_attention(0)
            window_attention(4)
            window_sums(5)
            class_token(0)
            norm_dve("ln0", 0, hT, xT, CH, EPS_LN, drained=[("gkv_ready", 8)])
            att = att0_scores(0)
            run(att, 2 + CUT_SCORES)
            window_attention(5)
            window_sums(6)
            run(att)
            softmax_shift("att0", 4)
            window_attention(6)
            window_sums(7)
            softmax_scale("att0", 0, 4)
            att = att0_weigh(0)
            run(att, CUT_WEIGH)
            window_attention(7)
            run(att)
            done("att0")
            local_out(1)
            att0_gated(0)
            norm_dve("lnga", 1, yT, xT, LC, EPS_LN, drained=[("proj_ready", 8)])
            att0_output(0)
            global_attention(1)
            mqa_softmax(0)
            class_token(1)
            norm_dve("ln0", 1, hT, xT, CH, EPS_LN, drained=[("gkv_ready", 16)])
            att1_output(0)
            router(0)
            att = att0_scores(1)
            att_w = att0_weigh(1)
            experts(0, 0, lambda n: run(att, 1 if n < 17 else None))
            softmax_shift("att0", 4)
            experts(0, 1, lambda n: softmax_scale("att0", 1, 4) if n == 0 else run(att_w, 1))
            run(att_w)
            done("att0")
            norm_dve("ln2", 0, hT, xT, CH, EPS_LN)
            att0_gated(1)
            att0_output(1)
            mqa_softmax(1)
            att1_output(1)
            router(1)
            att = att2_scores(0)
            experts(1, 0, lambda n: run(att, 2))
            run(att)
            att_w = att2_weigh(0)
            experts(1, 1, lambda n: run(att_w, 1))
            run(att_w)
            att2_out(0)
            norm_dve("ln2", 1, hT, xT, CH, EPS_LN)
            ternary_mean()
            att2_gated(0)
            ternary_weights()
            add_to_h("l1o", 0, Y4)
            norm_dve("ln3", 0, hT, xT, CH, EPS_LN)
            run(att2_scores(1))
            att_w = att2_weigh(1)
            run(att_w, 8)
            final(0, 0, 0)
            final(0, 0, 1)
            run(att_w)
            final(0, 1, 0)
            final(0, 1, 1)
            att2_out(1)
            att2_gated(1)
            add_to_h("l1o", 1, Y4)
            norm_dve("ln3", 1, hT, xT, CH, EPS_LN)
            for c in range(2):
                for m in range(2):
                    final(1, c, m)


def fold(w):
    k = w.shape[0] // P
    return w.reshape(k, P, -1).transpose(1, 0, 2).reshape(P, -1)


def pair_order(w, heads, d):
    return w.reshape(w.shape[0], heads, d // 2, 2).transpose(0, 1, 3, 2).reshape(w.shape[0], heads * d)


def by_quarter(*ws):
    return np.concatenate([w.reshape(w.shape[0], 4, -1) for w in ws], axis=2)


def shape_tables():
    f = np.float32
    pos = np.arange(T, dtype=f)
    inv = (1.0 / np.power(f(2500), np.arange(0, 16, 2, dtype=f) / f(16))).astype(f)
    emb = np.outer(pos, inv).astype(f)
    emb = np.concatenate([emb, emb], -1)
    cs, sn = np.cos(emb)[:, ::2].astype(f), np.sin(emb)[:, ::2].astype(f)
    rope = np.stack([np.concatenate([cs, cs], -1), np.concatenate([-sn, sn], -1)])
    base = ((np.arange(0, 32, 2, dtype=f) + f(0.4 * 32)) / f(1.4 * 32)).astype(f)
    scale = np.power(base[None, :], pos[:, None] / f(512.0)).astype(f)
    ang = (pos[:, None] * (1.0 / np.power(f(10000.0), np.arange(16, dtype=f) / f(16)))[None, :]).astype(f)
    tabs = []
    for s in (scale, (1.0 / scale).astype(f)):
        c_, s_ = np.cos(ang) * s, np.sin(ang) * s
        tabs += [np.concatenate([c_, c_], -1), np.concatenate([-s_, s_], -1)]
    gammas = 1.0 - np.exp(np.linspace(np.log(1 / 32.0), np.log(1 / 512.0), 8)).astype(f)
    expo = (np.arange(T)[:, None] - np.arange(T)[None, :]).astype(f)
    d = np.where(expo[None] >= 0, np.exp(expo[None] * np.log(gammas)[:, None, None]), 0.0)
    decay = d.reshape(4, 2, T, T).transpose(0, 2, 3, 1).reshape(4, 1, T * T * 2)
    sel = np.repeat(np.eye(NEXP), P, axis=1)
    lower = (np.arange(8)[None, :] < np.arange(8)[:, None]).astype(f).reshape(1, 64)
    return {k: np.ascontiguousarray(x, dtype=f) for k, x in dict(
        rope=rope.reshape(1, -1), xpos=np.stack(tabs).reshape(1, -1), decay=decay, sel=sel, lower=lower,
        ident=np.eye(P)).items()}


def lay_out(i):
    g = {k: np.asarray(x) for k, x in i.items()}
    t = lambda n: g["L0_tok_" + n]
    at = lambda n: g["L0_attn_" + n].T
    ff = lambda n: g["L0_ffn_" + n]
    l1 = lambda n: g["L1_attn_" + n]
    x = g["x"].reshape(2, HB, 3, 4, 3, 14, 4, 3, 14).transpose(0, 3, 2, 5, 8, 4, 7, 6, 1)
    x = x.reshape(ITERS, PATCH_K, NCG, CONV_N).transpose(0, 2, 1, 3).reshape(ITERS * NCG, PATCH_K, CONV_N)
    wc = t("conv_w").reshape(C, PATCH_K).T
    a = {
        "x_main": x[:, 0:512].reshape(ITERS * NCG, 4, P, CONV_N).transpose(0, 2, 1, 3),
        "x_rest": x[:, 512:],
        "w_conv": wc[0:512].reshape(4, P, C).transpose(1, 0, 2),
        "w_convr": wc[512:],
        "la_wkv": t("la_wkv").reshape(2, P, 512).transpose(1, 0, 2),
        "la_wq": t("la_wq").reshape(2, P, C).transpose(1, 0, 2),
        "la_proj_w": fold(t("la_proj_w")), "mod_w": fold(t("mod_w")),
        "ga_wkv": fold(by_quarter(t("ga_wkv")[:, 0:C], t("ga_wkv")[:, C:]).reshape(C, -1)),
        "ga_wq": fold(t("ga_wq")), "ga_proj_w": fold(t("ga_proj_w")),
        "attn_qkvg": fold(by_quarter(pair_order(at("W_q"), 16, 16), pair_order(at("W_k"), 16, 16),
                                  at("W_v"), at("W_gv")).reshape(C, -1)),
        "attn_go": fold(at("W_go")), "attn_o": fold(at("W_o")),
        "ffn_o": fold(ff("Wo").T), "ffn_r": fold(ff("Wr").T), "ebias": ff("expert_bias").reshape(1, NEXP),
        "l1_g": fold(l1("W_G")), "l1_o": fold(l1("W_O")),
        "w1": fold(g["L1_ffn_W1"].T).reshape(P, 2, 1024), "w2": fold(g["L1_ffn_W2"].T).reshape(P, 8, C),
    }
    kc, vc = ff("Wkc").T, ff("Wvc").T
    a["ffn_qkv"] = fold(np.concatenate([ff("Wq").T, kc, kc, vc], 1))
    heads = lambda n: l1(n).transpose(1, 0, 2).reshape(C, C)
    a["l1_qkv"] = fold(by_quarter(pair_order(heads("W_Q"), 8, 32), pair_order(heads("W_K"), 8, 32),
                               heads("W_V")).reshape(C, -1))
    ex = [np.stack([fold(w.T) for w in (ff("eW1")[e], ff("eW3")[e], ff("eW2")[e])], 1) for e in range(NEXP)]
    ex.append(np.stack([fold(w.T) for w in (ff("sW1"), ff("sW3"), ff("sW2"))], 1))
    a["experts"] = np.stack(ex, 1).reshape(P, 9, 3, 2, C)
    src = {"class_emb": t("class_emb"), "g1": ff("g1"), "g2": ff("g2"), "gn_weight": l1("gn_weight"),
           "gn_bias": l1("gn_bias"), "b1": g["L1_ffn_b1"], "b2": g["L1_ffn_b2"]}
    a["vec"] = np.concatenate([(src[n] if n in src else t(n)).reshape(k, P).T for n, k in VEC], axis=1)
    return {k: np.ascontiguousarray(x) for k, x in a.items()}


def kernel(**inputs):
    import concourse.bacc as _bacc
    from concourse.bass_utils import run_bass_kernel_spmd as _run

    nc = _bacc.Bacc("TRN2", target_bir_lowering=False, num_devices=1)
    arrays = {**lay_out(inputs), **shape_tables()}
    aps = {n: nc.dram_tensor(n + "_dram", x.shape, F32, kind="ExternalInput").ap() for n, x in arrays.items()}
    out = nc.dram_tensor("out_dram", (P, 2, NT), F32, kind="ExternalOutput").ap()
    build(nc, aps, out)
    r = _run(nc, [{n + "_dram": x for n, x in arrays.items()}], core_ids=[0])
    got = r.results[0]["out_dram"]
    return np.ascontiguousarray(got.reshape(P, 2, 2, T, HB).transpose(2, 4, 3, 1, 0).reshape(B, T, C))
```

```python
from contextlib import ExitStack

import numpy as np
import concourse.bass as bass
from concourse import mybir

F32 = mybir.dt.float32
ALU = mybir.AluOpType
ACT = mybir.ActivationFunctionType
AX = mybir.AxisListType

P = 128
B = 64
HB = B // 2
T = 17
HW = 16
C = 256
PATCH_K = 588
K_REST = PATCH_K - 4 * P
NJ = 9
ITERS = 8
XC = NJ * P
CONV_N = 384
NCG = XC // CONV_N
XRING = 4
NT = B * T
NH = HB * T
NWH = HB * HW
CH = NH // 2
LC = NWH // 2
QC = C // 4
FIXED = T * 256 + T * T * 4 + NJ * C + 2 * T * 16
LATER = 24900
NEXP = 8
KVN = C + 1
KVS = KVN + 1
EPS_LN = 1e-5
EPS_RMS = 1e-6
MASKED = -1e30

VEC = [("la_ln_q_g", 2), ("la_ln_q_b", 2), ("la_ln_kv_g", 2), ("la_ln_kv_b", 2), ("la_proj_b", 2),
       ("ga_ln_q_g", 2), ("ga_ln_q_b", 2), ("ga_ln_kv_g", 2), ("ga_ln_kv_b", 2), ("ga_proj_b", 2),
       ("mod_b", 2), ("class_emb", 2), ("g1", 2), ("g2", 2), ("gn_weight", 2), ("gn_bias", 2),
       ("b1", 8), ("b2", 2)]
VCOL = {}
_n = 0
for _name, _k in VEC:
    VCOL[_name] = _n
    _n += _k
NVEC = _n


CUT_RETENTION = ((8,), (9,))
GROUPS = ((0, 8), (8, 9), (9, T))
CUT_SCORES, CUT_WEIGH = (11, 13), (8,)
CAUSAL = [t + 1 for t in range(T)]


def build(nc, a, out):
    ctx = ExitStack()
    with ctx:
        def sb(name, shape):
            return ctx.enter_context(nc.sbuf_tensor(name, shape, F32))

        sems = {}

        def sem(name):
            if name not in sems:
                sems[name] = ctx.enter_context(nc.semaphore(name))
            return sems[name]

        ps = ctx.enter_context(nc.psum_tensor("ps", [P, 8, 512], F32))

        hT, xT, yT, oT = (sb(n, [P, 2, NT]) for n in ("hT", "xT", "yT", "oT"))
        sqb = sb("sqb", [P, 2, 2, CH])
        lnv = sb("lnv", [P, 2, CH])
        vec = sb("vec", [P, NVEC])
        ident = sb("ident", [P, P])
        avg = sb("avg", [P, P])
        small = sb("small", [P, 512])
        ebias = sb("ebias", [P, NEXP])
        lower = sb("lower", [P, NEXP * NEXP])
        wtok = sb("wtok", [P, 6 * 512])
        wattn = sb("wattn", [P, 6 * 512])

        def v(name, i=0):
            return vec[:, VCOL[name] + i:VCOL[name] + i + 1]

        def w2(ap):
            return ap.rearrange("p (k n) -> p k n", k=2)

        def wq4(ap):
            return ap.rearrange("p (k q n) -> p k q n", k=2, q=4)

        w_proj, w_mod = w2(wtok[:, 0:512]), w2(wtok[:, 512:1024])
        w_gkv, w_gq, w_gproj = wq4(wtok[:, 1024:2048]), wq4(wtok[:, 2048:2560]), w2(wtok[:, 2560:3072])
        w_l1qkv, w_l1g, w_l1o = wq4(wtok[:, 0:1536]), w2(wtok[:, 1536:2048]), w2(wtok[:, 2048:2560])
        w_qkvg, w_go, w_o = wq4(wattn[:, 0:2048]), w2(wattn[:, 2048:2560]), w2(wattn[:, 2560:3072])

        ARENA = FIXED + LATER
        arena = sb("arena", [P, ARENA])
        at = [0]

        def take(n):
            at[0] += n
            assert at[0] <= ARENA, at[0]
            return arena[:, at[0] - n:at[0]]

        qkv_of = [take(T * 256), None]
        S = take(T * T * 4)
        prodW = take(NJ * C)
        prods = [prodW[:, 0:T * QC], prodW[:, T * QC:2 * T * QC]]
        rope = take(2 * T * 16).rearrange("p (f t d) -> p f t d", f=2, t=T)
        assert at[0] == FIXED, at[0]
        x_main = [take(4 * CONV_N).rearrange("p (k n) -> p k n", k=4) for _ in range(XRING)]
        x_rest = [take(CONV_N) for _ in range(XRING)]
        w_conv = take(4 * C).rearrange("p (k n) -> p k n", k=4)
        w_convr = take(C)
        patch_emb = take(2 * XC).rearrange("p (m n) -> p m n", m=2)
        patch_sq = take(2 * XC).rearrange("p (m n) -> p m n", m=2)
        kv_flat = take(NJ * 2 * KVS)
        kv_raw = kv_flat.rearrange("p (j s n) -> p j s n", j=NJ, s=2)
        w_kv = kv_flat[:, 0:1024].rearrange("p (k n) -> p k n", k=2)
        w_lq = kv_flat[:, 1024:1536].rearrange("p (k n) -> p k n", k=2)
        bcol = kv_flat[:, 1536:1792].rearrange("p (k n) -> p k n", k=2)
        sq_sum = take(XC)
        red = take(C).rearrange("p (m n) -> p m n", m=2)
        red_sq = take(C).rearrange("p (m n) -> p m n", m=2)
        rsq_sum = take(P)
        w_kvc = take(2 * 2 * KVS).rearrange("p (k s n) -> p k s n", k=2, s=2)
        w_lqc = take(2 * KVS).rearrange("p (k n) -> p k n", k=2)
        q_win = take(C)
        qk_tmp = take(C)
        bias_row = take(3 * C)
        sc = take(NJ * 8)
        sm8 = take(8)
        qb8 = take(8)
        st10 = take(10)
        mean10 = take(10)
        aggW = take(4 * C).rearrange("p (i c) -> p i c", i=4)
        at[0] = FIXED
        exp_flat = take(9 * 3 * 512)
        w_exp = exp_flat.rearrange("p (e w k n) -> p e w k n", e=9, w=3, k=2)
        qkv_of[1] = take(T * 256)
        eh = [take(CH) for _ in range(3)]
        esil = [take(CH) for _ in range(2)]
        emul = [take(CH) for _ in range(2)]
        w_mqa_flat, w_mo_flat, w_r_flat = take(2 * (C + P + QC)), take(512), take(16)
        w_mqa, w_mo = w2(w_mqa_flat), w2(w_mo_flat)
        w_mq, w_mk, w_mv = w_mqa[:, :, 0:C], w_mqa[:, :, C:C + P], w_mqa[:, :, C + P:C + P + QC]
        w_r = w_r_flat.rearrange("p (k n) -> p k n", k=2)
        xpos_flat = take(4 * T * 32)
        xpos = xpos_flat.rearrange("p (f t d) -> p f t d", f=4, t=T)
        decay = take(T * T * 2)
        sel = sb("sel", [NEXP, NEXP * P])
        cmbT = sb("cmbT", [NEXP, NH])
        w_f1 = exp_flat[:, 0:2048].rearrange("p (k n) -> p k n", k=2)
        w_f2 = exp_flat[:, 2048:4096].rearrange("p (k n) -> p k n", k=8)
        tern = exp_flat[:, 4096:8192]
        w_t1 = tern[:, 0:2048].rearrange("p (k n) -> p k n", k=2)
        w_t2 = tern[:, 2048:4096].rearrange("p (k n) -> p k n", k=8)
        gs, gs_top, gs_inv = small[:, 340:372], small[:, 372:374], small[:, 374:376]
        gam = small[:, 400:410]
        hid = qkv_of[0][:, 0:16 * CH].rearrange("p (u k n) -> p u k n", u=2, k=8)

        class Mqa:
            def __init__(self, s):
                at_ = [0]

                def part(n):
                    at_[0] += n
                    return qkv_of[s][:, at_[0] - n:at_[0]]

                self.q = part(2 * NH).rearrange("p (m n) -> p m n", m=2)
                self.k = part(NH)
                self.v_flat = part(8 * QC)
                self.v = self.v_flat.rearrange("p (g d) -> p g d", g=8)
                self.p = part(HB * 32)
                self.p3 = self.p.rearrange("p (i k) -> p i k", k=32)
                self.pT = part(8 * P).rearrange("p (g n) -> p g n", g=8)
                self.top, self.inv = part(HB), part(HB)

        mqa_of = [Mqa(0), Mqa(1)]

        def qkv(s, n):
            return qkv_of[s][:, 0:T * n].rearrange("p (t n) -> p t n", t=T)

        X4 = [2, 3, 4, 5]
        Y4 = [6, 7, 0, 1]

        def cols(s, c, n=CH):
            return slice(s * NH + c * n, s * NH + (c + 1) * n)

        def after(eng, s, value):
            if value > 0:
                eng.wait_ge(sem(s), value)

        NORMS = [("lnga", 0), ("ln0", 0), ("lnga", 1), ("ln0", 1), ("ln1", 0), ("rms1", 0), ("rms2", 0),
                 ("ln2", 0), ("ln1", 1), ("rms1", 1), ("rms2", 1), ("ln2", 1), ("ln3", 0), ("ln3", 1)]
        NORM_BANKS = {"lnga": X4, "ln0": X4, "ln1": Y4, "rms1": None, "rms2": Y4, "ln2": X4, "ln3": X4}

        def norm(name, s, step, n):
            none = {"mu2": ("rms1", "rms2"), "sq": ("rms1",), "stat": ("rms1",)}.get(step, ())
            before = [x for x in NORMS[:NORMS.index((name, s))] if x[0] not in none]
            return "norm_" + step, 2 * len(before) + n

        def spot(name, s, c):
            return 2 * NORMS.index((name, s)) + c

        block = ctx.enter_context(nc.Block())

        @block.sync
        def _(sp):
            def load(dst, src, s):
                sp.dma_start(dst, src).then_inc(sem(s), 16)

            def load_x(g):
                load(x_main[g % XRING], a["x_main"][g], f"x_in{g % XRING}")
                load(x_rest[g % XRING][0:K_REST, :], a["x_rest"][g], f"x_in{g % XRING}")

            load(w_conv, a["w_conv"], "w_conv_in")
            load(w_convr[0:K_REST, :], a["w_convr"], "w_conv_in")
            load_x(0)
            load(vec[:, :], a["vec"], "w_first_in")
            load(ident[:, :], a["ident"], "w_first_in")
            load(w_kv, a["la_wkv"], "w_first_in")
            load(w_lq, a["la_wq"], "w_first_in")
            for g in range(1, XRING):
                load_x(g)
            load(wtok[:, 0:512], a["la_proj_w"], "w_tok_in")
            load(wtok[:, 512:1024], a["mod_w"], "w_tok_in")
            load(wtok[:, 1024:2048], a["ga_wkv"], "w_tok_in")
            load(wtok[:, 2048:2560], a["ga_wq"], "w_tok_in")
            load(wtok[:, 2560:3072], a["ga_proj_w"], "w_tok_in")
            load(wattn[:, 0:2048], a["attn_qkvg"], "w_attn_in")
            load(wattn[:, 2048:2560], a["attn_go"], "w_attn_in")
            load(wattn[:, 2560:3072], a["attn_o"], "w_attn_in")
            load(ebias[:, :], a["ebias"].partition_broadcast(P), "tab_in")
            load(lower[:, :], a["lower"].partition_broadcast(P), "tab_in")
            load(sel[:, :], a["sel"], "tab_in")
            load(rope, a["rope"].partition_broadcast(P), "tab_in")
            for g in range(XRING, ITERS * NCG):
                sp.wait_ge(sem("conv_evac"), 2 * (g - XRING) + 2)
                load_x(g)
            sp.wait_ge(sem("win_done"), ITERS)
            load(w_mqa_flat, a["ffn_qkv"], "w_ffn_in")
            load(w_mo_flat, a["ffn_o"], "w_ffn_in")
            load(w_r_flat, a["ffn_r"], "w_ffn_in")
            for e in range(9):
                load(w_exp[:, e], a["experts"][:, e], "w_exp_in")
            sp.wait_ge(sem("aggT_ready"), 4)
            load(xpos_flat, a["xpos"].partition_broadcast(P), "w_l1_in")
            for q in range(4):
                load(decay[32 * q:32 * q + 32, :], a["decay"][q].partition_broadcast(32), "w_l1_in")
            sp.wait_ge(sem("gproj_ready"), 4)
            load(wtok[:, 0:1536], a["l1_qkv"], "w_l1_in")
            load(wtok[:, 1536:2048], a["l1_g"], "w_l1_in")
            load(wtok[:, 2048:2560], a["l1_o"], "w_l1_in")
            sp.wait_ge(sem("edown"), 54 + 6)
            load(w_f1, a["w1"], "w_f_in")
            load(w_f2, a["w2"], "w_f_in")
            for s in range(2):
                for c in range(2):
                    sp.wait_ge(sem("final"), 4 * s + 2 * c + 2)
                    load(out[:, :, cols(s, c)], hT[:, :, cols(s, c)], "out_done")
            sp.wait_ge(sem("out_done"), 64)

        @block.tensor
        def _(pe):
            mm = nc.tensor.matmul

            def waits(pairs):
                for s, value in pairs:
                    after(pe, s, value)

            def weight_means():
                pe.wait_ge(sem("w_scaled"), 1)
                for k in range(2):
                    mm(ps[:, 2, :].rearrange("p (s n) -> p s n", s=2), avg[:, :], w_kvc[:, k, :, 0:C],
                       start=(k == 0), stop=(k == 1))
                for k in range(2):
                    last = mm(ps[:, 3, 0:C], avg[:, :], w_lqc[:, k, 0:C], start=(k == 0), stop=(k == 1))
                last.then_inc(sem("w_means"), 1)

            def kv_bias():
                pe.wait_ge(sem("kv_bcol"), 1)
                for k in range(2):
                    last = mm(ps[:, 4, :], bcol[:, k, :], w_kv[:, k, :], start=(k == 0), stop=(k == 1))
                last.then_inc(sem("kv_brow"), 1)

            def q_bias():
                pe.wait_ge(sem("q_bcol"), 1)
                for k in range(2):
                    last = mm(ps[:, 5, 0:C], bcol[:, k, :], w_lq[:, k, :], start=(k == 0), stop=(k == 1))
                last.then_inc(sem("q_brow"), 1)

            def conv(i, beside=None):
                for g in range(2 * NCG):
                    c, m = g // 2, g % 2
                    r = (NCG * i + c) % XRING
                    if m == 0:
                        pe.wait_ge(sem(f"x_in{r}"), 32 * ((NCG * i + c) // XRING + 1))
                    after(pe, "conv_evac", 6 * i + g - 1)
                    for kk in range(4):
                        mm(ps[:, g % 2, 0:CONV_N], w_conv[:, kk, m * P:(m + 1) * P],
                           x_main[r][:, kk, :], start=(kk == 0), stop=False)
                    mm(ps[:, g % 2, 0:CONV_N], w_convr[0:K_REST, m * P:(m + 1) * P],
                       x_rest[r][0:K_REST, :], start=False, stop=True).then_inc(sem("conv_ready"), 1)
                    if beside and g in beside:
                        beside[g]()

            def window_kv(i, drained=()):
                waits(drained)
                for j in range(NJ):
                    if j % 3 == 0:
                        pe.wait_ge(sem("conv_evac"), 6 * i + 2 * (j // 3) + 2)
                    b = 2 + 2 * (j % 2)
                    after(pe, "kv_evac", 9 * i + j - 1)
                    for s in range(2):
                        for kk in range(2):
                            last = mm(ps[:, b + s, 0:KVN], patch_emb[:, kk, j * P:(j + 1) * P],
                                      w_kvc[:, kk, s, 0:KVN], start=(kk == 0), stop=(kk == 1))
                    last.then_inc(sem("kv_ready"), 1)
                pe.wait_ge(sem("sums_ready"), i + 1)
                after(pe, "win_done", i - 1)
                st = ps[:, 6 + i % 2, :]
                for j in range(NJ):
                    mm(st[:, 300 + j:301 + j], sq_sum[:, j * P:(j + 1) * P], avg[:, 0:1], start=True, stop=True)
                mm(st[:, 309:310], rsq_sum, avg[:, 0:1], start=True, stop=True)
                for kk in range(2):
                    last = mm(st[:, 0:KVN], red[:, kk, :], w_lqc[:, kk, 0:KVN], start=(kk == 0), stop=(kk == 1))
                last.then_inc(sem("stat_ready"), 1)

            def agg_transposes(s):
                pe.wait_ge(sem("kv_evac"), NJ * 4 * (s + 1))
                for g in range(2):
                    pe.wait_ge(sem("win_done"), 4 * s + 2 * g + 2)
                    for i in range(2):
                        for m in range(2):
                            last = nc.tensor.transpose(ps[:, X4[g], (2 * i + m) * P:(2 * i + m + 1) * P],
                                                       aggW[:, 2 * g + i, m * P:(m + 1) * P], ident[:, :])
                    last.then_inc(sem("aggT_ready"), 1)

            def linear(name, s, w, src, n, banks, src_ready, drained=(), chunks=(0, 1)):
                waits(drained)
                for c in chunks:
                    waits(src_ready(c))
                    for m in range(2):
                        for k in range(2):
                            last = mm(ps[:, banks[2 * c + m], 0:n], w[:, k, m * P:(m + 1) * P],
                                      src[:, k, cols(s, c, n)], start=(k == 0), stop=(k == 1))
                        last.then_inc(sem(name + "_ready"), 1)

            def norm_stats(name, s, src, n, src_ready, drained=(), chunks=(0, 1)):
                banks = NORM_BANKS[name]
                waits(drained)
                for c in chunks:
                    waits(src_ready(c))
                    if not name.startswith("rms"):
                        for k in range(2):
                            mm(ps[:, banks[2 * c], 0:n], avg[:, :], src[:, k, cols(s, c, n)],
                               start=(k == 0), stop=(k == 1))
                    after(pe, *norm(name, s, "sq", c + 1))
                    for k in range(2):
                        last = mm(ps[:, banks[2 * c + 1], 0:n], avg[:, :], sqb[:, spot(name, s, c) % 2, k, 0:n],
                                  start=(k == 0), stop=(k == 1))
                    last.then_inc(sem("norm_stat"), 1)

            def to_images(name, s, w, src, n, nt, banks, src_ready, drained=()):
                groups = (nt + 1) // 2
                waits(drained)
                for g in range(groups):
                    if g >= 4:
                        after(pe, name + "_used", groups * s + g - 3)
                    for t in range(2 * g, min(2 * g + 2, nt)):
                        waits(src_ready(t))
                        for k in range(2):
                            for q in range(4):
                                last = mm(ps[32 * q:32 * q + 32, banks[g % 4], (t % 2) * n:(t % 2 + 1) * n],
                                          src[:, k, s * NH + t * HB:s * NH + (t + 1) * HB], w[:, k, q, :],
                                          start=(k == 0), stop=(k == 1), skip_group_check=True)
                    last.then_inc(sem(name + "_ready"), 1)

            spread = ident[:, :].rearrange("p (m r b) -> p r m b", m=2, r=2)

            def to_channels(name, s, src, groups, banks, ready, drained=()):
                waits(drained)
                waits(ready)
                for g, (t0, t1) in groups:
                    for t in range(t0, t1):
                        for r in range(2):
                            last = mm(ps[64 * r:64 * r + 64, banks[g], (t - t0) * QC:(t - t0 + 1) * QC]
                                      .rearrange("p (m b) -> p m b", m=2),
                                      src[:, t, 0:QC], spread[:, r], start=True, stop=True, skip_group_check=True)
                    last.then_inc(sem(name + "_ready"), 1)

            groups = list(enumerate(GROUPS))

            def token_ready(name, s, n=CH):
                return lambda t: [norm(name, s, "out", min(2, ((t + 1) * HB - 1) // n + 1))]

            def local_output(s):
                agg_transposes(s)
                linear("proj", s, w_proj, xT, LC, X4, lambda c: [("aggT_used", 2 * s + c + 1)],
                       [("w_tok_in", 80), ("aggT_used", 2 * s + 2)])

            def patch_output(s):
                linear("mod", s, w_mod, yT, LC, X4, lambda c: [("local_out", 4 * s + 2 * c + 2)],
                       [("local_out", 4 * s + 4)])

            def lnga_stats(s):
                norm_stats("lnga", s, yT, LC, lambda c: [], [("h_tok", 4 * s + 4), ("kv_evac", NJ * (5 + 3 * s))])

            def class_stats():
                pe.wait_ge(sem("cls_cols"), 1)
                for k in range(2):
                    last = mm(ps[:, 2, 0:2], avg[:, :], small[:, 2 * k:2 * k + 2], start=(k == 0), stop=(k == 1))
                last.then_inc(sem("cls_stat"), 1)

            def class_query():
                pe.wait_ge(sem("cls_bcast"), 1)
                pe.wait_ge(sem("w_tok_in"), 80)
                for q in range(4):
                    for k in range(2):
                        last = mm(ps[32 * q:32 * q + 32, 3, 0:QC], small[:, 16 + 64 * k:16 + 64 * k + 32],
                                  w_gq[:, k, q, :], start=(k == 0), stop=(k == 1))
                last.then_inc(sem("gq_ready"), 1)

            def global_kv(s):
                to_images("gkv", s, w_gkv, xT, 128, HW, X4, lambda t: [("lnga_aff", 2 * s + t // 8 + 1)],
                          [norm("lnga", s, "out", 2)])

            def class_output(s):
                to_channels("gagg", s, small[:, 272:336].unsqueeze(1), [(0, (0, 1))], X4,
                            [("gatt_done", s + 1)], [("gkv_used", 8 * s + 8), ("kv_evac", NJ * 6)])
                pe.wait_ge(sem("gagg_used"), s + 1)
                for m in range(2):
                    for k in range(2):
                        last = mm(ps[:, 3 + m, 0:HB], w_gproj[:, k, m * P:(m + 1) * P],
                                  oT[:, k, s * NH:s * NH + HB], start=(k == 0), stop=(k == 1))
                    last.then_inc(sem("gproj_ready"), 1)

            def ln0_stats(s):
                norm_stats("ln0", s, hT, CH, lambda c: [], [("h_tok", 4 * s + 4), ("h_cls", 2 * s + 2)])

            def att0_qkv(s):
                to_images("qkv0", s, w_qkvg, xT, 256, T, X4, token_ready("ln0", s),
                          [("w_attn_in", 48), norm("ln0", s, "out", 2)])

            def att0_gate(s):
                linear("go", s, w_go, xT, CH, X4, lambda c: [], [("qkv0_used", 9 * s + 9)])

            def of_tokens(ap, i):
                return ap.rearrange("p (t b) -> p b t", b=HB)[:, i, :]

            def att0_channels(s):
                to_channels("att0", s, qkv(s, 256), groups, Y4, [("att0_done", s + 1)],
                            [("win_done", ITERS), ("moe_used", 4 * s)])

            def att0_output(s):
                linear("wo", s, w_o, oT, CH, Y4, lambda c: [("att0_gated", 2 * s + c + 1)], [("att0_used", 3 * s + 3)])
                norm_stats("ln1", s, hT, CH, lambda c: [("wo_used", 4 * s + 2 * c + 2)], [("wo_used", 4 * s + 4)])

            def mqa_scores(s):
                t_ = mqa_of[s]
                linear("mq", s, w_mq, yT, CH, Y4, lambda c: [norm("rms1", s, "out", c + 1)],
                       [norm("ln1", s, "out", 2), ("w_ffn_in", 48)])
                pe.wait_ge(sem("mq_used"), 4 * s + 3)
                for c in range(2):
                    for k in range(2):
                        last = mm(ps[:, Y4[c], 0:CH], w_mk[:, k, :], yT[:, k, cols(s, c)],
                                  start=(k == 0), stop=(k == 1))
                    last.then_inc(sem("mk_ready"), 1)
                for g in range(8):
                    for k in range(2):
                        for j in range(4):
                            last = mm(ps[32 * j:32 * j + T, Y4[2], g * QC:(g + 1) * QC],
                                      of_tokens(yT[:, k, s * NH:(s + 1) * NH], 4 * g + j), w_mv[:, k, :],
                                      start=(k == 0), stop=(k == 1), skip_group_check=True)
                last.then_inc(sem("mv_ready"), 1)
                pe.wait_ge(sem("mk_used"), 2 * s + 2)
                for i in range(HB):
                    for h in range(4):
                        r = 64 * (h % 2)
                        last = mm(ps[32 * h:32 * h + T, Y4[i // 16], (i % 16) * T:(i % 16 + 1) * T],
                                  of_tokens(t_.q[r:r + 64, h // 2, :], i), of_tokens(t_.k[r:r + 64, :], i),
                                  start=True, stop=True, skip_group_check=True)
                    if i % 16 == 15:
                        last.then_inc(sem("msc_ready"), 1)

            def mqa_weigh(s):
                t_ = mqa_of[s]
                pe.wait_ge(sem("mq_used"), 4 * s + 4)
                pe.wait_ge(sem("mv_used"), s + 1)
                pe.wait_ge(sem("msc_done"), s + 1)
                for g in range(8):
                    last = nc.tensor.transpose(ps[:, Y4[2 + g // 4], (g % 4) * P:(g % 4 + 1) * P],
                                               t_.p[:, g * P:(g + 1) * P], ident[:, :])
                    if g % 4 == 3:
                        last.then_inc(sem("mpT_ready"), 1)
                pe.wait_ge(sem("mpT_used"), 2 * s + 2)
                for g in range(8):
                    for j in range(4):
                        w_ = t_.pT[32 * j:32 * j + T, g, :].rearrange("p (m r t) -> p r m t", m=2, r=2)
                        for r in range(2):
                            last = mm(ps[64 * r:64 * r + 64, Y4[j], 2 * T * g:2 * T * (g + 1)]
                                      .rearrange("p (m t) -> p m t", m=2),
                                      t_.v[32 * j:32 * j + T, g, :], w_[:, r, :, 0:T],
                                      start=True, stop=True, skip_group_check=True)
                        if g == 7:
                            last.then_inc(sem("att1_ready"), 1)

            def att1_output(s):
                linear("mo", s, w_mo, oT, CH, Y4, lambda c: [("att1_used", 4 * s + 4)])
                norm_stats("rms2", s, xT, CH, lambda c: [("mo_used", 4 * s + 2 * c + 2)], [("mo_used", 4 * s + 4)])

            def router(s):
                after(pe, *norm("rms2", s, "out", 2))
                for t in range(5):
                    n = min(P, NH - t * P)
                    for k in range(2):
                        c0 = s * NH + t * P
                        last = mm(ps[0:n, Y4[0], t * NEXP:(t + 1) * NEXP], yT[:, k, c0:c0 + n], w_r[:, k, :],
                                  start=(k == 0), stop=(k == 1))
                last.then_inc(sem("logits_ready"), 1)

            def combine(s):
                pe.wait_ge(sem("combine_done"), s + 1)
                cw = small[:, 0:40].rearrange("p (t e) -> p t e", t=5)
                for t in range(5):
                    n = min(P, NH - t * P)
                    last = nc.tensor.transpose(ps[0:NEXP, Y4[1 + t // 4], (t % 4) * P:(t % 4) * P + n],
                                               cw[0:n, t, :], ident[0:n, 0:n])
                last.then_inc(sem("cmb_ready"), 1)
                pe.wait_ge(sem("cmb_used"), s + 1)

            def gate_and_up(s, c, n):
                for w in range(2):
                    for k in range(2):
                        last = mm(ps[:, 2 + 2 * (n % 2) + w, 0:CH],
                                  w_exp[:, n // 2, w, k, (n % 2) * P:(n % 2 + 1) * P],
                                  yT[:, k, cols(s, c)], start=(k == 0), stop=(k == 1))
                return last

            def spread_weight(e, c):
                return mm(ps[:, 6 + e % 2, 0:CH], sel[:, e * P:(e + 1) * P],
                          cmbT[:, c * CH:(c + 1) * CH], start=True, stop=True)

            def first_expert(s):
                pe.wait_ge(sem("w_exp_in"), 16 * 9)
                pe.wait_ge(sem("tab_in"), 64)
                waits([("go_used", 8), ("qkv2_used", 9 * s), ("g_used", 4 * s)])
                for n in range(2):
                    gate_and_up(s, 0, n)

            def experts(s, c):
                base = 36 * s + 18 * c
                after(pe, "moe_used", 4 * s + 2 * c)
                if c == 0:
                    spread_weight(0, c).then_inc(sem("eup_ready"), 2)
                for n in range(2 if c == 0 else 0, 18 + 2):
                    if n < 18:
                        e = n // 2
                        if n >= 2:
                            pe.wait_ge(sem("eh_ready"), base + n - 1)
                        if n % 2 == 0 and e < NEXP:
                            spread_weight(e, c)
                        gate_and_up(s, c, n).then_inc(sem("eup_ready"), 1)
                    if n >= 2:
                        d = n - 2
                        e, k = d // 2, d % 2
                        pe.wait_ge(sem("eh_ready"), base + d + 1)
                        for m in range(2):
                            last = mm(ps[:, m, 0:CH], w_exp[:, e, 2, k, m * P:(m + 1) * P], eh[d % 3],
                                      start=(d == 0), stop=(d == 17))
                        last.then_inc(sem("edown"), 1)

            def retention_stats(s):
                norm_stats("ln2", s, hT, CH, lambda c: [("moe_used", 4 * s + 2 * c + 2)])

            def retention_qkv(s):
                to_images("qkv2", s, w_l1qkv, xT, 192, T, X4, token_ready("ln2", s),
                          [("w_l1_in", 128), norm("ln2", s, "out", 2)])

            def retention_gate(s):
                linear("g", s, w_l1g, xT, CH, X4, lambda c: [], [("qkv2_used", 9 * s + 9)])

            def att2_channels(s, c):
                to_channels("att2", s, qkv(s, 192), groups[0:2] if c == 0 else groups[2:], Y4,
                            [("att2_done", 2 * s + c + 1)], [("moe_used", 8), ("hid_done", 16 * s + 8 * s * c)])

            def ternary_gamma():
                pe.wait_ge(sem("gam_sum"), 2)
                mm(ps[:, Y4[3], 0:2], avg[:, :], gam[:, 0:2], start=True, stop=True).then_inc(sem("gam_ready"), 1)

            def att2_output(s, chunks=(0, 1)):
                linear("l1o", s, w_l1o, oT, CH, Y4, lambda c: [("att2_gated", 2 * s + c + 1)],
                       [("att2_used", 3 * s + 2 + chunks[-1]), ("gam_used", 1)], chunks)

            def mlp(s, chunks=(0, 1)):
                pe.wait_ge(sem("tern_done"), 1)
                norm_stats("ln3", s, hT, CH, lambda c: [("l1o_used", 4 * s + 2 * c + 2), ("final", s * (2 * c + 2))],
                           [("qkv2_used", 18), ("g_used", 8)], chunks)
                for c in chunks:
                    after(pe, *norm("ln3", s, "out", c + 1))
                    pe.wait_ge(sem("l1o_used"), 4 * s + 2 * (chunks[-1] + 1))
                    k0 = 2 * s + c
                    for f in range(8):
                        after(pe, "hid_done", 8 * k0 + f - 3)
                        for k in range(2):
                            last = mm(ps[:, Y4[f % 4], 0:CH], w_t1[:, k, f * P:(f + 1) * P],
                                      xT[:, k, cols(s, c)], start=(k == 0), stop=(k == 1))
                        last.then_inc(sem("fc1_ready"), 1)
                    pe.wait_ge(sem("hid_done"), 8 * k0 + 8)
                    for m in range(2):
                        for f in range(8):
                            last = mm(ps[:, X4[2 * c + m], 0:CH], w_t2[:, f, m * P:(m + 1) * P],
                                      hid[:, c, f, :], start=(f == 0), stop=(f == 7))
                        last.then_inc(sem("fc2_ready"), 1)

            pe.wait_ge(sem("w_conv_in"), 32)
            pe.wait_ge(sem("bank_filled"), 1)
            conv(0, {0: weight_means, 1: kv_bias, 2: q_bias, 3: class_stats, 5: class_query})
            window_kv(0, [("w_kv_ready", 1), ("gq_used", 1)])
            for i in range(1, 4):
                conv(i)
                window_kv(i)
            conv(4)
            local_output(0)
            patch_output(0)
            window_kv(4, [("h_tok", 4)])
            conv(5, {2: lambda: lnga_stats(0)})
            global_kv(0)
            window_kv(5, [("gkv_used", 8)])
            conv(6, {0: lambda: class_output(0), 1: lambda: ln0_stats(0), 4: lambda: att0_qkv(0)})
            att0_gate(0)
            window_kv(6, [("go_used", 4)])
            conv(7)
            window_kv(7)
            local_output(1)
            patch_output(1)
            lnga_stats(1)
            global_kv(1)
            att0_channels(0)
            class_output(1)
            ln0_stats(1)
            att0_output(0)
            att0_qkv(1)
            mqa_scores(0)
            att0_gate(1)
            mqa_weigh(0)
            att1_output(0)
            router(0)
            first_expert(0)
            combine(0)
            experts(0, 0)
            experts(0, 1)
            att0_channels(1)
            retention_stats(0)
            att0_output(1)
            retention_qkv(0)
            mqa_scores(1)
            retention_gate(0)
            mqa_weigh(1)
            att1_output(1)
            router(1)
            first_expert(1)
            combine(1)
            experts(1, 0)
            experts(1, 1)
            for c in range(2):
                att2_channels(0, c)
            ternary_gamma()
            retention_stats(1)
            att2_output(0)
            retention_qkv(1)
            retention_gate(1)
            mlp(0)
            for c in range(2):
                att2_channels(1, c)
                att2_output(1, (c,))
                mlp(1, (c,))

        @block.scalar
        def _(act):
            A = nc.scalar.activation

            def waits(pairs):
                for s, value in pairs:
                    after(act, s, value)

            def window_rstd(i):
                act.wait_ge(sem("var10"), i + 1)
                A(st10, st10, ACT.Ln).then_inc(sem("ln10"), 1)
                act.wait_ge(sem("ln10"), i + 1)
                A(st10, st10, ACT.Exp, scale=-0.5).then_inc(sem("rstd10"), 1)

            def window_exp(i):
                act.wait_ge(sem("sc_max"), i + 1)
                A(sc, sc, ACT.Exp, scale=C ** -0.5).then_inc(sem("sc_exp"), 1)

            def conv_evac(i, beside=None, rstd_at=0, exp_at=2):
                for g in range(2 * NCG):
                    c, m = g // 2, g % 2
                    pc = slice(c * CONV_N, (c + 1) * CONV_N)
                    act.wait_ge(sem("conv_ready"), 6 * i + g + 1)
                    if g == 0:
                        after(act, "sums_ready", i)
                    A(patch_emb[:, m, pc], ps[:, g % 2, 0:CONV_N], ACT.Copy)
                    A(patch_sq[:, m, pc], ps[:, g % 2, 0:CONV_N], ACT.Square).then_inc(sem("conv_evac"), 1)
                    if beside and g in beside:
                        beside[g]()
                    if g == rstd_at and i > 0:
                        window_rstd(i - 1)
                    if g == exp_at and i > 0:
                        window_exp(i - 1)

            def kv_evac(i, beside=None):
                after(act, "win_done", i)
                for j in range(NJ):
                    act.wait_ge(sem("kv_ready"), 9 * i + j + 1)
                    b = 2 + 2 * (j % 2)
                    A(kv_raw[:, j, :, 0:KVN], ps[:, b:b + 2, 0:KVN], ACT.Copy).then_inc(sem("kv_evac"), 1)
                    if beside and j in beside:
                        beside[j]()

            def norm_act(name, s, src, n, src_ready, drained=(), chunks=(0, 1)):
                banks = NORM_BANKS[name]
                waits(drained)
                for c in chunks if name != "rms1" else ():
                    waits(src_ready(c))
                    after(act, "norm_stat", norm(name, s, "stat", c + 1)[1] - 2)
                    A(sqb[:, spot(name, s, c) % 2, :, 0:n], src[:, :, cols(s, c, n)],
                      ACT.Square).then_inc(sem("norm_sq"), 1)
                if not name.startswith("rms"):
                    for c in chunks:
                        after(act, *norm(name, s, "stat", c + 1))
                        after(act, "norm_out", spot(name, s, c) - 1)
                        A(lnv[:, spot(name, s, c) % 2, 0:n], ps[:, banks[2 * c], 0:n],
                          ACT.Square).then_inc(sem("norm_mu2"), 1)
                for c in chunks:
                    r = lnv[:, spot(name, s, c) % 2, 0:n]
                    after(act, *norm(name, s, "var", c + 1))
                    A(r, r, ACT.Ln).then_inc(sem("norm_ln"), 1)
                    after(act, *norm(name, s, "ln", c + 1))
                    A(r, r, ACT.Exp, scale=-0.5).then_inc(sem("norm_rstd"), 1)

            def images_evac(name, s, dst, n, nt, banks, gate=False):
                for g in range((nt + 1) // 2):
                    k = min(2, nt - 2 * g)
                    act.wait_ge(sem(name + "_ready"), (nt + 1) // 2 * s + g + 1)
                    src = ps[:, banks[g % 4], 0:k * n].rearrange("p (t n) -> p t n", t=k)
                    to = dst[:, 2 * g:2 * g + k, :]
                    if gate:
                        A(to[:, :, 0:3 * QC], src[:, :, 0:3 * QC], ACT.Copy)
                        last = A(to[:, :, 3 * QC:4 * QC], src[:, :, 3 * QC:4 * QC], ACT.Sigmoid)
                    else:
                        last = A(to, src, ACT.Copy)
                    last.then_inc(sem(name + "_used"), 1)

            def channels_evac(name, s, banks, groups=(0, 1, 2)):
                for g in groups:
                    t0, t1 = GROUPS[g]
                    act.wait_ge(sem(name + "_ready"), 3 * s + g + 1)
                    to = oT[:, :, s * NH + t0 * HB:s * NH + t1 * HB].rearrange("p m (t b) -> p m t b", b=HB)
                    src = ps[:, banks[g], 0:(t1 - t0) * QC].rearrange("p (t m b) -> p m t b", m=2, b=HB)
                    if name == "att2":
                        for m in range(2):
                            last = A(to[:, m], src[:, m], ACT.Identity, bias=v("gn_bias", m), scale=v("gn_weight", m))
                    else:
                        last = A(to, src, ACT.Copy)
                    last.then_inc(sem(name + "_used"), 1)

            def local_output(s):
                for g in range(2):
                    act.wait_ge(sem("aggT_ready"), 2 * s + g + 1)
                    c0 = s * NH + 2 * g * P
                    A(xT[:, :, c0:c0 + 2 * P].rearrange("p m (i n) -> p m i n", i=2),
                      ps[:, X4[g], :].rearrange("p (i m n) -> p m i n", i=2, m=2),
                      ACT.Copy).then_inc(sem("aggT_used"), 1)

            def patch_output(s):
                for c in range(2):
                    for m in range(2):
                        act.wait_ge(sem("mod_ready"), 4 * s + 2 * c + m + 1)
                        A(hT[:, m, cols(s, c, LC)], ps[:, X4[2 * c + m], 0:LC], ACT.Identity,
                          bias=v("mod_b", m)).then_inc(sem("h_tok"), 1)

            def lnga(s):
                norm_act("lnga", s, yT, LC, lambda c: [("local_out", 4 * s + 2 * c + 2)])
                for c in range(2):
                    after(act, *norm("lnga", s, "out", c + 1))
                    for m in range(2):
                        y = xT[:, m, cols(s, c, LC)]
                        last = A(y, y, ACT.Identity, bias=v("ga_ln_kv_b", m), scale=v("ga_ln_kv_g", m))
                    last.then_inc(sem("lnga_aff"), 1)

            def class_norm():
                act.wait_ge(sem("cls_var"), 1)
                A(small[:, 8:9], small[:, 8:9], ACT.Ln).then_inc(sem("cls_ln"), 1)
                act.wait_ge(sem("cls_ln"), 1)
                A(small[:, 8:9], small[:, 8:9], ACT.Exp, scale=-0.5).then_inc(sem("cls_rstd"), 1)

            def global_kv(s):
                if s == 1:
                    act.wait_ge(sem("win_done"), ITERS)
                images_evac("gkv", s, qkv(s, 128), 128, HW, X4)

            def ga_exp(s):
                act.wait_ge(sem("gsc_max"), s + 1)
                A(gs, gs, ACT.Exp, scale=C ** -0.5).then_inc(sem("gsc_exp"), 1)

            def class_output(s):
                act.wait_ge(sem("gagg_ready"), s + 1)
                A(oT[:, :, s * NH:s * NH + HB], ps[:, 2, 0:QC].rearrange("p (m b) -> p m b", m=2),
                  ACT.Copy).then_inc(sem("gagg_used"), 1)

            def ln0(s):
                norm_act("ln0", s, hT, CH, lambda c: [("h_tok", 4 * s + 4), ("h_cls", 2 * s + 2)])

            def att0_qkv(s):
                act.wait_ge(sem("gatt_done"), s + 1)
                images_evac("qkv0", s, qkv(s, 256), 256, T, X4, gate=True)

            def att0_gate(s):
                for c in range(2):
                    for m in range(2):
                        act.wait_ge(sem("go_ready"), 4 * s + 2 * c + m + 1)
                        A(yT[:, m, cols(s, c)], ps[:, X4[2 * c + m], 0:CH], ACT.Sigmoid).then_inc(sem("go_used"), 1)

            def att_exp(name, s, nh, scale):
                act.wait_ge(sem(name + "_max"), s + 1)
                A(S[:, 0:T * T * nh], S[:, 0:T * T * nh], ACT.Exp, scale=scale).then_inc(sem(name + "_exp"), 1)

            def att0_channels(s):
                channels_evac("att0", s, Y4)

            def att0_output(s):
                norm_act("ln1", s, hT, CH, lambda c: [("wo_used", 4 * s + 2 * c + 2)])
                norm_act("rms1", s, xT, CH, lambda c: [])

            def mqa_scores(s):
                t_ = mqa_of[s]
                for c in range(2):
                    for m in range(2):
                        act.wait_ge(sem("mq_ready"), 4 * s + 2 * c + m + 1)
                        A(t_.q[:, m, c * CH:(c + 1) * CH], ps[:, Y4[2 * c + m], 0:CH],
                          ACT.Copy).then_inc(sem("mq_used"), 1)
                for c in range(2):
                    act.wait_ge(sem("mk_ready"), 2 * s + c + 1)
                    A(t_.k[:, c * CH:(c + 1) * CH], ps[:, Y4[c], 0:CH], ACT.Copy).then_inc(sem("mk_used"), 1)
                act.wait_ge(sem("mv_ready"), s + 1)
                A(t_.v_flat, ps[:, Y4[2], :], ACT.Copy).then_inc(sem("mv_used"), 1)

            def mqa_exp(s):
                t_ = mqa_of[s]
                act.wait_ge(sem("att1_max"), s + 1)
                A(t_.p3[:, :, 0:T], t_.p3[:, :, 0:T], ACT.Exp, scale=QC ** -0.5).then_inc(sem("att1_exp"), 1)

            def mqa_weigh(s):
                t_ = mqa_of[s]
                for b in range(2):
                    act.wait_ge(sem("mpT_ready"), 2 * s + b + 1)
                    A(t_.pT[:, 4 * b:4 * b + 4, :], ps[:, Y4[2 + b], :].rearrange("p (g n) -> p g n", g=4),
                      ACT.Copy).then_inc(sem("mpT_used"), 1)
                for b in range(4):
                    act.wait_ge(sem("att1_ready"), 4 * s + b + 1)
                    to = oT[:, :, s * NH:(s + 1) * NH].rearrange("p m (t g j) -> p m t g j", g=8, j=4)
                    A(to[:, :, :, :, b],
                      ps[:, Y4[b], 0:8 * 2 * T].rearrange("p (b m t) -> p m t b", b=8, m=2),
                      ACT.Copy).then_inc(sem("att1_used"), 1)

            def att1_output(s):
                norm_act("rms2", s, xT, CH, lambda c: [("mo_used", 4 * s + 2 * c + 2)])

            def router(s):
                act.wait_ge(sem("lg_max"), s + 1)
                A(small[:, 0:40], small[:, 0:40], ACT.Exp).then_inc(sem("lg_exp"), 1)
                act.wait_ge(sem("rw_max"), s + 1)
                A(small[:, 40:80], small[:, 40:80], ACT.Exp).then_inc(sem("rw_exp"), 1)

            def combine(s):
                act.wait_ge(sem("cmb_ready"), s + 1)
                A(cmbT[:, 0:512], ps[0:NEXP, Y4[1], :], ACT.Copy)
                A(cmbT[:, 512:NH], ps[0:NEXP, Y4[2], 0:NH - 512], ACT.Copy).then_inc(sem("cmb_used"), 1)

            def experts(s, c, at_=None, other=None):
                base = 36 * s + 18 * c
                for n in range(18):
                    act.wait_ge(sem("eup_ready"), base + n + 1)
                    after(act, "eh_ready", base + n - 1)
                    A(esil[n % 2], ps[:, 2 + 2 * (n % 2), 0:CH], ACT.Silu).then_inc(sem("esil_ready"), 1)
                    if n == at_:
                        other()

            def retention_stats(s):
                norm_act("ln2", s, hT, CH, lambda c: [("moe_used", 4 * s + 2 * c + 2)])

            def retention_qkv(s):
                images_evac("qkv2", s, qkv(s, 192), 192, T, X4)

            def retention_gate(s):
                for c in range(2):
                    for m in range(2):
                        act.wait_ge(sem("g_ready"), 4 * s + 2 * c + m + 1)
                        A(yT[:, m, cols(s, c)], ps[:, X4[2 * c + m], 0:CH], ACT.Silu).then_inc(sem("g_used"), 1)

            def group_norm(n, t0, t1):
                r = S[:, 2 * t0:2 * t1]
                act.wait_ge(sem("gn_var"), n + 1)
                A(r, r, ACT.Ln).then_inc(sem("gn_ln"), 1)
                act.wait_ge(sem("gn_ln"), n + 1)
                A(r, r, ACT.Exp, scale=-0.5).then_inc(sem("gn_rstd"), 1)

            def mlp(s, chunks=(0, 1)):
                norm_act("ln3", s, hT, CH, lambda c: [("l1o_used", 4 * s + 2 * c + 2)], (), chunks)
                for c in chunks:
                    k0 = 2 * s + c
                    for f in range(8):
                        act.wait_ge(sem("fc1_ready"), 8 * k0 + f + 1)
                        if f == 0:
                            after(act, "fc2_ready", 2 * k0 - 2)
                        A(hid[:, c, f, :], ps[:, Y4[f % 4], 0:CH], ACT.Relu,
                          bias=v("b1", f)).then_inc(sem("hid_done"), 1)

            def ln_exp_table():
                nc.scalar.preload_act_table_set("natural_log_exp_and_others")

            ln_exp_table()
            act.wait_ge(sem("w_first_in"), 64)
            conv_evac(0, {4: class_norm})
            kv_evac(0)
            for i in range(1, 4):
                conv_evac(i)
                kv_evac(i)
            conv_evac(4)
            local_output(0)
            patch_output(0)
            kv_evac(4)
            conv_evac(5, {2: lambda: lnga(0)}, exp_at=3)
            global_kv(0)
            kv_evac(5, {4: lambda: ga_exp(0)})
            conv_evac(6, {0: lambda: class_output(0), 1: lambda: ln0(0), 4: lambda: att0_qkv(0)}, 1, 3)
            att0_gate(0)
            ln_exp_table()
            kv_evac(6)
            conv_evac(7)
            kv_evac(7)
            att_exp("att0", 0, 4, 16 ** -0.5)
            window_rstd(7)
            window_exp(7)
            local_output(1)
            patch_output(1)
            lnga(1)
            global_kv(1)
            att0_channels(0)
            ga_exp(1)
            class_output(1)
            ln0(1)
            att0_output(0)
            att0_qkv(1)
            mqa_scores(0)
            ln_exp_table()
            mqa_exp(0)
            att0_gate(1)
            ln_exp_table()
            mqa_weigh(0)
            att1_output(0)
            router(0)
            combine(0)
            experts(0, 0, 8, lambda: att_exp("att0", 1, 4, 16 ** -0.5))
            experts(0, 1)
            ln_exp_table()
            att0_channels(1)
            retention_stats(0)
            att0_output(1)
            retention_qkv(0)
            mqa_scores(1)
            mqa_exp(1)
            mqa_weigh(1)
            retention_gate(0)
            ln_exp_table()
            att1_output(1)
            router(1)
            combine(1)
            experts(1, 0)
            experts(1, 1, 7, lambda: group_norm(0, 0, T))
            ln_exp_table()
            channels_evac("att2", 0, Y4)
            retention_stats(1)
            retention_qkv(1)
            retention_gate(1)
            ln_exp_table()
            mlp(0)
            group_norm(1, 0, 9)
            channels_evac("att2", 1, Y4, (0, 1))
            mlp(1, (0,))
            group_norm(2, 9, T)
            channels_evac("att2", 1, Y4, (2,))
            mlp(1, (1,))

        @block.vector
        def _(dve):
            V = nc.vector
            steps = [0]

            def waits(pairs):
                for s, value in pairs:
                    after(dve, s, value)

            def mark(ins):
                steps[0] += 1
                ins.then_inc(sem("dve_step"), 1)
                return steps[0]

            def need(count):
                dve.wait_ge(sem("dve_step"), count)

            def link(ins):
                need(mark(ins))

            V.memset(ps[:, Y4[2], :], 0.0).then_inc(sem("bank_filled"), 1)
            link(V.memset(avg[:, :], 1.0 / C))
            dve.wait_ge(sem("w_first_in"), 64)
            for k in range(2):
                V.tensor_scalar(w_kvc[:, k, :, 0:C], w_kv[:, k, :].rearrange("p (s n) -> p s n", s=2),
                                v("la_ln_kv_g", k), None, ALU.mult)
                V.tensor_scalar(w_lqc[:, k, 0:C], w_lq[:, k, :], v("la_ln_q_g", k), None, ALU.mult)
            V.memset(w_kvc[:, :, :, C:KVS], 1.0 / C)
            V.memset(w_lqc[:, :, C:KVS], 1.0 / C).then_inc(sem("w_scaled"), 1)
            for k in range(2):
                last = V.tensor_scalar(bcol[:, k, :], avg[:, :], v("la_ln_kv_b", k), float(C), ALU.mult, ALU.mult)
            last.then_inc(sem("kv_bcol"), 1)
            dve.wait_ge(sem("w_means"), 1)
            for k in range(2):
                V.tensor_tensor(w_kvc[:, k, :, 0:C], w_kvc[:, k, :, 0:C],
                                ps[:, 2, :].rearrange("p (s n) -> p s n", s=2), ALU.subtract)
                last = V.tensor_tensor(w_lqc[:, k, 0:C], w_lqc[:, k, 0:C], ps[:, 3, 0:C], ALU.subtract)
            link(last)
            dve.wait_ge(sem("kv_brow"), 1)
            link(V.tensor_copy(bias_row[:, 0:2 * C], ps[:, 4, :]))
            for k in range(2):
                last = V.tensor_scalar(bcol[:, k, :], avg[:, :], v("la_ln_q_b", k), float(C), ALU.mult, ALU.mult)
            last.then_inc(sem("q_bcol"), 1)
            dve.wait_ge(sem("q_brow"), 1)
            V.tensor_copy(bias_row[:, 2 * C:3 * C], ps[:, 5, 0:C]).then_inc(sem("w_kv_ready"), 1)
            dve.wait_ge(sem("w_kv_ready"), 1)

            sc3 = sc.rearrange("p (j h) -> p j h", j=NJ)

            def window_sums(i):
                s, r = i // 4, i % 4
                dve.wait_ge(sem("conv_evac"), 6 * i + 6)
                after(dve, "stat_ready", i)
                link(V.tensor_reduce(red_sq, patch_emb.rearrange("p m (j n) -> p m n j", j=NJ), AX.X, ALU.add))
                link(V.tensor_scalar(red, red_sq, 1.0 / NJ, None, ALU.mult))
                V.tensor_copy(yT[:, :, s * NH + r * P:s * NH + (r + 1) * P], red)
                link(V.tensor_tensor(red_sq, red, red, ALU.mult))
                link(V.tensor_tensor(rsq_sum, red_sq[:, 0, :], red_sq[:, 1, :], ALU.add))
                V.tensor_tensor(sq_sum, patch_sq[:, 0, :], patch_sq[:, 1, :], ALU.add).then_inc(sem("sums_ready"), 1)

            def window_scores(i):
                dve.wait_ge(sem("stat_ready"), i + 1)
                dve.wait_ge(sem("kv_evac"), 9 * i + 9)
                st = ps[:, 6 + i % 2, :]
                V.tensor_copy(mean10[:, 0:NJ], kv_raw[:, :, 0, C])
                link(V.tensor_copy(mean10[:, NJ:NJ + 1], st[:, C:C + 1]))
                link(V.tensor_tensor(mean10, mean10, mean10, ALU.mult))
                link(V.tensor_tensor(st10, st[:, 300:310], mean10, ALU.subtract))
                V.tensor_scalar(st10, st10, 0.0, EPS_LN, ALU.max, ALU.add).then_inc(sem("var10"), 1)
                dve.wait_ge(sem("rstd10"), i + 1)
                link(V.scalar_tensor_tensor(out=q_win, in0=st[:, 0:C], scalar=st10[:, NJ:NJ + 1],
                                            in1=bias_row[:, 2 * C:3 * C], op0=ALU.mult, op1=ALU.add))
                prod3 = prodW.rearrange("p (j n) -> p j n", j=NJ)
                V.tensor_tensor(qk_tmp, q_win, bias_row[:, 0:C], ALU.mult)
                link(V.tensor_tensor(prod3, kv_raw[:, :, 0, 0:C],
                                     q_win.unsqueeze(1).to_broadcast([P, NJ, C]), ALU.mult))
                V.tensor_reduce(qb8, qk_tmp.rearrange("p (h d) -> p h d", h=8), AX.X, ALU.add)
                link(V.tensor_reduce(sc, prodW.rearrange("p (a d) -> p a d", d=32), AX.X, ALU.add))
                r9 = st10[:, 0:NJ].unsqueeze(2).to_broadcast([P, NJ, 8])
                link(V.tensor_tensor(sc3, sc3, r9, ALU.mult))
                link(V.tensor_tensor(sc3, sc3, qb8.unsqueeze(1).to_broadcast([P, NJ, 8]), ALU.add))
                link(V.tensor_reduce(sm8, sc.rearrange("p (j h) -> p h j", j=NJ), AX.X, ALU.max))
                V.tensor_tensor(sc3, sc3, sm8.unsqueeze(1).to_broadcast([P, NJ, 8]),
                                ALU.subtract).then_inc(sem("sc_max"), 1)

            def window_output(i):
                r9 = st10[:, 0:NJ].unsqueeze(2).to_broadcast([P, NJ, 8])
                dve.wait_ge(sem("sc_exp"), i + 1)
                if i == 4:
                    dve.wait_ge(sem("aggT_ready"), 2)
                link(V.tensor_reduce(sm8, sc.rearrange("p (j h) -> p h j", j=NJ), AX.X, ALU.add))
                link(V.reciprocal(qb8, sm8))
                link(V.tensor_tensor(sc3, sc3, qb8.unsqueeze(1).to_broadcast([P, NJ, 8]), ALU.mult))
                link(V.tensor_tensor(sc3, sc3, r9, ALU.mult))
                link(V.tensor_tensor(prodW.rearrange("p (j h d) -> p j h d", j=NJ, h=8),
                                     kv_raw[:, :, 1, 0:C].rearrange("p j (h d) -> p j h d", h=8),
                                     sc3.unsqueeze(3).to_broadcast([P, NJ, 8, 32]), ALU.mult))
                link(V.tensor_reduce(qk_tmp, prodW.rearrange("p (j n) -> p n j", j=NJ), AX.X, ALU.add))
                V.tensor_tensor(aggW[:, i % 4, :], qk_tmp, bias_row[:, C:2 * C], ALU.add).then_inc(sem("win_done"), 1)
                dve.wait_ge(sem("win_done"), i + 1)

            def norm_dve(name, s, src, dst, n, eps, gain=None, drained=(), chunks=(0, 1)):
                banks = NORM_BANKS[name]
                centred = not name.startswith("rms")
                waits(drained)
                x = {}
                for c in chunks:
                    r = lnv[:, spot(name, s, c) % 2, 0:n]
                    cc = cols(s, c, n)
                    if name != "rms1":
                        after(dve, *norm(name, s, "stat", c + 1))
                    if name == "rms1":
                        after(dve, "norm_out", spot(name, s, c) - 1)
                        link(V.tensor_tensor(r, r, r, ALU.mult))
                        link(V.tensor_tensor(r, r, sqb[:, c, 0, 0:n], ALU.mult))
                        V.tensor_scalar(r, r, eps, None, ALU.add).then_inc(sem("norm_var"), 1)
                    elif centred:
                        after(dve, *norm(name, s, "mu2", c + 1))
                        link(V.tensor_tensor(r, ps[:, banks[2 * c + 1], 0:n], r, ALU.subtract))
                        if name == "ln1":
                            V.tensor_scalar(sqb[:, c, 0, 0:n], r, 0.0, None, ALU.max)
                        V.tensor_scalar(r, r, 0.0, eps, ALU.max, ALU.add).then_inc(sem("norm_var"), 1)
                        x[c] = (mark(V.tensor_tensor(
                            dst[:, :, cc], src[:, :, cc],
                            ps[:, banks[2 * c], 0:n].unsqueeze(1).to_broadcast([P, 2, n]), ALU.subtract)))
                    else:
                        after(dve, "norm_out", spot(name, s, c) - 1)
                        V.tensor_scalar(r, ps[:, banks[2 * c + 1], 0:n], eps, None,
                                        ALU.add).then_inc(sem("norm_var"), 1)
                for c in chunks:
                    r = lnv[:, spot(name, s, c) % 2, 0:n]
                    cc = cols(s, c, n)
                    after(dve, *norm(name, s, "rstd", c + 1))
                    if centred:
                        need(x[c])
                        last = V.tensor_tensor(dst[:, :, cc], dst[:, :, cc],
                                               r.unsqueeze(1).to_broadcast([P, 2, n]), ALU.mult)
                    else:
                        for m in range(2):
                            last = V.scalar_tensor_tensor(out=dst[:, m, cc], in0=src[:, m, cc], scalar=v(gain, m),
                                                          in1=r, op0=ALU.mult, op1=ALU.mult)
                    last.then_inc(sem("norm_out"), 1)

            gq = small[:, 144:144 + QC]

            def class_query():
                for k in range(2):
                    V.tensor_copy(small[:, 2 * k:2 * k + 1], v("class_emb", k))
                    last = V.tensor_tensor(small[:, 2 * k + 1:2 * k + 2], v("class_emb", k), v("class_emb", k),
                                           ALU.mult)
                last.then_inc(sem("cls_cols"), 1)
                dve.wait_ge(sem("cls_stat"), 1)
                link(V.tensor_copy(small[:, 6:8], ps[:, 2, 0:2]))
                link(V.tensor_tensor(small[:, 5:6], small[:, 6:7], small[:, 6:7], ALU.mult))
                link(V.tensor_tensor(small[:, 8:9], small[:, 7:8], small[:, 5:6], ALU.subtract))
                V.tensor_scalar(small[:, 8:9], small[:, 8:9], 0.0, EPS_LN, ALU.max, ALU.add).then_inc(sem("cls_var"), 1)
                dve.wait_ge(sem("cls_rstd"), 1)
                for k in range(2):
                    link(V.tensor_scalar(small[:, 10 + k:11 + k], v("class_emb", k), small[:, 6:7], small[:, 8:9],
                                         ALU.subtract, ALU.mult))
                    link(V.scalar_tensor_tensor(out=small[:, 12 + k:13 + k], in0=small[:, 10 + k:11 + k],
                                                scalar=v("ga_ln_q_g", k), in1=v("ga_ln_q_b", k),
                                                op0=ALU.mult, op1=ALU.add))
                for k in range(2):
                    last = V.tensor_scalar(small[:, 16 + 64 * k:48 + 64 * k], avg[:, 0:32], small[:, 12 + k:13 + k],
                                           float(C), ALU.mult, ALU.mult)
                last.then_inc(sem("cls_bcast"), 1)
                dve.wait_ge(sem("gq_ready"), 1)
                V.tensor_copy(gq, ps[:, 3, 0:QC]).then_inc(sem("gq_used"), 1)
                dve.wait_ge(sem("gq_used"), 1)
                link(V.tensor_tensor(small[:, 4:6], vec[:, VCOL["class_emb"]:VCOL["class_emb"] + 2],
                                     vec[:, VCOL["ga_proj_b"]:VCOL["ga_proj_b"] + 2], ALU.add))

            def local_out(s):
                for c in range(2):
                    for m in range(2):
                        dve.wait_ge(sem("proj_ready"), 4 * s + 2 * c + m + 1)
                        y = yT[:, m, cols(s, c, LC)]
                        V.scalar_tensor_tensor(out=y, in0=ps[:, X4[2 * c + m], 0:LC], scalar=v("la_proj_b", m),
                                               in1=y, op0=ALU.add, op1=ALU.add).then_inc(sem("local_out"), 1)

            def global_attention(s):
                gkv = qkv(s, 128)[:, 0:HW, :]
                dve.wait_ge(sem("gkv_used"), 8 * s + 8)
                pa = prods[0][:, 0:HW * QC]
                gs3 = gs.rearrange("p (t h) -> p t h", t=HW)
                g2, gi = gs_top, gs_inv
                link(V.tensor_tensor(pa.rearrange("p (t n) -> p t n", t=HW), gkv[:, :, 0:QC],
                                     gq.unsqueeze(1).to_broadcast([P, HW, QC]), ALU.mult))
                link(V.tensor_reduce(gs, pa.rearrange("p (a d) -> p a d", d=32), AX.X, ALU.add))
                link(V.tensor_reduce(g2, gs.rearrange("p (t h) -> p h t", t=HW), AX.X, ALU.max))
                V.tensor_tensor(gs3, gs3, g2.unsqueeze(1).to_broadcast([P, HW, 2]),
                                ALU.subtract).then_inc(sem("gsc_max"), 1)
                dve.wait_ge(sem("gsc_exp"), s + 1)
                link(V.tensor_reduce(g2, gs.rearrange("p (t h) -> p h t", t=HW), AX.X, ALU.add))
                link(V.reciprocal(gi, g2))
                link(V.tensor_tensor(gs3, gs3, gi.unsqueeze(1).to_broadcast([P, HW, 2]), ALU.mult))
                link(V.tensor_tensor(pa.rearrange("p (t h d) -> p t h d", t=HW, h=2),
                                     gkv[:, :, QC:2 * QC].rearrange("p t (h d) -> p t h d", h=2),
                                     gs3.unsqueeze(3).to_broadcast([P, HW, 2, 32]), ALU.mult))
                V.tensor_reduce(small[:, 272:336], pa.rearrange("p (t n) -> p n t", t=HW), AX.X,
                                ALU.add).then_inc(sem("gatt_done"), 1)

            def class_token(s):
                for m in range(2):
                    dve.wait_ge(sem("gproj_ready"), 2 * s + m + 1)
                    V.tensor_scalar(hT[:, m, s * NH + NWH:(s + 1) * NH], ps[:, 3 + m, 0:HB], small[:, 4 + m:5 + m],
                                    None, ALU.add).then_inc(sem("h_cls"), 1)

            def rotate(x, nh, d, cs, sn):
                xv = x.rearrange("p t (h d) -> p t h d", h=nh)
                pv = prods[0].rearrange("p (t h d) -> p t h d", t=T, h=nh)
                h_ = d // 2
                half = [P, T, nh, h_]
                V.tensor_tensor(pv[:, :, :, 0:h_], xv[:, :, :, h_:d],
                                sn[:, :, 0:h_].unsqueeze(2).to_broadcast(half), ALU.mult)
                link(V.tensor_tensor(pv[:, :, :, h_:d], xv[:, :, :, 0:h_],
                                     sn[:, :, h_:d].unsqueeze(2).to_broadcast(half), ALU.mult))
                link(V.tensor_tensor(xv, xv, cs.unsqueeze(2).to_broadcast([P, T, nh, d]), ALU.mult))
                link(V.tensor_tensor(xv, xv, pv, ALU.add))

            def weighted(product, reduce, cuts):
                for first, end in zip((0, *cuts), (*cuts, T)):
                    p_done, s_done = [], []
                    for t in range(end - first + 1):
                        if t < end - first:
                            if t >= 2:
                                need(s_done[t - 2])
                            p_done.append(mark(product(first + t)))
                        if t >= 1:
                            need(p_done[t - 1])
                            s_done.append(mark(reduce(first + t - 1)))
                            if t == end - first:
                                need(s_done[-1])
                            yield

            def scores(q, k_, nh, sizes, cuts=()):
                d = QC // nh
                return weighted(
                    lambda t: V.tensor_tensor(
                        prods[t % 2][:, 0:sizes[t] * QC].rearrange("p (k c) -> p k c", c=QC), k_[:, 0:sizes[t], :],
                        q[:, t, :].unsqueeze(1).to_broadcast([P, sizes[t], QC]), ALU.mult),
                    lambda t: V.tensor_reduce(
                        S[:, t * T * nh:t * T * nh + sizes[t] * nh],
                        prods[t % 2][:, 0:sizes[t] * QC].rearrange("p (a d) -> p a d", d=d), AX.X, ALU.add), cuts)

            def weigh(v_, o_, nh, sizes, cuts=()):
                d = QC // nh
                return weighted(
                    lambda t: V.tensor_tensor(
                        prods[t % 2][:, 0:sizes[t] * QC].rearrange("p (k h d) -> p k h d", h=nh, d=d),
                        v_[:, 0:sizes[t], :].rearrange("p k (h d) -> p k h d", h=nh),
                        S[:, t * T * nh:t * T * nh + sizes[t] * nh].rearrange("p (k h) -> p k h", h=nh)
                        .unsqueeze(3).to_broadcast([P, sizes[t], nh, d]), ALU.mult),
                    lambda t: V.tensor_reduce(
                        o_[:, t, :], prods[t % 2][:, 0:sizes[t] * QC].rearrange("p (k c) -> p c k", c=QC),
                        AX.X, ALU.add), cuts)

            def softmax_shift(name, nh):
                s4 = S[:, 0:T * T * nh].rearrange("p (t k h) -> p t k h", t=T, k=T)
                mx = prods[0][:, 0:T * nh].rearrange("p (t h) -> p t h", t=T)
                link(V.tensor_reduce(mx, S[:, 0:T * T * nh].rearrange("p (t k h) -> p t h k", t=T, k=T),
                                     AX.X, ALU.max))
                V.tensor_tensor(s4, s4, mx.unsqueeze(2).to_broadcast([P, T, T, nh]),
                                ALU.subtract).then_inc(sem(name + "_max"), 1)

            def softmax_scale(name, s, nh):
                s4 = S[:, 0:T * T * nh].rearrange("p (t k h) -> p t k h", t=T, k=T)
                ri = prods[0][:, T * nh:2 * T * nh]
                dve.wait_ge(sem(name + "_exp"), s + 1)
                link(V.tensor_reduce(prods[0][:, 0:T * nh].rearrange("p (t h) -> p t h", t=T),
                                     S[:, 0:T * T * nh].rearrange("p (t k h) -> p t h k", t=T, k=T), AX.X, ALU.add))
                link(V.reciprocal(ri, prods[0][:, 0:T * nh]))
                link(V.tensor_tensor(s4, s4, ri.rearrange("p (t h) -> p t h", t=T).unsqueeze(2)
                                     .to_broadcast([P, T, T, nh]), ALU.mult))

            def att0_scores(s):
                q = qkv(s, 256)
                link(V.memset(S, MASKED))
                dve.wait_ge(sem("tab_in"), 64)
                dve.wait_ge(sem("qkv0_used"), 9 * s + 9)
                link(V.tensor_tensor(q[:, :, 128:192], q[:, :, 128:192], q[:, :, 192:256], ALU.mult))
                rotate(q[:, :, 0:64], 4, 16, rope[:, 0], rope[:, 1])
                yield
                rotate(q[:, :, 64:128], 4, 16, rope[:, 0], rope[:, 1])
                yield
                yield from scores(q[:, :, 0:64], q[:, :, 64:128], 4, CAUSAL, cuts=CUT_SCORES)

            def att0_weigh(s):
                q = qkv(s, 256)
                yield from weigh(q[:, :, 128:192], q[:, :, 0:64], 4, CAUSAL, cuts=CUT_WEIGH)

            def mqa_softmax(s):
                t_ = mqa_of[s]
                link(V.memset(t_.p, 0.0))
                for b in range(2):
                    dve.wait_ge(sem("msc_ready"), 2 * s + b + 1)
                    half = slice(16 * b, 16 * b + 16)
                    sc_ = ps[:, Y4[b], 0:16 * T].rearrange("p (i k) -> p i k", k=T)
                    link(V.tensor_reduce(t_.top[:, half], sc_, AX.X, ALU.max))
                    last = V.tensor_tensor(t_.p3[:, half, 0:T], sc_,
                                           t_.top[:, half].unsqueeze(2).to_broadcast([P, 16, T]), ALU.subtract)
                last.then_inc(sem("att1_max"), 1)
                dve.wait_ge(sem("att1_exp"), s + 1)
                link(V.tensor_reduce(t_.top, t_.p3[:, :, 0:T], AX.X, ALU.add))
                link(V.reciprocal(t_.inv, t_.top))
                V.tensor_tensor(t_.p3[:, :, 0:T], t_.p3[:, :, 0:T], t_.inv.unsqueeze(2).to_broadcast([P, HB, T]),
                                ALU.mult).then_inc(sem("msc_done"), 1)

            def att2_scores(s):
                q = qkv(s, 192)
                dve.wait_ge(sem("w_l1_in"), 128)
                dve.wait_ge(sem("qkv2_used"), 9 * s + 9)
                rotate(q[:, :, 0:64], 2, 32, xpos[:, 0], xpos[:, 1])
                yield
                rotate(q[:, :, 64:128], 2, 32, xpos[:, 2], xpos[:, 3])
                yield
                yield from scores(q[:, :, 0:64], q[:, :, 64:128], 2, CAUSAL, cuts=CUT_RETENTION[s])

            def att2_decay(t0, t1):
                for t in range(t0, t1):
                    w = slice(t * T * 2, t * T * 2 + (t + 1) * 2)
                    last = V.tensor_tensor(S[:, w], S[:, w], decay[:, w], ALU.mult)
                link(last)

            def att2_weigh(s):
                q = qkv(s, 192)
                yield from weigh(q[:, :, 128:192], q[:, :, 0:64], 2, CAUSAL, cuts=CUT_RETENTION[s])

            def done(name, s):
                V.memset(small[:, 380:381], 0.0).then_inc(sem(name + "_done"), 1)
                dve.wait_ge(sem(name + "_done"), s + 1)

            def run(steps_, n=None):
                for i, _ in enumerate(steps_):
                    if n is not None and i + 1 >= n:
                        return

            def att0_gated(s):
                for c in range(2):
                    dve.wait_ge(sem("att0_used"), 3 * s + min(3, ((c + 1) * CH - 1) // 256 + 1))
                    dve.wait_ge(sem("go_used"), 4 * s + 4)
                    V.tensor_tensor(oT[:, :, cols(s, c)], oT[:, :, cols(s, c)], yT[:, :, cols(s, c)],
                                    ALU.mult).then_inc(sem("att0_gated"), 1)

            def add_to_h(name, s, banks, chunks=(0, 1)):
                for c in chunks:
                    for m in range(2):
                        y = hT[:, m, cols(s, c)]
                        dve.wait_ge(sem(name + "_ready"), 4 * s + 2 * c + m + 1)
                        V.tensor_tensor(y, y, ps[:, banks[2 * c + m], 0:CH], ALU.add).then_inc(sem(name + "_used"), 1)

            def att0_output(s):
                add_to_h("wo", s, Y4)
                norm_dve("ln1", s, hT, xT, CH, EPS_LN)
                for c in range(2):
                    after(dve, *norm("ln1", s, "out", c + 1))
                    link(V.tensor_tensor(hT[:, :, cols(s, c)], hT[:, :, cols(s, c)], xT[:, :, cols(s, c)], ALU.add))
                norm_dve("rms1", s, xT, yT, CH, EPS_RMS, gain="g1")

            def att1_output(s):
                for c in range(2):
                    for m in range(2):
                        pb = ps[:, Y4[2 * c + m], 0:CH]
                        dve.wait_ge(sem("mo_ready"), 4 * s + 2 * c + m + 1)
                        V.tensor_tensor(hT[:, m, cols(s, c)], hT[:, m, cols(s, c)], pb, ALU.add)
                        V.tensor_tensor(xT[:, m, cols(s, c)], xT[:, m, cols(s, c)], pb,
                                        ALU.add).then_inc(sem("mo_used"), 1)
                norm_dve("rms2", s, xT, yT, CH, EPS_RMS, gain="g2")

            def router(s):
                rw = small[:, 0:40]
                rw3 = rw.rearrange("p (t e) -> p t e", t=5)
                w3 = small[:, 40:80].rearrange("p (t e) -> p t e", t=5)
                top, inv = small[:, 144:149], small[:, 153:158]
                cmpA = prods[0][:, 0:320].rearrange("p (t e j) -> p t e j", t=5, e=8)
                cmpB = prods[0][:, 320:640].rearrange("p (t e j) -> p t e j", t=5, e=8)
                rank = prods[0][:, 640:680].rearrange("p (t e) -> p t e", t=5)
                s58, s588 = [P, 5, 8], [P, 5, 8, 8]
                link(V.memset(small[:, 0:160], 0.0))
                dve.wait_ge(sem("logits_ready"), s + 1)
                V.tensor_copy(small[0:32, 0:40], ps[0:32, Y4[0], 0:40])
                V.tensor_copy(small[32:64, 0:32], ps[32:64, Y4[0], 0:32])
                link(V.tensor_copy(small[64:128, 0:32], ps[64:128, Y4[0], 0:32]))
                link(V.tensor_tensor(rw3, rw3, ebias[:, :].unsqueeze(1).to_broadcast(s58), ALU.add))
                link(V.tensor_reduce(top, rw3, AX.X, ALU.max))
                V.tensor_tensor(rw3, rw3, top.unsqueeze(2).to_broadcast(s58), ALU.subtract).then_inc(sem("lg_max"), 1)
                dve.wait_ge(sem("lg_exp"), s + 1)
                link(V.tensor_reduce(top, rw3, AX.X, ALU.add))
                link(V.reciprocal(inv, top))
                link(V.tensor_tensor(rw3, rw3, inv.unsqueeze(2).to_broadcast(s58), ALU.mult))
                V.tensor_tensor(cmpA, rw3.unsqueeze(2).to_broadcast(s588), rw3.unsqueeze(3).to_broadcast(s588),
                                ALU.is_gt)
                link(V.tensor_tensor(cmpB, rw3.unsqueeze(2).to_broadcast(s588), rw3.unsqueeze(3).to_broadcast(s588),
                                     ALU.is_equal))
                low = lower[:, :].rearrange("p (e j) -> p e j", e=8).unsqueeze(1).to_broadcast(s588)
                link(V.tensor_tensor(cmpB, cmpB, low, ALU.mult))
                link(V.tensor_tensor(cmpA, cmpA, cmpB, ALU.add))
                link(V.tensor_reduce(rank, cmpA, AX.X, ALU.add))
                link(V.tensor_scalar(rank, rank, 2.0, None, ALU.is_lt))
                link(V.tensor_reduce(top, rw3, AX.X, ALU.max))
                V.tensor_tensor(w3, rw3, top.unsqueeze(2).to_broadcast(s58), ALU.subtract).then_inc(sem("rw_max"), 1)
                dve.wait_ge(sem("rw_exp"), s + 1)
                link(V.tensor_tensor(w3, w3, rank, ALU.mult))
                link(V.tensor_reduce(top, w3, AX.X, ALU.add))
                link(V.reciprocal(inv, top))
                V.tensor_tensor(rw3, w3, inv.unsqueeze(2).to_broadcast(s58), ALU.mult).then_inc(sem("combine_done"), 1)
                dve.wait_ge(sem("combine_done"), s + 1)

            def experts(s, c, between):
                base = 36 * s + 18 * c
                for n in range(18):
                    e = n // 2
                    up = ps[:, 3 + 2 * (n % 2), 0:CH]
                    dve.wait_ge(sem("esil_ready"), base + n + 1)
                    after(dve, "edown", base + n - 2)
                    if e < NEXP:
                        link(V.tensor_tensor(emul[n % 2], esil[n % 2], up, ALU.mult))
                        V.tensor_tensor(eh[n % 3], emul[n % 2], ps[:, 6 + e % 2, 0:CH],
                                        ALU.mult).then_inc(sem("eh_ready"), 1)
                    else:
                        V.tensor_tensor(eh[n % 3], esil[n % 2], up, ALU.mult).then_inc(sem("eh_ready"), 1)
                    between(n)
                dve.wait_ge(sem("edown"), base + 18)
                for m in range(2):
                    y = hT[:, m, cols(s, c)]
                    V.tensor_tensor(y, y, ps[:, m, 0:CH], ALU.add).then_inc(sem("moe_used"), 1)

            def att2_norm(s, n=0, t0=0, t1=T):
                q = qkv(s, 192)
                nt = t1 - t0
                y4 = q[:, t0:t1, 0:64].rearrange("p t (h d) -> p t h d", h=2)
                shape = [P, nt, 2, 32]
                gm = S[:, 100 + 2 * t0:100 + 2 * t1].rearrange("p (t h) -> p t h", t=nt)
                var = S[:, 2 * t0:2 * t1]
                gv = var.rearrange("p (t h) -> p t h", t=nt)
                p4 = prods[0][:, 0:nt * QC].rearrange("p (t h d) -> p t h d", t=nt, h=2)
                link(V.tensor_reduce(gm, y4, AX.X, ALU.add))
                link(V.tensor_scalar(gm, gm, 1.0 / 32, None, ALU.mult))
                link(V.tensor_tensor(y4, y4, gm.unsqueeze(3).to_broadcast(shape), ALU.subtract))
                yield
                link(V.tensor_tensor(p4, y4, y4, ALU.mult))
                link(V.tensor_reduce(gv, p4, AX.X, ALU.add))
                V.tensor_scalar(var, var, 1.0 / 32, EPS_LN, ALU.mult, ALU.add).then_inc(sem("gn_var"), 1)
                yield
                dve.wait_ge(sem("gn_rstd"), n + 1)
                chunks = 1 if nt < T else 2
                V.tensor_tensor(y4, y4, gv.unsqueeze(3).to_broadcast(shape),
                                ALU.mult).then_inc(sem("att2_done"), chunks)
                dve.wait_ge(sem("att2_done"), n + 2)

            def att2_gated(s, chunks=(0, 1)):
                for c in chunks:
                    dve.wait_ge(sem("att2_used"), 3 * s + 2 + c)
                    dve.wait_ge(sem("g_used"), 4 * s + 4)
                    V.tensor_tensor(oT[:, :, cols(s, c)], oT[:, :, cols(s, c)], yT[:, :, cols(s, c)],
                                    ALU.mult).then_inc(sem("att2_gated"), 1)

            def ternary_mean(w):
                dve.wait_ge(sem("w_f_in"), 32)
                V.tensor_reduce(gam[:, w:w + 1], exp_flat[:, 2048 * w:2048 * (w + 1)], AX.X, ALU.add,
                                apply_absolute_value=True).then_inc(sem("gam_sum"), 1)

            def ternary_thresholds():
                dve.wait_ge(sem("gam_ready"), 1)
                V.tensor_scalar(gam[:, 2:4], ps[:, Y4[3], 0:2], 1.0 / 1024, EPS_LN, ALU.mult,
                                ALU.add).then_inc(sem("gam_used"), 1)
                dve.wait_ge(sem("gam_used"), 1)
                link(V.tensor_scalar(gam[:, 4:6], gam[:, 2:4], 0.5, None, ALU.mult))
                link(V.tensor_scalar(gam[:, 6:8], gam[:, 2:4], -0.5, None, ALU.mult))

            def ternary_weights():
                for w in range(2):
                    raw, t_ = exp_flat[:, 2048 * w:2048 * (w + 1)], tern[:, 2048 * w:2048 * (w + 1)]
                    link(V.tensor_scalar(t_, raw, gam[:, 6 + w:7 + w], None, ALU.is_lt))
                    last = V.scalar_tensor_tensor(out=t_, in0=raw, scalar=gam[:, 4 + w:5 + w], in1=t_,
                                                  op0=ALU.is_gt, op1=ALU.subtract)
                last.then_inc(sem("tern_done"), 1)

            def final(s, c, m):
                y = hT[:, m, cols(s, c)]
                dve.wait_ge(sem("fc2_ready"), 4 * s + 2 * c + m + 1)
                V.scalar_tensor_tensor(out=y, in0=ps[:, X4[2 * c + m], 0:CH], scalar=v("b2", m), in1=y,
                                       op0=ALU.add, op1=ALU.add).then_inc(sem("final"), 1)

            class_query()
            for i in range(4):
                window_sums(i)
                window_scores(i)
                window_output(i)
            local_out(0)
            window_sums(4)
            window_scores(4)
            norm_dve("lnga", 0, yT, xT, LC, EPS_LN, drained=[("proj_ready", 4)])
            window_output(4)
            window_sums(5)
            global_attention(0)
            class_token(0)
            norm_dve("ln0", 0, hT, xT, CH, EPS_LN, drained=[("gkv_ready", 8)])
            window_scores(5)
            window_output(5)
            att, att_w = att0_scores(0), att0_weigh(0)
            run(att, 2)
            window_sums(6)
            run(att, CUT_SCORES[0])
            window_scores(6)
            run(att, CUT_SCORES[1] - CUT_SCORES[0])
            window_output(6)
            window_sums(7)
            run(att)
            softmax_shift("att0", 4)
            window_scores(7)
            window_output(7)
            softmax_scale("att0", 0, 4)
            local_out(1)
            run(att_w, CUT_WEIGH[0])
            norm_dve("lnga", 1, yT, xT, LC, EPS_LN, drained=[("proj_ready", 8)])
            run(att_w)
            done("att0", 0)
            global_attention(1)
            att0_gated(0)
            class_token(1)
            norm_dve("ln0", 1, hT, xT, CH, EPS_LN, drained=[("gkv_ready", 16)])
            att0_output(0)
            att, att_w = att0_scores(1), att0_weigh(1)
            run(att, 2)
            mqa_softmax(0)
            run(att, CUT_SCORES[0])
            att1_output(0)
            router(0)

            def between(n):
                if n < 8:
                    run(att, 1)
                elif n == 8:
                    run(att)
                    softmax_shift("att0", 4)
                elif n == 10:
                    softmax_scale("att0", 1, 4)
                elif n > 10:
                    run(att_w, 1)

            experts(0, 0, between)
            experts(0, 1, lambda n: run(att_w, 1))
            run(att_w)
            done("att0", 1)
            att0_gated(1)
            norm_dve("ln2", 0, hT, xT, CH, EPS_LN)
            att0_output(1)
            att, att_w, att_n = att2_scores(0), att2_weigh(0), att2_norm(0)
            run(att, 2)
            mqa_softmax(1)
            run(att, CUT_RETENTION[0][0])
            att1_output(1)
            router(1)

            def between(n):
                if n < 9:
                    run(att, 1)
                elif n == 9:
                    run(att)
                    att2_decay(0, T)
                else:
                    run(att_w, 2 if n < 13 else 1)

            experts(1, 0, between)

            def between(n):
                if n < 5:
                    run(att_w, 1)
                elif n < 8:
                    run(att_w)
                    run(att_n, 1)
                elif n > 15:
                    ternary_mean(n - 16)

            experts(1, 1, between)
            att2_gated(0)
            ternary_thresholds()
            norm_dve("ln2", 1, hT, xT, CH, EPS_LN)
            add_to_h("l1o", 0, Y4)
            ternary_weights()
            att, att_w = att2_scores(1), att2_weigh(1)
            att_n = att2_norm(1, 1, 0, 9)
            run(att, 2)
            norm_dve("ln3", 0, hT, xT, CH, EPS_LN)
            run(att, 9)
            att2_decay(0, 9)
            run(att_w, 9)
            run(att_n, 2)
            run(att, 3)
            run(att_n)
            run(att, 2)
            for c in range(2):
                for m in range(2):
                    final(0, c, m)
            att2_gated(1, (0,))
            run(att, 1)
            add_to_h("l1o", 1, Y4, (0,))
            run(att)
            att2_decay(9, T)
            norm_dve("ln3", 1, hT, xT, CH, EPS_LN, chunks=(0,))
            run(att_w)
            run(att2_norm(1, 2, 9, T))
            for c in range(2):
                if c == 1:
                    att2_gated(1, (1,))
                    add_to_h("l1o", 1, Y4, (1,))
                    norm_dve("ln3", 1, hT, xT, CH, EPS_LN, chunks=(1,))
                for m in range(2):
                    final(1, c, m)


def fold(w):
    k = w.shape[0] // P
    return w.reshape(k, P, -1).transpose(1, 0, 2).reshape(P, -1)


def pair_order(w, heads, d):
    return w.reshape(w.shape[0], heads, d // 2, 2).transpose(0, 1, 3, 2).reshape(w.shape[0], heads * d)


def by_quarter(*ws):
    return np.concatenate([w.reshape(w.shape[0], 4, -1) for w in ws], axis=2)


def shape_tables():
    f = np.float32
    pos = np.arange(T, dtype=f)
    inv = (1.0 / np.power(f(2500), np.arange(0, 16, 2, dtype=f) / f(16))).astype(f)
    emb = np.outer(pos, inv).astype(f)
    emb = np.concatenate([emb, emb], -1)
    cs, sn = np.cos(emb)[:, ::2].astype(f), np.sin(emb)[:, ::2].astype(f)
    rope = np.stack([np.concatenate([cs, cs], -1), np.concatenate([-sn, sn], -1)])
    base = ((np.arange(0, 32, 2, dtype=f) + f(0.4 * 32)) / f(1.4 * 32)).astype(f)
    scale = np.power(base[None, :], pos[:, None] / f(512.0)).astype(f)
    ang = (pos[:, None] * (1.0 / np.power(f(10000.0), np.arange(16, dtype=f) / f(16)))[None, :]).astype(f)
    tabs = []
    for s in (scale, (1.0 / scale).astype(f)):
        c_, s_ = np.cos(ang) * s, np.sin(ang) * s
        tabs += [np.concatenate([c_, c_], -1), np.concatenate([-s_, s_], -1)]
    gammas = 1.0 - np.exp(np.linspace(np.log(1 / 32.0), np.log(1 / 512.0), 8)).astype(f)
    expo = (np.arange(T)[:, None] - np.arange(T)[None, :]).astype(f)
    d = np.where(expo[None] >= 0, np.exp(expo[None] * np.log(gammas)[:, None, None]), 0.0)
    decay = d.reshape(4, 2, T, T).transpose(0, 2, 3, 1).reshape(4, 1, T * T * 2)
    sel = np.repeat(np.eye(NEXP), P, axis=1)
    lower = (np.arange(8)[None, :] < np.arange(8)[:, None]).astype(f).reshape(1, 64)
    return {k: np.ascontiguousarray(x, dtype=f) for k, x in dict(
        rope=rope.reshape(1, -1), xpos=np.stack(tabs).reshape(1, -1), decay=decay, sel=sel, lower=lower,
        ident=np.eye(P)).items()}


def lay_out(i):
    g = {k: np.asarray(x) for k, x in i.items()}
    t = lambda n: g["L0_tok_" + n]
    at = lambda n: g["L0_attn_" + n].T
    ff = lambda n: g["L0_ffn_" + n]
    l1 = lambda n: g["L1_attn_" + n]
    x = g["x"].reshape(2, HB, 3, 4, 3, 14, 4, 3, 14).transpose(0, 3, 2, 5, 8, 4, 7, 6, 1)
    x = x.reshape(ITERS, PATCH_K, NCG, CONV_N).transpose(0, 2, 1, 3).reshape(ITERS * NCG, PATCH_K, CONV_N)
    wc = t("conv_w").reshape(C, PATCH_K).T
    a = {
        "x_main": x[:, 0:512].reshape(ITERS * NCG, 4, P, CONV_N).transpose(0, 2, 1, 3),
        "x_rest": x[:, 512:],
        "w_conv": wc[0:512].reshape(4, P, C).transpose(1, 0, 2),
        "w_convr": wc[512:],
        "la_wkv": t("la_wkv").reshape(2, P, 512).transpose(1, 0, 2),
        "la_wq": t("la_wq").reshape(2, P, C).transpose(1, 0, 2),
        "la_proj_w": fold(t("la_proj_w")), "mod_w": fold(t("mod_w")),
        "ga_wkv": fold(by_quarter(t("ga_wkv")[:, 0:C], t("ga_wkv")[:, C:]).reshape(C, -1)),
        "ga_wq": fold(t("ga_wq")), "ga_proj_w": fold(t("ga_proj_w")),
        "attn_qkvg": fold(by_quarter(pair_order(at("W_q"), 16, 16), pair_order(at("W_k"), 16, 16),
                                  at("W_v"), at("W_gv")).reshape(C, -1)),
        "attn_go": fold(at("W_go")), "attn_o": fold(at("W_o")),
        "ffn_o": fold(ff("Wo").T), "ffn_r": fold(ff("Wr").T), "ebias": ff("expert_bias").reshape(1, NEXP),
        "l1_g": fold(l1("W_G")), "l1_o": fold(l1("W_O")),
        "w1": fold(g["L1_ffn_W1"].T).reshape(P, 2, 1024), "w2": fold(g["L1_ffn_W2"].T).reshape(P, 8, C),
    }
    kc, vc = ff("Wkc").T, ff("Wvc").T
    a["ffn_qkv"] = fold(np.concatenate([ff("Wq").T, kc, kc, vc], 1))
    heads = lambda n: l1(n).transpose(1, 0, 2).reshape(C, C)
    a["l1_qkv"] = fold(by_quarter(pair_order(heads("W_Q"), 8, 32), pair_order(heads("W_K"), 8, 32),
                               heads("W_V")).reshape(C, -1))
    ex = [np.stack([fold(w.T) for w in (ff("eW1")[e], ff("eW3")[e], ff("eW2")[e])], 1) for e in range(NEXP)]
    ex.append(np.stack([fold(w.T) for w in (ff("sW1"), ff("sW3"), ff("sW2"))], 1))
    a["experts"] = np.stack(ex, 1).reshape(P, 9, 3, 2, C)
    src = {"class_emb": t("class_emb"), "g1": ff("g1"), "g2": ff("g2"), "gn_weight": l1("gn_weight"),
           "gn_bias": l1("gn_bias"), "b1": g["L1_ffn_b1"], "b2": g["L1_ffn_b2"]}
    a["vec"] = np.concatenate([(src[n] if n in src else t(n)).reshape(k, P).T for n, k in VEC], axis=1)
    return {k: np.ascontiguousarray(x) for k, x in a.items()}


def kernel(**inputs):
    import concourse.bacc as _bacc
    from concourse.bass_utils import run_bass_kernel_spmd as _run

    nc = _bacc.Bacc("TRN2", target_bir_lowering=False, num_devices=1)
    arrays = {**lay_out(inputs), **shape_tables()}
    aps = {n: nc.dram_tensor(n + "_dram", x.shape, F32, kind="ExternalInput").ap() for n, x in arrays.items()}
    out = nc.dram_tensor("out_dram", (P, 2, NT), F32, kind="ExternalOutput").ap()
    build(nc, aps, out)
    r = _run(nc, [{n + "_dram": x for n, x in arrays.items()}], core_ids=[0])
    got = r.results[0]["out_dram"]
    return np.ascontiguousarray(got.reshape(P, 2, 2, T, HB).transpose(2, 4, 3, 1, 0).reshape(B, T, C))
```
